# Optimizing a Trainium2 kernel written in Bass

```python
import numpy as np
import jax
import jax.numpy as jnp

def _softmax(x, axis=-1):
    return jax.nn.softmax(x, axis=axis)

def _gelu(x):
    return jax.nn.gelu(x, approximate=True)

def _silu(x):
    return jax.nn.silu(x)

def _sigmoid(x):
    return jax.nn.sigmoid(x)

def _layernorm(x, axis=-1, eps=1e-05):
    m = jnp.mean(x, axis=axis, keepdims=True)
    v = jnp.var(x, axis=axis, keepdims=True)
    return (x - m) / jnp.sqrt(v + eps)

def _scatter_add(tgt, idx, src, axis=0):
    return tgt.at[idx].add(src)

def _segment_sum(src, seg, n):
    return jax.ops.segment_sum(src, seg, n)
kernel_name = 'mk_gps_d2_gnn_r32_0def3b'

def setup_inputs(seed: int=0):
    np.random.seed(seed)
    _w = jnp.asarray

    def _rec_inputs():
        import jax
        import jax.numpy as jnp
        _gk = jax.random.key(seed)
        x = -0.0002117 + 1 * jax.random.normal(jax.random.fold_in(_gk, 1), (3125, 256), jnp.float32)
        src = jax.random.randint(jax.random.fold_in(_gk, 2), (50000,), 0, 3125, jnp.int32)
        dst = jnp.minimum((3125 * jax.random.uniform(jax.random.fold_in(_gk, 3), (50000,)) ** 2.0).astype(jnp.int32), 99999)
        _o = jnp.argsort(dst, stable=True)
        src = src[_o]
        dst = dst[_o]
        edge_weight = jax.random.uniform(jax.random.fold_in(_gk, 12), (50000,), jnp.float32, 0.0, 0.999998)
        return (x, src, dst, edge_weight)
    x, src, dst, edge_weight = _rec_inputs()

    def _L0_gnn_setup():
        import jax, jax.numpy as jnp
        import numpy as np
        N, D, E = (3125, 256, 312500)
        H = 2 * D
        EPS = 0.0
        key = jax.random.key(seed)
        k1, k2, k3, k4, k5, k6, k7 = jax.random.split(key, 7)
        x = jax.random.normal(k1, (N, D), dtype=jnp.float32)
        edge_index = jax.random.randint(k2, (2, E), 0, N, dtype=jnp.int64)
        edge_weight = jax.random.uniform(k3, (E,), dtype=jnp.float32)
        s1 = 1.0 / np.sqrt(D)
        s2 = 1.0 / np.sqrt(H)
        W1 = jax.random.uniform(k4, (D, H), dtype=jnp.float32, minval=-s1, maxval=s1)
        b1 = jax.random.uniform(k5, (H,), dtype=jnp.float32, minval=-s1, maxval=s1)
        W2 = jax.random.uniform(k6, (H, D), dtype=jnp.float32, minval=-s2, maxval=s2)
        b2 = jax.random.uniform(k7, (D,), dtype=jnp.float32, minval=-s2, maxval=s2)
        return {'x': x, 'edge_index': edge_index, 'edge_weight': edge_weight, 'W1': W1, 'b1': b1, 'W2': W2, 'b2': b2}
    _L0_gnn_all = _L0_gnn_setup()
    _L0_gnn_in = {k: v for k, v in _L0_gnn_all.items() if k in ('W1', 'b1', 'W2', 'b2')}
    del _L0_gnn_all

    def _L0_mix_setup():
        import jax, jax.numpy as jnp
        import numpy as np
        B, L, D, H = (4, 512, 256, 8)
        DK = D // H

        def _heads(t):
            b, l, d = t.shape
            return t.reshape(b, l, H, DK).transpose(0, 2, 1, 3)
        key = jax.random.key(seed)
        ks = jax.random.split(key, 9)
        s = 0.02
        return {'x': jax.random.normal(ks[0], (B, L, D), dtype=jnp.float32), 'Wq': jax.random.normal(ks[1], (D, D), dtype=jnp.float32) * s, 'bq': jnp.zeros((D,), dtype=jnp.float32), 'Wk': jax.random.normal(ks[2], (D, D), dtype=jnp.float32) * s, 'bk': jnp.zeros((D,), dtype=jnp.float32), 'Wv': jax.random.normal(ks[3], (D, D), dtype=jnp.float32) * s, 'bv': jnp.zeros((D,), dtype=jnp.float32), 'Wfc': jax.random.normal(ks[4], (D, D), dtype=jnp.float32) * s, 'bfc': jnp.zeros((D,), dtype=jnp.float32)}
    _L0_mix_all = _L0_mix_setup()
    _L0_mix_in = {k: v for k, v in _L0_mix_all.items() if k in ('Wq', 'bq', 'Wk', 'bk', 'Wv', 'bv', 'Wfc', 'bfc')}
    del _L0_mix_all

    def _L0_ffn_setup():
        import math
        import jax, jax.numpy as jnp
        import numpy as np
        CAPACITY_FACTOR = 1.25
        key = jax.random.key(seed)
        ks = jax.random.split(key, 5)
        B, L, D, F, E = (8, 256, 256, 1024, 8)
        h = jax.random.normal(ks[0], (B, L, D), dtype=jnp.float32)
        gate_w = jax.random.normal(ks[1], (D, E), dtype=jnp.float32) * 0.02
        gate_b = jnp.zeros((E,), dtype=jnp.float32)
        w1 = jax.random.normal(ks[2], (E, D, F), dtype=jnp.float32) * (1.0 / math.sqrt(D))
        b1 = jnp.zeros((E, F), dtype=jnp.float32)
        w2 = jax.random.normal(ks[3], (E, F, D), dtype=jnp.float32) * (1.0 / math.sqrt(F))
        b2 = jnp.zeros((E, D), dtype=jnp.float32)
        return {'h': h, 'gate_w': gate_w, 'gate_b': gate_b, 'w1': w1, 'b1': b1, 'w2': w2, 'b2': b2}
    _L0_ffn_all = _L0_ffn_setup()
    _L0_ffn_in = {k: v for k, v in _L0_ffn_all.items() if k in ('gate_w', 'gate_b', 'w1', 'b1', 'w2', 'b2')}
    del _L0_ffn_all

    def _L1_gnn_setup():
        import jax, jax.numpy as jnp
        import numpy as np
        N = 10000
        E = 10000
        D = 256
        key = jax.random.key(seed)
        ks = jax.random.split(key, 10)
        s = 1.0 / np.sqrt(D)
        return {'x0': jax.random.normal(ks[0], (N, D), jnp.float32), 'edge_index': jax.random.randint(ks[1], (2, E), 0, N, jnp.int32), 'W1': jax.random.normal(ks[2], (D, D), jnp.float32) * s, 'b1': jax.random.normal(ks[3], (D,), jnp.float32) * s, 'W2': jax.random.normal(ks[4], (D, D), jnp.float32) * s, 'b2': jax.random.normal(ks[5], (D,), jnp.float32) * s, 'wa1': jax.random.normal(ks[6], (D,), jnp.float32) * s, 'ba1': jax.random.normal(ks[7], (1,), jnp.float32) * s, 'wa2': jax.random.normal(ks[8], (D,), jnp.float32) * s, 'ba2': jax.random.normal(ks[9], (1,), jnp.float32) * s}
    _L1_gnn_all = _L1_gnn_setup()
    _L1_gnn_in = {k: v for k, v in _L1_gnn_all.items() if k in ('W1', 'b1', 'W2', 'b2', 'wa1', 'ba1', 'wa2', 'ba2')}
    del _L1_gnn_all

    def _L1_mix_setup():
        import jax, jax.numpy as jnp
        import numpy as np
        NUM_HEADS = 8
        key = jax.random.key(seed)
        ks = jax.random.split(key, 5)
        B, N, C = (8, 512, 256)
        x = jax.random.normal(ks[0], (B, N, C), dtype=jnp.float32)
        Wq = jax.random.normal(ks[1], (C, C), dtype=jnp.float32) * 0.02
        Wkv = jax.random.normal(ks[2], (2 * C, C), dtype=jnp.float32) * 0.02
        Wproj = jax.random.normal(ks[3], (C, C), dtype=jnp.float32) * 0.02
        bproj = jnp.zeros((C,), dtype=jnp.float32)
        return {'x': x, 'Wq': Wq, 'Wkv': Wkv, 'Wproj': Wproj, 'bproj': bproj}
    _L1_mix_all = _L1_mix_setup()
    _L1_mix_in = {k: v for k, v in _L1_mix_all.items() if k in ('Wq', 'Wkv', 'Wproj', 'bproj')}
    del _L1_mix_all

    def _L1_ffn_setup():
        import jax, jax.numpy as jnp
        import numpy as np
        TOP_K = 2
        key = jax.random.key(seed)
        ks = jax.random.split(key, 4)
        B, L, D, H, E = (8, 128, 256, 1024, 8)
        s = 0.02
        return {'x': jax.random.normal(ks[0], (B, L, D), jnp.float32), 'Wg': jax.random.normal(ks[1], (D, E), jnp.float32) * s, 'bg': jnp.zeros((E,), jnp.float32), 'W1': jax.random.normal(ks[2], (E, D, H), jnp.float32) * s, 'b1': jnp.zeros((E, H), jnp.float32), 'W2': jax.random.normal(ks[3], (E, H, D), jnp.float32) * s, 'b2': jnp.zeros((E, D), jnp.float32)}
    _L1_ffn_all = _L1_ffn_setup()
    _L1_ffn_in = {k: v for k, v in _L1_ffn_all.items() if k in ('Wg', 'bg', 'W1', 'b1', 'W2', 'b2')}
    del _L1_ffn_all
    return {'x': x, 'src': src, 'dst': dst, 'edge_weight': edge_weight, 'L0_gnn_W1': _L0_gnn_in['W1'], 'L0_gnn_b1': _L0_gnn_in['b1'], 'L0_gnn_W2': _L0_gnn_in['W2'], 'L0_gnn_b2': _L0_gnn_in['b2'], 'L0_mix_Wq': _L0_mix_in['Wq'], 'L0_mix_bq': _L0_mix_in['bq'], 'L0_mix_Wk': _L0_mix_in['Wk'], 'L0_mix_bk': _L0_mix_in['bk'], 'L0_mix_Wv': _L0_mix_in['Wv'], 'L0_mix_bv': _L0_mix_in['bv'], 'L0_mix_Wfc': _L0_mix_in['Wfc'], 'L0_mix_bfc': _L0_mix_in['bfc'], 'L0_ffn_gate_w': _L0_ffn_in['gate_w'], 'L0_ffn_gate_b': _L0_ffn_in['gate_b'], 'L0_ffn_w1': _L0_ffn_in['w1'], 'L0_ffn_b1': _L0_ffn_in['b1'], 'L0_ffn_w2': _L0_ffn_in['w2'], 'L0_ffn_b2': _L0_ffn_in['b2'], 'L1_gnn_W1': _L1_gnn_in['W1'], 'L1_gnn_b1': _L1_gnn_in['b1'], 'L1_gnn_W2': _L1_gnn_in['W2'], 'L1_gnn_b2': _L1_gnn_in['b2'], 'L1_gnn_wa1': _L1_gnn_in['wa1'], 'L1_gnn_ba1': _L1_gnn_in['ba1'], 'L1_gnn_wa2': _L1_gnn_in['wa2'], 'L1_gnn_ba2': _L1_gnn_in['ba2'], 'L1_mix_Wq': _L1_mix_in['Wq'], 'L1_mix_Wkv': _L1_mix_in['Wkv'], 'L1_mix_Wproj': _L1_mix_in['Wproj'], 'L1_mix_bproj': _L1_mix_in['bproj'], 'L1_ffn_Wg': _L1_ffn_in['Wg'], 'L1_ffn_bg': _L1_ffn_in['bg'], 'L1_ffn_W1': _L1_ffn_in['W1'], 'L1_ffn_b1': _L1_ffn_in['b1'], 'L1_ffn_W2': _L1_ffn_in['W2'], 'L1_ffn_b2': _L1_ffn_in['b2']}

def reference(x, src, dst, edge_weight, L0_gnn_W1, L0_gnn_b1, L0_gnn_W2, L0_gnn_b2, L0_mix_Wq, L0_mix_bq, L0_mix_Wk, L0_mix_bk, L0_mix_Wv, L0_mix_bv, L0_mix_Wfc, L0_mix_bfc, L0_ffn_gate_w, L0_ffn_gate_b, L0_ffn_w1, L0_ffn_b1, L0_ffn_w2, L0_ffn_b2, L1_gnn_W1, L1_gnn_b1, L1_gnn_W2, L1_gnn_b2, L1_gnn_wa1, L1_gnn_ba1, L1_gnn_wa2, L1_gnn_ba2, L1_mix_Wq, L1_mix_Wkv, L1_mix_Wproj, L1_mix_bproj, L1_ffn_Wg, L1_ffn_bg, L1_ffn_W1, L1_ffn_b1, L1_ffn_W2, L1_ffn_b2):
    import jax
    import jax.numpy as jnp

    def _L0_gnn_ref(x, edge_index, edge_weight, W1, b1, W2, b2):
        import jax, jax.numpy as jnp
        import numpy as np
        N, D, E = (3125, 256, 312500)
        H = 2 * D
        EPS = 0.0
        row, col = (edge_index[0], edge_index[1])
        messages = x[col] * edge_weight[:, None]
        agg = jax.ops.segment_sum(messages, row, num_segments=N)
        h = (1.0 + EPS) * x + agg
        h = jax.nn.relu(h @ W1 + b1)
        out = h @ W2 + b2
        return out

    def _L0_mix_ref(x, Wq, bq, Wk, bk, Wv, bv, Wfc, bfc):
        import jax, jax.numpy as jnp
        import numpy as np
        B, L, D, H = (4, 512, 256, 8)
        DK = D // H

        def _heads(t):
            b, l, d = t.shape
            return t.reshape(b, l, H, DK).transpose(0, 2, 1, 3)
        q = _heads(x @ Wq.T + bq)
        k = _heads(x @ Wk.T + bk)
        v = _heads(x @ Wv.T + bv)
        seq_len = q.shape[-2]
        p_attn = jnp.einsum('bhnd,bhne->bhde', k, v) / seq_len
        out = jnp.einsum('bhnd,bhde->bhne', q, p_attn)
        out = out.transpose(0, 2, 1, 3).reshape(x.shape[0], seq_len, H * DK)
        return out @ Wfc.T + bfc

    def _L0_ffn_ref(h, gate_w, gate_b, w1, b1, w2, b2):
        import math
        import jax, jax.numpy as jnp
        import numpy as np
        CAPACITY_FACTOR = 1.25
        B, L, D = h.shape
        E = gate_w.shape[1]
        T = B * L
        C = max(1, math.ceil(CAPACITY_FACTOR * T / E))
        x = h.reshape(T, D)
        logits = x @ gate_w + gate_b
        probs = jax.nn.softmax(logits, axis=-1)
        idx = jnp.argmax(probs, axis=-1)
        prb = jnp.take_along_axis(probs, idx[:, None], axis=1)[:, 0]
        one_hot = jax.nn.one_hot(idx, E, dtype=jnp.float32)
        pos = (jnp.cumsum(one_hot, axis=0) * one_hot).sum(-1).astype(jnp.int32) - 1
        kept = pos < C
        pos_safe = jnp.where(kept, pos, C)
        buf = jnp.zeros((E, C, D), dtype=h.dtype).at[idx, pos_safe].set(x, mode='drop')
        hmid = jax.nn.relu(jnp.einsum('ecd,edf->ecf', buf, w1) + b1[:, None, :])
        ybuf = jnp.einsum('ecf,efd->ecd', hmid, w2) + b2[:, None, :]
        pos_g = jnp.minimum(pos, C - 1)
        y_tok = ybuf[idx, pos_g] * (prb * kept)[:, None]
        y = y_tok.reshape(B, L, D)
        y = jnp.nan_to_num(y, nan=0.0, posinf=10000.0, neginf=-10000.0)
        return y

    def _L1_gnn_ref(x0, edge_index, W1, b1, W2, b2, wa1, ba1, wa2, ba2):
        import jax, jax.numpy as jnp
        import numpy as np
        N = 10000
        E = 10000
        D = 256
        n = x0.shape[0]
        leaky = lambda v: jax.nn.leaky_relu(v, 0.2)
        x0_i = leaky(x0 @ W1 + b1)
        x0_j = leaky(x0 @ W2 + b2)
        a1 = x0_i @ wa1 + ba1[0]
        a2 = x0_j @ wa2 + ba2[0]
        row, col = (edge_index[0], edge_index[1])
        att = jax.nn.sigmoid(a1[row] + a2[col])
        msg = att[:, None] * x0_j[col]
        out = jax.ops.segment_sum(msg, row, num_segments=n)
        return out + x0

    def _L1_mix_ref(x, Wq, Wkv, Wproj, bproj):
        import jax, jax.numpy as jnp
        import numpy as np
        NUM_HEADS = 8
        B, N, C = x.shape
        h = NUM_HEADS
        d = C // h
        q = jnp.einsum('bnc,oc->bno', x, Wq).reshape(B, N, h, d).transpose(0, 2, 1, 3)
        kv = jnp.einsum('bnc,oc->bno', x, Wkv).reshape(B, N, 2, h, d)
        k = kv[:, :, 0].transpose(0, 2, 1, 3)
        v = kv[:, :, 1].transpose(0, 2, 1, 3)
        q = jax.nn.elu(q) + 1.0
        k = jax.nn.elu(k) + 1.0
        k_sum = k.sum(axis=2)
        D_inv = 1.0 / jnp.maximum(jnp.einsum('bhnd,bhd->bhn', q, k_sum), 1e-06)
        context = jnp.einsum('bhnd,bhne->bhde', k, v)
        attn = jnp.einsum('bhnd,bhde->bhne', q, context) * D_inv[..., None]
        out = attn.transpose(0, 2, 1, 3).reshape(B, N, C)
        out = jnp.einsum('bnc,oc->bno', out, Wproj) + bproj
        return out

    def _L1_ffn_ref(x, Wg, bg, W1, b1, W2, b2):
        import jax, jax.numpy as jnp
        import numpy as np
        TOP_K = 2
        B, L, D = x.shape
        E = W1.shape[0]
        xf = x.reshape(-1, D)
        gate_logits = xf @ Wg + bg
        top_w, top_i = jax.lax.top_k(gate_logits, TOP_K)
        top_w = jax.nn.softmax(top_w, axis=-1)
        w_dense = jnp.sum(jax.nn.one_hot(top_i, E, dtype=xf.dtype) * top_w[..., None], axis=1)
        out = jnp.zeros_like(xf)
        for e in range(E):
            h = jax.nn.gelu(xf @ W1[e] + b1[e], approximate=False)
            out = out + w_dense[:, e:e + 1] * (h @ W2[e] + b2[e])
        return out.reshape(B, L, D)
    edge_index = jnp.stack([src, dst])
    xn = _layernorm(x, axis=-1)
    x = x + _L0_gnn_ref(xn, edge_index, edge_weight, L0_gnn_W1, L0_gnn_b1, L0_gnn_W2, L0_gnn_b2) + _L0_mix_ref(xn[None], L0_mix_Wq, L0_mix_bq, L0_mix_Wk, L0_mix_bk, L0_mix_Wv, L0_mix_bv, L0_mix_Wfc, L0_mix_bfc)[0]
    x = x + _L0_ffn_ref(_layernorm(x, axis=-1)[None], L0_ffn_gate_w, L0_ffn_gate_b, L0_ffn_w1, L0_ffn_b1, L0_ffn_w2, L0_ffn_b2)[0]
    xn = _layernorm(x, axis=-1)
    x = x + _L1_gnn_ref(xn, edge_index, L1_gnn_W1, L1_gnn_b1, L1_gnn_W2, L1_gnn_b2, L1_gnn_wa1, L1_gnn_ba1, L1_gnn_wa2, L1_gnn_ba2) + _L1_mix_ref(xn[None], L1_mix_Wq, L1_mix_Wkv, L1_mix_Wproj, L1_mix_bproj)[0]
    x = x + _L1_ffn_ref(_layernorm(x, axis=-1)[None], L1_ffn_Wg, L1_ffn_bg, L1_ffn_W1, L1_ffn_b1, L1_ffn_W2, L1_ffn_b2)[0]
    return x

_drawn_inputs = setup_inputs


def setup_inputs(seed=0):
    import zlib

    import numpy as np

    out = dict(_drawn_inputs(seed))
    spreads = {'L0_mix_bq': (0.0, 0.8),
     'L0_mix_bk': (0.0, 0.8),
     'L0_mix_bv': (0.0, 0.8),
     'L0_mix_bfc': (0.0, 0.8),
     'L0_ffn_gate_b': (0.0, 0.8),
     'L0_ffn_b1': (0.0, 2.0),
     'L0_ffn_b2': (0.0, 2.0),
     'L1_mix_bproj': (0.0, 2.0),
     'L1_ffn_bg': (0.0, 0.649),
     'L1_ffn_b1': (0.0, 2.0),
     'L1_ffn_b2': (0.0, 2.0)}
    factors = {'L0_gnn_b1': 26.848,
     'L0_mix_Wq': 8.0,
     'L0_mix_Wk': 8.0,
     'L0_mix_Wv': 8.0,
     'L0_mix_Wfc': 8.0,
     'L1_gnn_b1': 36.189,
     'L1_mix_Wq': 45.115,
     'L1_mix_Wkv': 8.0,
     'L1_mix_Wproj': 8.0,
     'L1_ffn_Wg': 2.692,
     'L1_ffn_W1': 3.476,
     'L1_ffn_W2': 3.244,
     'edge_weight': 6.238,
     'L0_gnn_W1': 3.334,
     'L0_gnn_b2': 8.0,
     'L0_ffn_gate_w': 8.0,
     'L0_ffn_w1': 8.0,
     'L0_ffn_w2': 8.0,
     'L1_gnn_b2': 4.376}
    for name, (base, spread) in spreads.items():
        noise = np.random.default_rng([zlib.crc32(name.encode()), seed]).standard_normal(out[name].shape)
        drawn = base * np.exp(spread * noise) if base else spread * noise
        out[name] = jnp.asarray(drawn.astype(out[name].dtype))
    for name, factor in factors.items():
        out[name] = (out[name] * factor).astype(out[name].dtype)
    return out
```

```python
from contextlib import ExitStack

import concourse.bass as bass
from concourse import mybir

F32 = mybir.dt.float32
I32 = mybir.dt.int32
BF16 = mybir.dt.bfloat16
U16 = mybir.dt.uint16
ALU = mybir.AluOpType
ACT = mybir.ActivationFunctionType
AX = mybir.AxisListType

N, D, E = 3125, 256, 50000
P, T = 125, 25
KD = D // 128
EC = E // P
F0 = 512
FF, KF = 1024, 1024 // 128
X = 8
HD = 32
HEADS = D // HD
GT = 5
GR = T // GT
EB = 16
ET = -(-((E + T * 127) // 128) // EB) * EB
ETP = ET + EB
CAP0 = -(-5 * N // (4 * X))
ROW0 = 512
CH = 256
NCH = (2 * N + X * (CH - 1)) // CH
PK1, PK2, PKB = KD * FF, KF * D, KF
PACK = PK1 + PK2 + PKB + D
ROUND = 12582912.0
BIG = 3.4028234663852886e38
XJW = 264


class Chain:

    def __init__(self, eng, sem, base=0):
        self.eng, self.sem, self.n, self.base = eng, sem, 0, base

    def mark(self, ins):
        self.n += 1
        ins.then_inc(self.sem, 1)

    def join(self):
        self.eng.wait_ge(self.sem, self.base + self.n)

    def link(self, ins):
        self.mark(ins)
        self.join()


def one_ahead(eng, *sems):
    for s in sems:
        eng.sem_inc(s, 1)


def build(nc, a):
    persist = ExitStack()

    def sb(name, shape, dt=F32, ctx=persist):
        return ctx.enter_context(nc.sbuf_tensor(name, shape, dt))

    with persist:
        k = Shared(nc, sb, a)
        k.landed = [persist.enter_context(nc.semaphore(f"landed{s}")) for s in range(EB)]
        k.got = [persist.enter_context(nc.semaphore(f"got{t}")) for t in range(T)]
        prepare(nc, a, k)
        aggregate(nc, a, k, 0)
        gin_and_attention(nc, a, k)
        route(nc, a, k, 0)
        experts(nc, a, k, 0)
        combine(nc, a, k, 0)
        k.recycle(nc)
        project(nc, a, k)
        aggregate(nc, a, k, 1)
        attention(nc, a, k)
        route(nc, a, k, 1)
        experts(nc, a, k, 1)
        combine(nc, a, k, 1)


class Shared:

    def sem(self, nc, name):
        self.sems.append(nc.alloc_semaphore(name))
        return self.sems[-1]

    def recycle(self, nc):
        nc.clear_and_free_semaphores(self.sems)
        nc.all_engine_barrier()
        self.sems = []

    def __init__(self, nc, sb, a):
        self.sems = []
        self.x = sb("x_res", [P, T, D])
        self.xn_all = sb("x_normed", [128, T, D])
        self.xn = self.xn_all[0:P, :, :]
        self.acc_all = sb("node_sums", [128, T, D])
        self.acc = self.acc_all[0:P, :, :]
        self.xnT = sb("x_normed_T", [128, KD, N])
        self.edges = sb("sorted_edges", [128, ETP, 4])
        self.tile_bin = sb("tile_bin", [1, ETP], I32)
        self.ident = sb("ident", [128, 128])
        self.tri = sb("tri_strict", [128, 128])
        self.tri1 = sb("tri_incl", [128, 128])
        self.ones = sb("ones", [128, 128])
        self.iota = sb("iota_row", [128, 128])
        self.a1 = sb("a1_rows", [128, T, P])
        self.stats = sb("ln_stats", [P, T, 6])
        self.mean = sb("ln_mean", [P, T])
        self.rstd = sb("ln_rstd", [P, T])
        self.lnt = sb("ln_tmp", [P, 4, T])
        self.slots = sb("slots", [P, 2, T], I32)
        self.back = sb("slots_back", [P, 2, T], I32)
        self.gate = sb("gates", [P, 2, T])
        self.chunk_x = sb("chunk_expert", [1, NCH], I32)
        self.w = {}
        for name, shape in WEIGHTS.items():
            self.w[name] = sb("w_" + name, shape)
        self.R = sb("mix0_R", [128, KD, D])
        self.r0 = sb("mix0_r0", [1, D])
        self.ctx = sb("mix1_ctx", [128, KD, 2, 128])
        self.edges_d = nc.dram_tensor("edges_d", [128 * ETP, 4], F32).ap()
        self.xn_d = nc.dram_tensor("xn_d", [N, D], F32).ap()
        self.xj_d = nc.dram_tensor("xj_d", [N, XJW], F32).ap()
        self.buf = [nc.dram_tensor("rows0_d", [X * ROW0 + N, D], F32).ap(),
                    nc.dram_tensor("rows1_d", [NCH * CH, D], F32).ap()]
        self.ybuf = [nc.dram_tensor("y0_d", [X * ROW0, D], F32).ap(),
                     nc.dram_tensor("y1_d", [NCH * CH, D], F32).ap()]


WEIGHTS = {
    "g0_W1": [128, KD, F0], "g0_b1": [128, F0 // 128], "g0_W2": [128, F0 // 128, D], "g0_b2": [1, D],
    "m0_Wq": [128, KD, D], "m0_WkT": [128, KD, D], "m0_WvT": [128, KD, D], "m0_WfcT": [128, KD, D],
    "m0_bqc": [128, KD], "m0_bk": [1, D], "m0_bv": [1, D], "m0_bfc": [1, D],
    "f0_gw": [128, KD, X], "f0_gb": [128, T, X],
    "g1_W1": [128, KD, D], "g1_b1": [128, KD], "g1_W2": [128, KD, D], "g1_b2": [1, D],
    "g1_wa1": [128, KD, 128], "g1_ba1": [128, 1], "g1_wa2": [128, D], "g1_ba2": [128, 1],
    "m1_WqT": [128, KD, D], "m1_WkvT": [128, KD, 2 * D], "m1_WpT": [128, KD, D], "m1_bp": [128, D],
    "f1_gw": [128, KD, X], "f1_gb": [128, T, X],
}


def norm_scale_vector(nc, v, ch, k, var_ready, root_ready, n):
    st, t = k.stats, k.lnt
    even, odd = st[:, :, 1], st[:, :, 4]
    ch.mark(v.tensor_tensor(k.mean[:, :], even, odd, ALU.add))
    ch.mark(v.tensor_tensor(t[:, 0, :], even, odd, ALU.subtract))
    ch.link(v.tensor_tensor(t[:, 1, :], st[:, :, 2], st[:, :, 5], ALU.add))
    ch.mark(v.tensor_scalar(k.mean[:, :], k.mean[:, :], 0.5, None, ALU.mult))
    ch.mark(v.tensor_tensor(t[:, 0, :], t[:, 0, :], t[:, 0, :], ALU.mult))
    ch.link(v.tensor_scalar(t[:, 1, :], t[:, 1, :], 1.0 / D, 1e-5, ALU.mult, ALU.add))
    v.scalar_tensor_tensor(t[:, 1, :], t[:, 0, :], 0.25, t[:, 1, :], ALU.mult, ALU.add).then_inc(var_ready, 1)
    v.wait_ge(root_ready, n)
    ch.link(v.reciprocal(k.rstd[:, :], t[:, 2, :]))
    ch.link(v.tensor_tensor(t[:, 0, :], k.rstd[:, :], k.rstd[:, :], ALU.mult))
    ch.link(v.tensor_tensor(t[:, 0, :], t[:, 0, :], t[:, 1, :], ALU.mult))
    ch.link(v.tensor_scalar(t[:, 0, :], t[:, 0, :], -0.5, 1.5, ALU.mult, ALU.add))
    ch.link(v.tensor_tensor(k.rstd[:, :], k.rstd[:, :], t[:, 0, :], ALU.mult))


def norm_root_scalar(s, k, var_ready, root_ready, n):
    s.wait_ge(var_ready, n)
    s.activation(k.lnt[:, 2, :], k.lnt[:, 1, :], ACT.Sqrt).then_inc(root_ready, 1)


def prepare(nc, a, k):
    with ExitStack() as c:
        def sb(name, shape, dt=F32):
            return c.enter_context(nc.sbuf_tensor(name, shape, dt))

        def sem(name):
            return k.sem(nc, name)

        src_i, dst_i = sb("src_i", [P, EC], I32), sb("dst_i", [P, EC], I32)
        w_e = sb("w_e", [P, EC])
        rec = sb("edge_rec", [P, EC, 4])
        src_f, bin_f = sb("src_f", [P, EC]), sb("bin_f", [P, EC])
        mask = k.xnT[0:P, :, :].rearrange("p i n -> p (i n)").bitcast(BF16)[:, 0:T * EC]\
            .rearrange("p (t e) -> p t e", e=EC)
        run = k.acc[:, :, :].rearrange("p t c -> p (t c)").bitcast(U16)[:, 0:T * EC]\
            .rearrange("p (t e) -> p t e", e=EC)
        pos, tmp = sb("edge_pos", [P, EC]), sb("edge_tmp", [P, EC])
        pos_i, low_i = sb("edge_pos_i", [P, EC], I32), sb("edge_low_i", [P, EC], I32)
        cnt, off = sb("bin_cnt", [P, T]), sb("bin_off", [128, T])
        tot_i, tiles, tiles_to = sb("bin_tot_i", [128, T], I32), sb("bin_tiles", [128, T]), sb("bin_tiles_to", [128, T])
        tix, tb = sb("tile_ix", [1, ETP]), sb("tile_b", [1, ETP])
        iota_i, tix_i = sb("iota_i", [128, 128], I32), sb("tix_i", [1, ETP], I32)
        zero = k.a1[:, :, :].rearrange("p t n -> p (t n)")[:, 0:2048]
        idx_st = sb("scatter_idx", [P, 2, 8], I32)
        rec_st = sb("scatter_rec", [P, 2, 8, 4])
        G, scol, srow = sb("gram", [128, KD, D]), sb("xn_sum_col", [128, KD]), sb("xn_sum_row", [1, D])
        U, Ul, KV, M2 = sb("mix_U", [128, KD, D]), sb("mix_Ul", [1, D]), sb("mix_KV", [128, KD, D]), sb("mix_M2", [128, KD, D])
        nconst = sb("n_const", [1, 1])
        pc = c.enter_context(nc.psum_tensor("p_counts", [128, 512], F32))
        pg = [c.enter_context(nc.psum_tensor(f"p_gram{i}", [128, 512], F32)) for i in range(KD)]
        pu = [c.enter_context(nc.psum_tensor(f"p_mix{i}", [128, 512], F32)) for i in range(KD)]
        pcol = c.enter_context(nc.psum_tensor("p_sumcol", [128, 512], F32))
        psr = c.enter_context(nc.psum_tensor("p_sumrow", [128, 512], F32))

        x_in, edges_in, w_in = sem("x_in"), sem("edges_in"), sem("w_in")
        consts, iotas = sem("consts"), sem("iotas")
        prefilled, zeroed = sem("prefilled"), sem("zeroed")
        vec, cnt_ready, prefix = sem("vec"), sem("cnt_ready"), sem("prefix")
        idx_ready, begun = sem("idx_ready"), sem("scatter_begun")
        staged = [sem(f"staged{i}") for i in range(2)]
        scattered = [sem(f"scattered{i}") for i in range(2)]
        stage_free = [sem(f"stage_free{i}") for i in range(2)]
        reload, var_ready, root_ready = sem("reload"), sem("var_ready"), sem("root_ready")
        normed, xn_out = sem("normed"), sem("xn_out")
        gram_done, mixed, mix_copied = sem("gram_done"), sem("mixed"), sem("mix_copied")
        lnc = sem("ln_chain")

        with nc.Block() as block:
            @block.sync
            def _(sp):
                sp.dma_start(src_i[:, :], a["src"]).then_inc(edges_in, 16)
                sp.dma_start(dst_i[:, :], a["dst"]).then_inc(edges_in, 16)
                sp.dma_start(w_e[:, :], a["edge_weight"]).then_inc(edges_in, 16)
                sp.dma_start(k.x[:, :, :], a["x"]).then_inc(x_in, 16)
                sp.wait_ge(consts, 1)
                sp.dma_start(k.edges_d.rearrange("(p t) c -> p (t c)", p=128),
                             k.edges[:, :, :].rearrange("p t c -> p (t c)")).then_inc(prefilled, 16)
                fills = 0
                for buf, rows in ((k.buf[0], X * ROW0), (k.buf[1], NCH * CH)):
                    for r in range(0, rows, 1024):
                        sp.dma_start(buf[r:r + 1024, :].rearrange("(p t) c -> p (t c)", p=128),
                                     zero[:, :]).then_inc(zeroed, 16)
                        fills += 1
                sp.wait_ge(normed, T)
                sp.dma_start(k.xn_d.rearrange("(t p) c -> p t c", p=P), k.xn[:, :, :]).then_inc(xn_out, 16)
                one_ahead(sp, *stage_free)
                with sp.Fori(0, EC // 16) as r:
                    for h in range(2):
                        sp.wait_ge(scattered[h], r * 128 + 128)
                        sp.sem_inc(stage_free[h], 1)
                sp.dma_start(k.edges[:, :, :].rearrange("p t c -> p (t c)"),
                             k.edges_d.rearrange("(p t) c -> p (t c)", p=128)).then_inc(reload, 16)
                sp.wait_ge(reload, 16)
                sp.wait_ge(xn_out, 16)
                sp.wait_ge(zeroed, 16 * fills)

            @block.gpsimd
            def _(g):
                ch = Chain(g, iotas)
                ch.mark(g.memset(k.edges[:, :, :], 0.0))
                ch.mark(g.memset(zero[:, :], 0.0))
                ch.link(g.memset(k.ones[:, :], 1.0))
                ch.link(g.memset(k.edges[:, :, 1], -1.0))
                ch.mark(g.iota(iota_i[:, :], pattern=[[1, 128]], base=0, channel_multiplier=0))
                ch.mark(g.iota(tix_i[:, :], pattern=[[1, ETP]], base=0, channel_multiplier=0))
                ch.mark(g.affine_select(out=k.ident[:, :], in_=k.ones[:, :], compare_op=ALU.is_equal, fill=0.0,
                                        base=0, pattern=[[-1, 128]], channel_multiplier=1))
                ch.mark(g.affine_select(out=k.tri[:, :], in_=k.ones[:, :], compare_op=ALU.is_gt, fill=0.0,
                                        base=0, pattern=[[1, 128]], channel_multiplier=-1))
                ch.link(g.affine_select(out=k.tri1[:, :], in_=k.ones[:, :], compare_op=ALU.is_ge, fill=0.0,
                                        base=0, pattern=[[1, 128]], channel_multiplier=-1))
                ch.mark(g.tensor_copy(k.iota[:, :], iota_i[:, :]))
                ch.link(g.tensor_copy(tix[:, :], tix_i[:, :]))
                g.memset(nconst[:, :], float(N)).then_inc(consts, 1)
                g.wait_ge(prefilled, 16)
                with g.Fori(0, EC // 16) as r:
                    for h in range(2):
                        g.wait_ge(staged[h], r * 2 + 2)
                        g.sem_inc(begun, 1)
                        for j in range(8):
                            g.indirect_dma_start(
                                out=k.edges_d,
                                out_offset=bass.IndirectOffsetOnAxis(ap=idx_st[:, h, j:j + 1], axis=0),
                                in_=rec_st[:, h, j, :], in_offset=None).then_inc(scattered[h], 16)

            @block.scalar
            def _(s):
                for name in WEIGHTS:
                    ap = k.w[name]
                    s.dma_start(ap[tuple(slice(None) for _ in ap.shape)], a[name]).then_inc(w_in, 16)
                norm_root_scalar(s, k, var_ready, root_ready, 1)
                s.wait_ge(idx_ready, 1)
                with s.Fori(0, EC // 16) as r:
                    for h in range(2):
                        s.wait_ge(stage_free[h], r + 1)
                        col = bass.ds(r * 16 + h * 8, 8)
                        s.activation(idx_st[:, h, :], pos[:, col], ACT.Copy).then_inc(staged[h], 1)
                        s.activation(rec_st[:, h, :, :], rec[:, col, :], ACT.Copy).then_inc(staged[h], 1)

            @block.vector
            def _(v):
                ch = Chain(v, vec)
                ln = Chain(v, lnc)
                v.wait_ge(edges_in, 48)
                ch.mark(v.tensor_copy(src_f[:, :], src_i[:, :]))
                ch.mark(v.tensor_copy(rec[:, :, 0], dst_i[:, :]))
                ch.mark(v.tensor_copy(rec[:, :, 2], w_e[:, :]))
                ch.mark(v.memset(rec[:, :, 3], 0.0))
                ch.join()
                ch.link(v.tensor_scalar(bin_f[:, :], src_f[:, :], 1.0 / P, 0.5 / P - 0.5, ALU.mult, ALU.add))
                ch.link(v.tensor_scalar(bin_f[:, :], bin_f[:, :], ROUND, ROUND, ALU.add, ALU.subtract))
                ch.mark(v.scalar_tensor_tensor(rec[:, :, 1], bin_f[:, :], -float(P), src_f[:, :], ALU.mult, ALU.add))
                for b in range(T):
                    ch.mark(v.tensor_scalar(mask[:, b, :], bin_f[:, :], float(b), None, ALU.is_equal))
                ch.join()
                for b in range(T):
                    ch.mark(v.tensor_tensor_scan(run[:, b, :], mask[:, b, :], mask[:, b, :], 0.0, ALU.add, ALU.max))
                ch.join()
                v.tensor_copy(cnt[:, :], run[:, :, EC - 1]).then_inc(cnt_ready, 1)
                v.wait_ge(prefix, 2)
                ch.link(v.tensor_scalar(tot_i[:, :], pc[:, 32:32 + T], 127.0, None, ALU.add))
                ch.link(v.tensor_scalar(tot_i[:, :], tot_i[:, :], 7, None, ALU.logical_shift_right))
                ch.link(v.tensor_copy(tiles[:, :], tot_i[:, :]))
                v.wait_ge(iotas, 11)
                ch.link(v.tensor_tensor_scan(tiles_to[:, :], k.ones[:, 0:T], tiles[:, :], 0.0, ALU.mult, ALU.add))
                ch.link(v.tensor_tensor(off[:, :], tiles_to[:, :], tiles[:, :], ALU.subtract))
                ch.link(v.tensor_scalar(off[:, :], off[:, :], 128.0, -1.0, ALU.mult, ALU.add))
                ch.link(v.tensor_tensor(off[0:P, :], off[0:P, :], pc[0:P, 0:T], ALU.add))
                for b in range(T):
                    ch.link(v.scalar_tensor_tensor(run[:, b, :], run[:, b, :], off[0:P, b:b + 1], mask[:, b, :],
                                                   ALU.add, ALU.mult))
                    if b == 0:
                        ch.link(v.tensor_copy(tmp[:, :], run[:, b, :]))
                    else:
                        ch.link(v.tensor_tensor(tmp[:, :], tmp[:, :], run[:, b, :], ALU.add))
                ch.link(v.tensor_copy(pos_i[:, :], tmp[:, :]))
                ch.mark(v.tensor_scalar(low_i[:, :], pos_i[:, :], 127, None, ALU.bitwise_and))
                ch.link(v.tensor_scalar(pos_i[:, :], pos_i[:, :], 7, None, ALU.logical_shift_right))
                ch.mark(v.tensor_copy(tmp[:, :], low_i[:, :]))
                ch.link(v.tensor_copy(pos[:, :], pos_i[:, :]))
                v.scalar_tensor_tensor(pos[:, :], tmp[:, :], float(ETP), pos[:, :], ALU.mult, ALU.add)\
                    .then_inc(idx_ready, 1)
                v.wait_ge(x_in, 16)
                for t in range(T):
                    ln.mark(v.bn_stats(k.stats[:, t, :], k.x[:, t, :]))
                ln.join()
                norm_scale_vector(nc, v, ln, k, var_ready, root_ready, 1)
                for t in range(T):
                    v.tensor_scalar(k.xn[:, t, :], k.x[:, t, :], k.mean[:, t:t + 1], k.rstd[:, t:t + 1],
                                    ALU.subtract, ALU.mult).then_inc(normed, 1)
                v.wait_ge(normed, T)
                ln.mark(v.tensor_copy(k.acc[:, :, :], k.xn[:, :, :]))
                ln.link(v.tensor_scalar(tb[:, :], tix[:, :], tiles_to[0:1, 0:1], None, ALU.is_ge))
                for b in range(1, T - 1):
                    ln.link(v.scalar_tensor_tensor(tb[:, :], tix[:, :], tiles_to[0:1, b:b + 1], tb[:, :],
                                                   ALU.is_ge, ALU.add))
                ln.mark(v.tensor_copy(k.tile_bin[:, :], tb[:, :]))
                ln.mark(v.memset(KV[:, :, :], 0.0))
                v.wait_ge(gram_done, 1)
                for i in range(KD):
                    v.tensor_copy(G[:, i, :], pg[i][:, 0:D]).then_inc(mix_copied, 1)
                v.tensor_copy(scol[:, :], pcol[:, 0:KD]).then_inc(mix_copied, 1)
                v.tensor_copy(srow[:, :], psr[0:1, 0:D]).then_inc(mix_copied, 1)
                v.wait_ge(mixed, 1)
                for i in range(KD):
                    v.tensor_copy(U[:, i, :], pu[i][:, 0:D]).then_inc(mix_copied, 1)
                v.tensor_copy(Ul[:, :], psr[0:1, 0:D]).then_inc(mix_copied, 1)
                v.wait_ge(mixed, 2)
                ln.join()
                for h in range(HEADS):
                    i, q = h * HD // 128, h * HD % 128
                    v.tensor_scalar(KV[q:q + HD, i, h * HD:(h + 1) * HD], pu[i][q:q + HD, h * HD:(h + 1) * HD],
                                    1.0 / N, None, ALU.mult).then_inc(mix_copied, 1)
                v.wait_ge(mixed, 3)
                for i in range(KD):
                    v.tensor_copy(M2[:, i, :], pu[i][:, 0:D]).then_inc(mix_copied, 1)
                v.wait_ge(mixed, 4)
                for i in range(KD):
                    v.tensor_copy(k.R[:, i, :], pu[i][:, 0:D]).then_inc(mix_copied, 1)
                ln.link(v.tensor_tensor(k.r0[:, :], psr[0:1, 0:D], k.w["m0_bfc"][:, :], ALU.add))
                ln.link(v.tensor_tensor(k.r0[:, :], k.r0[:, :], k.w["g0_b2"][:, :], ALU.add))

            @block.tensor
            def _(pe):
                pe.wait_ge(cnt_ready, 1)
                pe.wait_ge(iotas, 11)
                nc.tensor.matmul(pc[0:P, 0:T], k.tri[0:P, 0:P], cnt[:, :], start=True, stop=True).then_inc(prefix, 1)
                nc.tensor.matmul(pc[:, 32:32 + T], k.ones[0:P, :], cnt[:, :], start=True, stop=True).then_inc(prefix, 1)
                for t in range(T):
                    pe.wait_ge(normed, t + 1)
                    for i in range(KD):
                        nc.tensor.matmul(pg[i][:, 0:D], k.xn[:, t, i * 128:(i + 1) * 128], k.xn[:, t, :],
                                         start=t == 0, stop=t == T - 1)
                    nc.tensor.matmul(psr[0:1, 0:D], k.ones[0:P, 0:1], k.xn[:, t, :], start=t == 0, stop=t == T - 1)
                for i in range(KD):
                    for t in range(T):
                        last = nc.tensor.matmul(pcol[:, i:i + 1], k.xn[:, t, i * 128:(i + 1) * 128],
                                                k.ones[0:P, 0:1], start=t == 0, stop=t == T - 1)
                last.then_inc(gram_done, 1)
                pe.wait_ge(w_in, 16 * len(WEIGHTS))
                pe.wait_ge(mix_copied, KD + 2)
                pe.wait_ge(consts, 1)
                w = k.w
                for i in range(KD):
                    for j in range(KD):
                        nc.tensor.matmul(pu[i][:, 0:D], G[:, j, i * 128:(i + 1) * 128], w["m0_WvT"][:, j, :],
                                         start=j == 0, stop=False)
                    nc.tensor.matmul(pu[i][:, 0:D], srow[:, i * 128:(i + 1) * 128], w["m0_bv"][:, :],
                                     start=False, stop=True)
                for j in range(KD):
                    nc.tensor.matmul(psr[0:1, 0:D], scol[:, j:j + 1], w["m0_WvT"][:, j, :], start=j == 0, stop=False)
                nc.tensor.matmul(psr[0:1, 0:D], nconst[:, :], w["m0_bv"][:, :], start=False, stop=True)\
                    .then_inc(mixed, 1)
                pe.wait_ge(mix_copied, 2 * (KD + 1) + 1)
                for i in range(KD):
                    for j in range(KD):
                        nc.tensor.matmul(pu[i][:, 0:D], U[:, j, i * 128:(i + 1) * 128], w["m0_WkT"][:, j, :],
                                         start=j == 0, stop=False)
                    last = nc.tensor.matmul(pu[i][:, 0:D], Ul[:, i * 128:(i + 1) * 128], w["m0_bk"][:, :],
                                            start=False, stop=True)
                last.then_inc(mixed, 1)
                n = 2 * (KD + 1) + 1 + HEADS
                pe.wait_ge(mix_copied, n)
                for i in range(KD):
                    for j in range(KD):
                        last = nc.tensor.matmul(pu[i][:, 0:D], KV[:, j, i * 128:(i + 1) * 128],
                                                w["m0_WfcT"][:, j, :], start=j == 0, stop=j == KD - 1)
                last.then_inc(mixed, 1)
                pe.wait_ge(mix_copied, n + KD)
                for i in range(KD):
                    for j in range(KD):
                        nc.tensor.matmul(pu[i][:, 0:D], w["m0_Wq"][:, j, i * 128:(i + 1) * 128], M2[:, j, :],
                                         start=j == 0, stop=j == KD - 1)
                for j in range(KD):
                    last = nc.tensor.matmul(psr[0:1, 0:D], w["m0_bqc"][:, j:j + 1], M2[:, j, :],
                                            start=j == 0, stop=j == KD - 1)
                last.then_inc(mixed, 1)


def bins_of(nc, k, engine, r, h):
    _, bins = nc.values_load_multi_w_load_instructions(
        k.tile_bin[0:1, bass.ds(r * EB + h * (EB // 2), EB // 2)], engines=(engine,), min_val=0, max_val=T - 1,
        skip_runtime_bounds_check_because="a count of at most T - 1 node tiles")
    return bins


def aggregate(nc, a, k, layer):
    width = (D, XJW)[layer]
    table = (k.xn_d, k.xj_d)[layer]
    H = EB // 2
    with ExitStack() as c:
        def sem(name):
            return k.sem(nc, f"{name}{layer}")

        rows = c.enter_context(nc.sbuf_tensor(f"edge_rows{layer}", [128, EB, width], F32))
        hot = c.enter_context(nc.sbuf_tensor(f"one_hot{layer}", [128, EB, P], F32))
        att = c.enter_context(nc.sbuf_tensor(f"att{layer}", [128, EB, P], F32)) if layer else None
        idx = c.enter_context(nc.sbuf_tensor(f"gather_idx{layer}", [128, 2, H], I32))
        part = [c.enter_context(nc.psum_tensor(f"p_part{layer}_{i}", [128, 512], F32)) for i in range(4)]
        staged = [sem(f"idx_staged{h}_") for h in range(2)]
        landed, past = k.landed, layer * (ET // EB) * 16
        begun = sem("gather_begun")
        att_ready, hot_ready, summed, added = sem("att_ready"), sem("hot_ready"), sem("summed"), sem("added")

        with nc.Block() as block:
            @block.gpsimd
            def _(g):
                with g.Fori(0, ET // EB) as r:
                    for s in range(EB):
                        if s % H == 0:
                            g.wait_ge(staged[s // H], r + 1)
                            g.sem_inc(begun, 1)
                        g.indirect_dma_start(
                            out=rows[:, s, :], out_offset=None, in_=table,
                            in_offset=bass.IndirectOffsetOnAxis(ap=idx[:, s // H, s % H:s % H + 1], axis=0))\
                            .then_inc(landed[s], 16)

            @block.scalar
            def _(sc):
                for h in range(2):
                    sc.activation(idx[:, h, :], k.edges[:, h * H:(h + 1) * H, 0], ACT.Copy).then_inc(staged[h], 1)
                with sc.Fori(0, ET // EB) as r:
                    for h in range(2):
                        if layer:
                            bins = bins_of(nc, k, mybir.EngineType.Activation, r, h)
                            for j in range(H):
                                s = h * H + j
                                sc.wait_ge(landed[s], past + r * 16 + 16)
                                sc.activation(att[:, s:s + 1, :], k.a1[:, bass.ds(bins[j], 1), :], ACT.Sigmoid,
                                              bias=rows[:, s, D:D + 1]).then_inc(att_ready, 1)
                        sc.wait_ge(summed, r * EB + (h + 1) * H)
                        sc.activation(idx[:, h, :], k.edges[:, bass.ds(r * EB + EB + h * H, H), 0], ACT.Copy)\
                            .then_inc(staged[h], 1)

            @block.vector
            def _(v):
                one_ahead(v, added)
                with v.Fori(0, ET // EB) as r:
                    for h in range(2):
                        bins = bins_of(nc, k, mybir.EngineType.DVE, r, h)
                        for j in range(H):
                            s = h * H + j
                            e = k.edges[:, bass.ds(r * EB + s, 1), :]
                            if layer:
                                v.wait_ge(att_ready, r * EB + s + 1)
                                v.scalar_tensor_tensor(hot[:, s, :], k.iota[:, 0:P], e[:, 0, 1:2], att[:, s, :],
                                                       ALU.is_equal, ALU.mult).then_inc(hot_ready, 1)
                            else:
                                v.tensor_scalar(hot[:, s, :], k.iota[:, 0:P], e[:, 0, 1:2], e[:, 0, 2:3],
                                                ALU.is_equal, ALU.mult).then_inc(hot_ready, 1)
                        for j in range(H):
                            s = h * H + j
                            dst = k.acc[:, bass.ds(bins[j], 1), :]
                            v.wait_ge(summed, r * EB + s + 1)
                            v.wait_ge(added, 1 + r * EB + s)
                            v.tensor_tensor(dst, dst, part[s % 4][0:P, 0:D].unsqueeze(1), ALU.add)\
                                .then_inc(added, 1)

            @block.tensor
            def _(pe):
                with pe.Fori(0, ET // EB) as r:
                    for s in range(EB):
                        pe.wait_ge(landed[s], past + r * 16 + 16)
                        pe.wait_ge(hot_ready, r * EB + s + 1)
                        pe.wait_ge(added, 1 + r * EB + max(s - 3, 0))
                        nc.tensor.matmul(part[s % 4][0:P, 0:D], hot[:, s, :], rows[:, s, 0:D],
                                         start=True, stop=True).then_inc(summed, 1)


def gin_and_attention(nc, a, k):
    KH = F0 // 128
    w = k.w
    with ExitStack() as c:
        def sb(name, shape):
            return c.enter_context(nc.sbuf_tensor(name, shape, F32))

        def sem(name):
            return k.sem(nc, name)

        def ps(name):
            return c.enter_context(nc.psum_tensor(name, [128, 512], F32))

        hs, xs = sb("gin_rows", [P, GT, D]), sb("mix_rows", [P, GT, D])
        xT, hT = sb("gin_T", [128, GT, 2 * KD, P]), sb("gin_hidden", [128, GT, KH, P])
        pT, pH, pO = [ps(f"p_gT{i}") for i in range(2)], [ps(f"p_gH{i}") for i in range(2)], [ps(f"p_gO{i}") for i in range(2)]
        rows_in, turned, copied = sem("g_rows_in"), sem("g_turned"), sem("g_copied")
        up, relued, down, added, stat = sem("g_up"), sem("g_relued"), sem("g_down"), sem("g_added"), sem("g_stat")

        with nc.Block() as block:
            @block.scalar
            def _(s):
                one_ahead(s, relued)
                with s.Fori(0, GR) as r:
                    s.wait_ge(down, 1 + r * GT)
                    s.activation(hs[:, :, :], k.acc[:, bass.ds(r * GT, GT), :], ACT.Copy).then_inc(rows_in, 1)
                    s.activation(xs[:, :, :], k.xn[:, bass.ds(r * GT, GT), :], ACT.Copy).then_inc(rows_in, 1)
                    for t in range(GT):
                        s.wait_ge(up, r * GT + t + 1)
                        for f in range(KH):
                            s.activation(hT[:, t, f, :], pH[t % 2][:, f * P:(f + 1) * P], ACT.Relu,
                                         bias=w["g0_b1"][:, f:f + 1]).then_inc(relued, 1)

            @block.vector
            def _(v):
                one_ahead(v, copied, added)
                with v.Fori(0, GR) as r:
                    for t in range(GT):
                        v.wait_ge(turned, r * GT + t + 1)
                        v.tensor_copy(xT[:, t, :, :], pT[t % 2][:, 0:2 * KD * P]
                                      .rearrange("p (a b) -> p a b", a=2 * KD)).then_inc(copied, 1)
                    for t in range(GT):
                        x = k.x[:, bass.ds(r * GT + t, 1), :]
                        v.wait_ge(down, 1 + r * GT + t + 1)
                        v.tensor_tensor(x, x, pO[t % 2][0:P, 0:D].unsqueeze(1), ALU.add).then_inc(added, 1)
                        v.wait_ge(added, 1 + r * GT + t + 1)
                        v.bn_stats(k.stats[:, bass.ds(r * GT + t, 1), :], x)

            @block.tensor
            def _(pe):
                one_ahead(pe, down)
                with pe.Fori(0, GR) as r:
                    pe.wait_ge(rows_in, r * 2 + 2)
                    for t in range(GT):
                        pe.wait_ge(copied, 1 + r * GT + max(t - 1, 0))
                        for q, rows in enumerate((hs, xs)):
                            for i in range(KD):
                                j = q * KD + i
                                last = nc.tensor.transpose(pT[t % 2][:, j * P:(j + 1) * P],
                                                           rows[:, t, i * 128:(i + 1) * 128], k.ident[0:P, 0:P])
                        last.then_inc(turned, 1)
                    for t in range(GT):
                        pe.wait_ge(copied, 1 + r * GT + t + 1)
                        pe.wait_ge(relued, 1 + r * GT * KH + max(t - 1, 0) * KH)
                        for f in range(KH):
                            for i in range(KD):
                                last = nc.tensor.matmul(pH[t % 2][:, f * P:(f + 1) * P],
                                                        w["g0_W1"][:, i, f * 128:(f + 1) * 128], xT[:, t, i, :],
                                                        start=i == 0, stop=i == KD - 1)
                        last.then_inc(up, 1)
                    for t in range(GT):
                        pe.wait_ge(relued, 1 + r * GT * KH + (t + 1) * KH)
                        pe.wait_ge(added, 1 + r * GT + max(t - 1, 0))
                        out = pO[t % 2][0:P, 0:D]
                        for i in range(KD):
                            nc.tensor.matmul(out, xT[:, t, KD + i, :], k.R[:, i, :], start=i == 0, stop=False)
                        nc.tensor.matmul(out, k.ones[0:1, 0:P], k.r0[:, :], start=False, stop=False)
                        for f in range(KH):
                            last = nc.tensor.matmul(out, hT[:, t, f, :], w["g0_W2"][:, f, :],
                                                    start=False, stop=f == KH - 1)
                        last.then_inc(down, 1)


def first_max(v, ch, lg, mx, rev, oh, at):
    ch.link(v.tensor_reduce(mx, lg, AX.X, ALU.max))
    ch.link(v.tensor_tensor(oh, lg, mx.unsqueeze(2).broadcast_to([P, T, X]), ALU.is_equal))
    ch.link(v.tensor_tensor(oh, oh, rev, ALU.mult))
    ch.link(v.tensor_reduce(at, oh, AX.X, ALU.max))
    ch.link(v.tensor_tensor(oh, rev, at.unsqueeze(2).broadcast_to([P, T, X]), ALU.is_equal))


def route(nc, a, k, layer):
    w = k.w
    picks = layer + 1
    gw, gb = w[f"f{layer}_gw"], w[f"f{layer}_gb"]
    with ExitStack() as c:
        def sb(name, shape, dt=F32):
            return c.enter_context(nc.sbuf_tensor(f"{name}_r{layer}", shape, dt))

        def sem(name):
            return k.sem(nc, f"{name}_r{layer}")

        def ps(name):
            return c.enter_context(nc.psum_tensor(f"{name}_r{layer}", [128, 512], F32))

        xs, xT = sb("rows", [P, GT, D]), sb("rowsT", [128, GT, KD, P])
        lg, lg2, rev, tmp = sb("logits", [P, T, X]), sb("logits2", [P, T, X]), sb("rev", [P, T, X]), sb("tmp", [P, T, X])
        oh = [sb(f"onehot{i}", [P, T, X]) for i in range(2)]
        both, tot, upto = sb("both", [P, T, X]), sb("tot", [P, T, X]), sb("upto", [P, T, X])
        mx = [sb(f"mx{i}", [P, T]) for i in range(2)]
        at = [sb(f"at{i}", [P, T]) for i in range(2)]
        e2, inv, pos, keep, node = sb("e2", [P, T]), sb("inv", [P, T]), sb("pos", [P, T]), sb("keep", [P, T]), sb("node", [P, T])
        ch_i, chn, cto = sb("chunks_i", [P, X], I32), sb("chunks", [P, X]), sb("chunks_to", [P, X])
        cx, cix, cix_i = sb("cx", [1, NCH]), sb("cix", [1, NCH]), sb("cix_i", [1, NCH], I32)
        rev_i, node_i = sb("rev_i", [P, T, X], I32), sb("node_i", [P, T], I32)
        pT, pL, pC, pN = [ps(f"p_T{i}") for i in range(2)], ps("p_L"), ps("p_cum"), ps("p_tot")
        normed, turned, copied, kept_x, logits = sem("normed"), sem("turned"), sem("copied"), sem("kept_x"), sem("logits")
        vec, var_ready, root_ready, iotas = sem("vec"), sem("var"), sem("root"), sem("iotas")
        e_in, e_out, hot_ready, cum_ready = sem("e_in"), sem("e_out"), sem("hot_ready"), sem("cum_ready")
        slots_ready, scattered = sem("slots_ready"), sem("scattered")

        with nc.Block() as block:
            @block.gpsimd
            def _(g):
                g.iota(rev_i[:, :, :], pattern=[[0, T], [-1, X]], base=X, channel_multiplier=0).then_inc(iotas, 1)
                g.iota(node_i[:, :], pattern=[[P, T]], base=X * ROW0, channel_multiplier=1).then_inc(iotas, 1)
                g.iota(cix_i[:, :], pattern=[[1, NCH]], base=0, channel_multiplier=0).then_inc(iotas, 1)
                g.wait_ge(slots_ready, 1)
                for t in range(T):
                    for i in range(picks):
                        g.indirect_dma_start(
                            out=k.buf[layer], out_offset=bass.IndirectOffsetOnAxis(ap=k.slots[:, i, t:t + 1], axis=0),
                            in_=k.xn[:, t, :], in_offset=None).then_inc(scattered, 16)
                g.wait_ge(scattered, 16 * T * picks)

            @block.scalar
            def _(s):
                one_ahead(s, kept_x, copied)
                norm_root_scalar(s, k, var_ready, root_ready, 1)
                with s.Fori(0, GR) as r:
                    s.wait_ge(logits, 1 + r * GT)
                    for t in range(GT):
                        s.wait_ge(turned, r * GT + t + 1)
                        s.activation(xT[:, t, :, :], pT[t % 2][:, 0:KD * P].rearrange("p (a b) -> p a b", a=KD),
                                     ACT.Copy).then_inc(copied, 1)
                        s.activation(k.xn[:, bass.ds(r * GT + t, 1), :], xs[:, t:t + 1, :], ACT.Copy)\
                            .then_inc(kept_x, 1)
                s.wait_ge(e_in, 1)
                if layer == 0:
                    s.activation(tmp[:, :, :], tmp[:, :, :], ACT.Exp).then_inc(e_out, 1)
                else:
                    s.activation(e2[:, :], e2[:, :], ACT.Exp).then_inc(e_out, 1)

            @block.tensor
            def _(pe):
                one_ahead(pe, logits)
                with pe.Fori(0, GR) as r:
                    for t in range(GT):
                        pe.wait_ge(normed, r * GT + t + 1)
                        pe.wait_ge(copied, 1 + r * GT + max(t - 1, 0))
                        for i in range(KD):
                            last = nc.tensor.transpose(pT[t % 2][:, i * P:(i + 1) * P],
                                                       xs[:, t, i * 128:(i + 1) * 128], k.ident[0:P, 0:P])
                        last.then_inc(turned, 1)
                    for t in range(GT):
                        pe.wait_ge(copied, 1 + r * GT + t + 1)
                        for i in range(KD):
                            last = nc.tensor.matmul(pL[0:P, bass.ds((r * GT + t) * X, X)], xT[:, t, i, :], gw[:, i, :],
                                                    start=i == 0, stop=i == KD - 1)
                        last.then_inc(logits, 1)
                pe.wait_ge(hot_ready, 1)
                hot = both[:, :, :].rearrange("p t x -> p (t x)")
                nc.tensor.matmul(pC[0:P, 0:T * X], k.tri1[0:P, 0:P], hot, start=True, stop=True)
                nc.tensor.matmul(pN[0:P, 0:T * X], k.ones[0:P, 0:P], hot, start=True, stop=True).then_inc(cum_ready, 1)

            @block.vector
            def _(v):
                ch = Chain(v, vec)
                norm_scale_vector(nc, v, ch, k, var_ready, root_ready, 1)
                with v.Fori(0, GR) as r:
                    for t in range(GT):
                        if t == 0:
                            v.wait_ge(kept_x, 1 + r * GT)
                        one = bass.ds(r * GT + t, 1)
                        v.tensor_scalar(xs[:, t:t + 1, :], k.x[:, one, :], k.mean[:, one], k.rstd[:, one],
                                        ALU.subtract, ALU.mult).then_inc(normed, 1)
                v.wait_ge(iotas, 3)
                ch.mark(v.tensor_copy(rev[:, :, :], rev_i[:, :, :]))
                ch.mark(v.tensor_copy(node[:, :], node_i[:, :]))
                ch.mark(v.tensor_copy(cix[:, :], cix_i[:, :]))
                v.wait_ge(logits, 1 + T)
                view = "p (t x) -> p t x"
                ch.link(v.tensor_tensor(lg[:, :, :], pL[0:P, 0:T * X].rearrange(view, x=X), gb[0:P, :, :], ALU.add))
                first_max(v, ch, lg[:, :, :], mx[0][:, :], rev[:, :, :], oh[0][:, :, :], at[0][:, :])
                if layer == 0:
                    v.tensor_tensor(tmp[:, :, :], lg[:, :, :], mx[0][:, :].unsqueeze(2).broadcast_to([P, T, X]),
                                    ALU.subtract).then_inc(e_in, 1)
                    v.tensor_copy(both[:, :, :], oh[0][:, :, :]).then_inc(hot_ready, 1)
                    v.wait_ge(e_out, 1)
                    ch.link(v.tensor_reduce(inv[:, :], tmp[:, :, :], AX.X, ALU.add))
                    ch.link(v.reciprocal(inv[:, :], inv[:, :]))
                else:
                    ch.link(v.scalar_tensor_tensor(lg2[:, :, :], oh[0][:, :, :], -BIG, lg[:, :, :], ALU.mult, ALU.add))
                    first_max(v, ch, lg2[:, :, :], mx[1][:, :], rev[:, :, :], oh[1][:, :, :], at[1][:, :])
                    v.tensor_tensor(both[:, :, :], oh[0][:, :, :], oh[1][:, :, :], ALU.add).then_inc(hot_ready, 1)
                    v.tensor_tensor(e2[:, :], mx[1][:, :], mx[0][:, :], ALU.subtract).then_inc(e_in, 1)
                    v.wait_ge(e_out, 1)
                    ch.link(v.tensor_scalar(inv[:, :], e2[:, :], 1.0, None, ALU.add))
                    ch.link(v.reciprocal(k.gate[:, 0, :], inv[:, :]))
                    ch.mark(v.tensor_tensor(k.gate[:, 1, :], k.gate[:, 0, :], e2[:, :], ALU.mult))
                v.wait_ge(cum_ready, 1)
                ch.link(v.tensor_copy(tot[:, :, :], pN[0:P, 0:T * X].rearrange(view, x=X)))
                for e in range(X):
                    ch.mark(v.tensor_tensor_scan(upto[:, :, e], k.ones[0:P, 0:T], tot[:, :, e], 0.0, ALU.mult, ALU.add))
                ch.join()
                ch.link(v.tensor_tensor(tot[:, :, :], upto[:, :, :], tot[:, :, :], ALU.subtract))
                ch.link(v.scalar_tensor_tensor(tot[:, :, :], tot[:, :, :], -1.0,
                                               pC[0:P, 0:T * X].rearrange(view, x=X), ALU.add, ALU.add))
                if layer == 0:
                    ch.link(v.tensor_tensor(tot[:, :, :], tot[:, :, :], oh[0][:, :, :], ALU.mult))
                    ch.link(v.tensor_reduce(pos[:, :], tot[:, :, :], AX.X, ALU.add))
                    ch.link(v.tensor_scalar(keep[:, :], pos[:, :], float(CAP0), None, ALU.is_lt))
                    ch.mark(v.tensor_tensor(k.gate[:, 0, :], inv[:, :], keep[:, :], ALU.mult))
                    ch.link(v.tensor_scalar(at[1][:, :], at[0][:, :], -float(ROW0), float(X * ROW0), ALU.mult, ALU.add))
                    ch.link(v.scalar_tensor_tensor(mx[1][:, :], pos[:, :], float(CAP0 - 1), at[1][:, :], ALU.min, ALU.add))
                    ch.mark(v.tensor_copy(k.back[:, 0, :], mx[1][:, :]))
                    ch.link(v.tensor_tensor(mx[0][:, :], mx[1][:, :], node[:, :], ALU.subtract))
                    ch.link(v.tensor_tensor(mx[0][:, :], mx[0][:, :], keep[:, :], ALU.mult))
                    ch.link(v.tensor_tensor(mx[0][:, :], mx[0][:, :], node[:, :], ALU.add))
                    v.tensor_copy(k.slots[:, 0, :], mx[0][:, :]).then_inc(slots_ready, 1)
                else:
                    ch.link(v.tensor_scalar(ch_i[:, :], upto[:, T - 1, :], float(CH - 1), None, ALU.add))
                    ch.link(v.tensor_scalar(ch_i[:, :], ch_i[:, :], CH.bit_length() - 1, None, ALU.logical_shift_right))
                    ch.link(v.tensor_copy(chn[:, :], ch_i[:, :]))
                    ch.link(v.tensor_tensor_scan(cto[:, :], k.ones[0:P, 0:X], chn[:, :], 0.0, ALU.mult, ALU.add))
                    ch.link(v.tensor_tensor(chn[:, :], cto[:, :], chn[:, :], ALU.subtract))
                    ch.link(v.tensor_scalar(chn[:, :], chn[:, :], float(CH), None, ALU.mult))
                    ch.link(v.tensor_tensor(tot[:, :, :], tot[:, :, :],
                                            chn[:, :].unsqueeze(1).broadcast_to([P, T, X]), ALU.add))
                    for i in range(2):
                        ch.link(v.tensor_tensor(tmp[:, :, :], tot[:, :, :], oh[i][:, :, :], ALU.mult))
                        ch.link(v.tensor_reduce(pos[:, :], tmp[:, :, :], AX.X, ALU.add))
                        ch.mark(v.tensor_copy(k.back[:, i, :], pos[:, :]))
                        ch.link(v.tensor_copy(k.slots[:, i, :], pos[:, :]))
                    ch.link(v.tensor_scalar(cx[:, :], cix[:, :], cto[0:1, 0:1], None, ALU.is_ge))
                    for e in range(1, X - 1):
                        ch.link(v.scalar_tensor_tensor(cx[:, :], cix[:, :], cto[0:1, e:e + 1], cx[:, :], ALU.is_ge, ALU.add))
                    v.tensor_copy(k.chunk_x[:, :], cx[:, :]).then_inc(slots_ready, 1)


def experts(nc, a, k, layer):
    chunks = (X, NCH)[layer]
    stride = (ROW0, CH)[layer]
    n = (CAP0, CH)[layer]
    nt = -(-n // 128)
    size = [min(128, n - 128 * t) for t in range(nt)]
    act = (ACT.Relu, ACT.Gelu)[layer]
    buf, ybuf = k.buf[layer], k.ybuf[layer]
    with ExitStack() as c:
        def sb(name, shape):
            return c.enter_context(nc.sbuf_tensor(f"{name}_e{layer}", shape, F32))

        def sem(name):
            return k.sem(nc, f"{name}_e{layer}")

        def ps(name):
            return c.enter_context(nc.psum_tensor(f"{name}_e{layer}", [128, 512], F32))

        W = [big[:, :, :].rearrange("p t c -> p (t c)")[:, 0:PACK] for big in (k.acc_all, k.xn_all)]
        rows = sb("rows", [128, 2, nt, D])
        xT = sb("rowsT", [128, 2, KD, n])
        hT = [k.xnT[:, :, :].rearrange("p i n -> p (i n)")[:, 0:KF * n].rearrange("p (f n) -> p f n", n=n),
              sb("hidden", [128, KF, n])]
        y = sb("out_rows", [128, 2, nt, D])
        pT, pH, pY = [ps(f"p_T{i}") for i in range(KD)], [ps(f"p_H{i}") for i in range(2)], [ps(f"p_Y{i}") for i in range(2)]
        w_in, rows_in, y_out = ([sem(f"{s}{h}") for h in range(2)] for s in ("w_in", "rows_in", "y_out"))
        turned, copied, up, acted, down, biased = (sem(s) for s in ("turned", "copied", "up", "acted", "down", "biased"))
        biased_init = sem("biased_init")
        y_free = [sem(f"y_free{h}") for h in range(2)]

        def w1(h, i, f):
            at = i * FF + f * 128
            return W[h][:, at:at + 128]

        def w2(h, f):
            at = PK1 + f * D
            return W[h][:, at:at + D]

        def b1(h, f):
            return W[h][:, PK1 + PK2 + f:PK1 + PK2 + f + 1]

        def b2(h, rows_n):
            return W[h][0:rows_n, PK1 + PK2 + PKB:PACK]

        with nc.Block() as block:
            @block.gpsimd
            def _(g):
                one_ahead(g, *y_free)
                with g.Fori(0, chunks // 2) as r:
                    for h in range(2):
                        g.wait_ge(y_out[h], r * 16 + 16)
                        g.sem_inc(y_free[h], 1)

            @block.sync
            def _(sp):
                with sp.Fori(0, chunks // 2) as r:
                    for h in range(2):
                        if layer:
                            e = sp.value_load(k.chunk_x[0:1, bass.ds(r * 2 + h, 1)], min_val=0, max_val=X - 1)
                        else:
                            e = r * 2 + h
                        sp.wait_ge(y_free[h], r + 1)
                        sp.dma_start(rows[:, h, :, :], buf[bass.ds((r * 2 + h) * stride, nt * 128), :]
                                     .rearrange("(t p) c -> p t c", p=128)).then_inc(rows_in[h], 16)
                        sp.dma_start(W[h], a[f"f{layer}_pack"][bass.ds(e, 1), :, :]
                                     .rearrange("e p c -> p (e c)")).then_inc(w_in[h], 16)

            @block.scalar
            def _(s):
                one_ahead(s, acted)
                def store(r, h):
                    s.wait_ge(biased, 1 + r * 2 * nt + (h + 1) * nt)
                    s.dma_start(ybuf[bass.ds((r * 2 + h) * stride, nt * 128), :].rearrange("(t p) c -> p t c", p=128),
                                y[:, h, :, :]).then_inc(y_out[h], 16)

                with s.Fori(0, chunks // 2) as r:
                    for h in range(2):
                        s.wait_ge(w_in[h], r * 16 + 16)
                        s.wait_ge(down, 1 + r * 2 * nt)
                        for f in range(KF):
                            s.wait_ge(up, 1 + r * 2 * KF + h * KF + f + 1)
                            s.activation(hT[h][:, f, :], pH[f % 2][:, 0:n], act, bias=b1(h, f)).then_inc(acted, 1)
                        if h == 1:
                            store(r, 0)
                    store(r, 1)
                for h in range(2):
                    s.wait_ge(y_out[h], chunks // 2 * 16)

            @block.vector
            def _(v):
                one_ahead(v, copied, biased)
                if n % 128:
                    for h in range(2):
                        v.memset(y[:, h, nt - 1, :], 0.0).then_inc(biased_init, 1)
                    v.wait_ge(biased_init, 2)

                def copy(r, h):
                    v.wait_ge(turned, r * 2 + h + 1)
                    v.wait_ge(up, 1 + r * 2 * KF)
                    for i in range(KD):
                        v.tensor_copy(xT[:, h, i, :], pT[i][:, 0:n]).then_inc(copied, 1)

                def bias(r, h):
                    v.wait_ge(w_in[h], r * 16 + 16)
                    v.wait_ge(y_free[h], r + 1)
                    for t in range(nt):
                        v.wait_ge(down, 1 + r * 2 * nt + h * nt + t + 1)
                        v.tensor_tensor(y[0:size[t], h, t, :], pY[t % 2][0:size[t], 0:D], b2(h, size[t]), ALU.add)\
                            .then_inc(biased, 1)

                with v.Fori(0, chunks // 2) as r:
                    copy(r, 0)
                    copy(r, 1)
                    bias(r, 0)
                    bias(r, 1)

            @block.tensor
            def _(pe):
                one_ahead(pe, down, up)
                def turn(r, h):
                    pe.wait_ge(rows_in[h], r * 16 + 16)
                    pe.wait_ge(copied, 1 + r * 2 * KD + h * KD)
                    for t in range(nt):
                        for i in range(KD):
                            last = nc.tensor.transpose(pT[i][:, t * 128:t * 128 + size[t]],
                                                       rows[0:size[t], h, t, i * 128:(i + 1) * 128],
                                                       k.ident[0:size[t], 0:size[t]])
                    last.then_inc(turned, 1)

                def first(r, h):
                    pe.wait_ge(w_in[h], r * 16 + 16)
                    pe.wait_ge(copied, 1 + r * 2 * KD + (h + 1) * KD)
                    for f in range(KF):
                        m = h * KF + f
                        pe.wait_ge(acted, 1 + r * 2 * KF + max(m - 1, 0))
                        for i in range(KD):
                            last = nc.tensor.matmul(pH[f % 2][:, 0:n], w1(h, i, f), xT[:, h, i, :],
                                                    start=i == 0, stop=i == KD - 1)
                        last.then_inc(up, 1)

                def second(r, h):
                    pe.wait_ge(acted, 1 + r * 2 * KF + (h + 1) * KF)
                    for t in range(nt):
                        m = h * nt + t
                        pe.wait_ge(biased, 1 + r * 2 * nt + max(m - 1, 0))
                        for f in range(KF):
                            last = nc.tensor.matmul(pY[t % 2][0:size[t], 0:D], hT[h][:, f, t * 128:t * 128 + size[t]],
                                                    w2(h, f), start=f == 0, stop=f == KF - 1)
                        last.then_inc(down, 1)

                with pe.Fori(0, chunks // 2) as r:
                    turn(r, 0)
                    first(r, 0)
                    turn(r, 1)
                    second(r, 0)
                    first(r, 1)
                    second(r, 1)


def combine(nc, a, k, layer):
    with ExitStack() as c:
        def sem(name):
            return k.sem(nc, f"{name}_c{layer}")

        got = k.got
        vec, stored = sem("vec"), sem("stored")
        held = [k.acc, k.xn]
        guard = [c.enter_context(nc.sbuf_tensor(f"guard{i}", [P, GT, D], F32)) for i in range(3)] if layer == 0 else None
        fin = c.enter_context(nc.sbuf_tensor("guard_ok", [P, GT, D], I32)) if layer == 0 else None

        with nc.Block() as block:
            @block.gpsimd
            def _(g):
                for t in range(T):
                    for i in range(layer + 1):
                        g.indirect_dma_start(
                            out=held[i][:, t, :], out_offset=None, in_=k.ybuf[layer],
                            in_offset=bass.IndirectOffsetOnAxis(ap=k.back[:, i, t:t + 1], axis=0)).then_inc(got[t], 16)

            @block.vector
            def _(v):
                ch = Chain(v, vec)
                if layer == 0:
                    for r in range(GR):
                        ts = slice(r * GT, (r + 1) * GT)
                        y = k.acc[:, ts, :]
                        for t in range(r * GT, (r + 1) * GT):
                            v.wait_ge(got[t], 16)
                            ch.mark(v.tensor_scalar(k.acc[:, t, :], k.acc[:, t, :], k.gate[:, 0, t:t + 1], None, ALU.mult))
                        ch.join()
                        ch.mark(v.tensor_scalar(fin[:, :, :], y, 0.0, 0.0, ALU.mult, ALU.is_equal))
                        ch.mark(v.tensor_scalar(guard[0][:, :, :], y, BIG, 1e4, ALU.is_gt, ALU.mult))
                        ch.link(v.tensor_scalar(guard[1][:, :, :], y, -BIG, -1e4, ALU.is_lt, ALU.mult))
                        ch.link(v.tensor_tensor(guard[2][:, :, :], guard[0][:, :, :], guard[1][:, :, :], ALU.add))
                        ch.link(v.copy_predicated(guard[2][:, :, :], fin[:, :, :], y))
                        ch.link(v.tensor_tensor(k.x[:, ts, :], k.x[:, ts, :], guard[2][:, :, :], ALU.add))
                        for t in range(r * GT, (r + 1) * GT):
                            ch.mark(v.bn_stats(k.stats[:, t, :], k.x[:, t, :]))
                else:
                    for t in range(T):
                        v.wait_ge(got[t], 16 + 32)
                        ch.link(v.scalar_tensor_tensor(k.x[:, t, :], k.acc[:, t, :], k.gate[:, 0, t:t + 1], k.x[:, t, :],
                                                       ALU.mult, ALU.add))
                        ch.mark(v.scalar_tensor_tensor(k.x[:, t, :], k.xn[:, t, :], k.gate[:, 1, t:t + 1], k.x[:, t, :],
                                                       ALU.mult, ALU.add))

            @block.sync
            def _(sp):
                if layer == 1:
                    for r in range(GR):
                        ts = slice(r * GT, (r + 1) * GT)
                        sp.wait_ge(vec, 2 * GT * (r + 1))
                        sp.dma_start(a["out"][:, ts, :], k.x[:, ts, :]).then_inc(stored, 16)
                    sp.wait_ge(stored, 16 * GR)


def project(nc, a, k):
    w = k.w
    with ExitStack() as c:
        def sb(name, shape):
            return c.enter_context(nc.sbuf_tensor(name, shape, F32))

        def sem(name):
            return k.sem(nc, name)

        def ps(name):
            return c.enter_context(nc.psum_tensor(name, [128, 512], F32))

        xs, xT = sb("p_rows", [P, GT, D]), sb("p_rowsT", [128, GT, KD, P])
        xj, junk = sb("xj", [P, GT, XJW]), sb("xj_wa2", [P, D])
        low, kk, vv = sb("k_low", [P, D]), sb("k_feat", [P, GT, D]), sb("v_rows", [P, GT, D + 1])
        xi = sb("xi_T", [128, KD, P])
        ba = sb("ba12", [128, 1])
        zero = sb("zero_row", [1, D + 1])
        pT, pJ, pK, pV, pI, pA = (ps(n) for n in ("p_pT", "p_xj", "p_k", "p_v", "p_xi", "p_a1"))
        pc = [ps(f"p_ctx{i}") for i in range(KD)]
        normed, turned, copied, kept = sem("p_normed"), sem("p_turned"), sem("p_copied"), sem("p_kept")
        init, vec, var_ready, root_ready = sem("p_init"), sem("p_vec"), sem("p_var"), sem("p_root")
        xj_mm, kv_mm, xi_mm, a1_mm, ctx_mm = sem("xj_mm"), sem("kv_mm"), sem("xi_mm"), sem("a1_mm"), sem("ctx_mm")
        xj_max, xi_max, xj_free = sem("xj_max"), sem("xi_max"), sem("xj_free")
        xj_act, a2_ready, v_ready, low_ready, exp_ready = sem("xj_act"), sem("a2_ready"), sem("v_ready"), sem("low_ready"), sem("exp_ready")
        k_ready, xi_ready, a1_ready, xj_out, sums = sem("k_ready"), sem("xi_ready"), sem("a1_ready"), sem("xj_out"), sem("p_sums")

        with nc.Block() as block:
            @block.gpsimd
            def _(g):
                g.memset(xj[:, :, D:XJW], 0.0).then_inc(init, 1)
                g.memset(vv[:, :, D], 1.0).then_inc(init, 1)
                g.memset(zero[:, :], 0.0).then_inc(init, 1)
                g.memset(k.ctx[:, :, :, :], 0.0).then_inc(init, 1)
                g.tensor_tensor(k.acc[:, :, :], k.x[:, :, :],
                                w["m1_bp"][0:P, :].unsqueeze(1).broadcast_to([P, T, D]), ALU.add).then_inc(sums, 1)
                g.wait_ge(sums, 1)
                g.wait_ge(kept, 1 + 2 * T)
                g.tensor_tensor(k.acc[:, :, :], k.acc[:, :, :], k.xn[:, :, :], ALU.add).then_inc(sums, 1)

            @block.sync
            def _(sp):
                one_ahead(sp, xj_free)
                with sp.Fori(0, GR) as r:
                    sp.wait_ge(a2_ready, r * GT + GT)
                    sp.dma_start(k.xj_d[bass.ds(r * GT * P, GT * P), :].rearrange("(t p) c -> p t c", p=P),
                                 xj[:, :, :]).then_inc(xj_out, 16)
                    sp.wait_ge(xj_out, r * 16 + 16)
                    sp.sem_inc(xj_free, 1)

            @block.scalar
            def _(s):
                one_ahead(s, kept, copied, v_ready, xi_ready, exp_ready)
                norm_root_scalar(s, k, var_ready, root_ready, 1)
                s.wait_ge(init, 4)
                with s.Fori(0, GR) as r:
                    for t in range(GT):
                        m = r * GT + t
                        s.wait_ge(turned, m + 1)
                        view = pT[:, 0:KD * P].rearrange("p (a b) -> p a b", a=KD)
                        s.activation(xT[:, t, :, :], view, ACT.Copy).then_inc(copied, 1)
                        s.activation(k.xnT[:, :, bass.ds(m * P, P)], view, ACT.Copy).then_inc(kept, 1)
                        s.activation(k.xn[:, bass.ds(m, 1), :], xs[:, t:t + 1, :], ACT.Copy).then_inc(kept, 1)
                        if t == 0:
                            s.wait_ge(xj_free, r + 1)
                        s.wait_ge(xj_mm, m + 1)
                        s.activation(xj[:, t, 0:D], pJ[0:P, 0:D], ACT.Copy, scale=0.2).then_inc(xj_act, 1)
                        s.wait_ge(kv_mm, m + 1)
                        if t == 0:
                            s.wait_ge(ctx_mm, 1 + r * GT)
                        s.activation(vv[:, t, 0:D], pV[0:P, 0:D], ACT.Copy).then_inc(v_ready, 1)
                        s.wait_ge(low_ready, m + 1)
                        s.activation(kk[:, t, :], low[:, :], ACT.Exp).then_inc(exp_ready, 1)
                        s.wait_ge(xi_mm, m + 1)
                        for i in range(KD):
                            s.activation(xi[:, i, :], pI[:, i * P:(i + 1) * P], ACT.Identity,
                                         bias=w["g1_b1"][:, i:i + 1]).then_inc(xi_ready, 1)

            @block.vector
            def _(v):
                one_ahead(v, xj_max, k_ready, a1_ready)
                ch = Chain(v, vec)
                norm_scale_vector(nc, v, ch, k, var_ready, root_ready, 1)
                ch.link(v.tensor_tensor(ba[:, :], w["g1_ba1"][:, :], w["g1_ba2"][:, :], ALU.add))
                v.wait_ge(init, 4)
                with v.Fori(0, GR) as r:
                    v.wait_ge(kept, 1 + r * 2 * GT)
                    for t in range(GT):
                        one = bass.ds(r * GT + t, 1)
                        v.tensor_scalar(xs[:, t:t + 1, :], k.x[:, one, :], k.mean[:, one], k.rstd[:, one],
                                        ALU.subtract, ALU.mult).then_inc(normed, 1)
                    for t in range(GT):
                        m = r * GT + t
                        v.wait_ge(kv_mm, m + 1)
                        v.wait_ge(exp_ready, 1 + m)
                        v.tensor_scalar(low[:, :], pK[0:P, 0:D], 0.0, None, ALU.min).then_inc(low_ready, 1)
                        v.wait_ge(xj_act, m + 1)
                        v.tensor_tensor(xj[:, t, 0:D], xj[:, t, 0:D], pJ[0:P, 0:D], ALU.max).then_inc(xj_max, 1)
                        v.wait_ge(xj_max, 1 + m + 1)
                        v.scalar_tensor_tensor(junk[:, :], xj[:, t, 0:D], 1.0, w["g1_wa2"][0:P, :], ALU.mult, ALU.mult,
                                               accum_out=xj[:, t, D:D + 1]).then_inc(a2_ready, 1)
                        v.wait_ge(a2_ready, m + 1)
                        v.wait_ge(exp_ready, 1 + m + 1)
                        v.scalar_tensor_tensor(kk[:, t, :], pK[0:P, 0:D], 0.0, kk[:, t, :], ALU.max, ALU.add)\
                            .then_inc(k_ready, 1)
                        v.wait_ge(xi_ready, 1 + (m + 1) * KD)
                        v.scalar_tensor_tensor(xi[:, :, :], xi[:, :, :], 0.2, xi[:, :, :], ALU.mult, ALU.max)\
                            .then_inc(xi_max, 1)
                        v.wait_ge(a1_mm, m + 1)
                        v.tensor_scalar(k.a1[:, bass.ds(m, 1), :], pA[:, 0:P].unsqueeze(1), ba[:, 0:1], None, ALU.add)\
                            .then_inc(a1_ready, 1)
                v.wait_ge(ctx_mm, 1 + T + 1)
                for h in range(HEADS):
                    i, q = h * HD // 128, h * HD % 128
                    v.tensor_copy(k.ctx[q:q + HD, i, 0, q:q + HD], pc[i][q:q + HD, h * HD:(h + 1) * HD])
                    v.tensor_copy(k.ctx[q:q + HD, i, 1, q:q + HD], pc[i][q:q + HD, D:D + 1].broadcast_to([HD, HD]))

            @block.tensor
            def _(pe):
                one_ahead(pe, ctx_mm)
                pe.wait_ge(init, 4)
                for i in range(KD):
                    nc.tensor.matmul(pc[i][:, 0:D + 1], k.ones[0:1, :], zero[:, :], start=True, stop=False)
                with pe.Fori(0, GR) as r:
                    for t in range(GT):
                        m = r * GT + t
                        pe.wait_ge(normed, m + 1)
                        pe.wait_ge(kept, 1 + m * 2)
                        pe.wait_ge(copied, 1 + m)
                        for i in range(KD):
                            last = nc.tensor.transpose(pT[:, i * P:(i + 1) * P], xs[:, t, i * 128:(i + 1) * 128],
                                                       k.ident[0:P, 0:P])
                        last.then_inc(turned, 1)
                        pe.wait_ge(copied, 1 + m + 1)
                        pe.wait_ge(xj_max, 1 + m)
                        for i in range(KD):
                            nc.tensor.matmul(pJ[0:P, 0:D], xT[:, t, i, :], w["g1_W2"][:, i, :], start=i == 0, stop=False)
                        nc.tensor.matmul(pJ[0:P, 0:D], k.ones[0:1, 0:P], w["g1_b2"][:, :], start=False, stop=True)\
                            .then_inc(xj_mm, 1)
                        pe.wait_ge(k_ready, 1 + m)
                        pe.wait_ge(v_ready, 1 + m)
                        for bank, at in ((pK, 0), (pV, D)):
                            for i in range(KD):
                                last = nc.tensor.matmul(bank[0:P, 0:D], xT[:, t, i, :], w["m1_WkvT"][:, i, at:at + D],
                                                        start=i == 0, stop=i == KD - 1)
                        last.then_inc(kv_mm, 1)
                        pe.wait_ge(xi_ready, 1 + m * KD)
                        for o in range(KD):
                            for i in range(KD):
                                last = nc.tensor.matmul(pI[:, o * P:(o + 1) * P], w["g1_W1"][:, i, o * 128:(o + 1) * 128],
                                                        xT[:, t, i, :], start=i == 0, stop=i == KD - 1)
                        last.then_inc(xi_mm, 1)
                        pe.wait_ge(xi_max, m + 1)
                        pe.wait_ge(a1_ready, 1 + m)
                        for o in range(KD):
                            last = nc.tensor.matmul(pA[:, 0:P], w["g1_wa1"][:, o, :], xi[:, o, :],
                                                    start=o == 0, stop=o == KD - 1)
                        last.then_inc(a1_mm, 1)
                        pe.wait_ge(k_ready, 1 + m + 1)
                        pe.wait_ge(v_ready, 1 + m + 1)
                        for i in range(KD):
                            last = nc.tensor.matmul(pc[i][:, 0:D + 1], kk[:, t, i * 128:(i + 1) * 128], vv[:, t, :],
                                                    start=False, stop=False)
                        last.then_inc(ctx_mm, 1)
                for i in range(KD):
                    last = nc.tensor.matmul(pc[i][:, 0:D + 1], k.ones[0:1, :], zero[:, :], start=False, stop=True)
                last.then_inc(ctx_mm, 1)


def attention(nc, a, k):
    w = k.w
    with ExitStack() as c:
        def sb(name, shape):
            return c.enter_context(nc.sbuf_tensor(name, shape, F32))

        def sem(name):
            return k.sem(nc, name)

        def ps(name):
            return c.enter_context(nc.psum_tensor(name, [128, 512], F32))

        low, q, inv, att = (sb(n, [128, 2, 256]) for n in ("q_low", "q_T", "a_inv", "a_T"))
        pQ, pA, pY = [ps(f"p_q{i}") for i in range(2)], [ps(f"p_att{i}") for i in range(2)], [ps(f"p_proj{i}") for i in range(2)]
        q_mm, low_ready, exp_ready, q_ready = sem("q_mm"), sem("q_low_ready"), sem("q_exp_ready"), sem("q_ready")
        att_mm, inv_ready, att_ready, y_mm, added = sem("att_mm"), sem("inv_ready"), sem("a_ready"), sem("y_mm"), sem("a_added")

        def tiles(n):
            return n

        blank = sem("a_blank")
        with nc.Block() as block:
            @block.gpsimd
            def _(g):
                for buf in (low, q, inv, att):
                    g.memset(buf[:, :, :], 0.0).then_inc(blank, 1)

            @block.scalar
            def _(s):
                with s.Fori(0, T) as m:
                    s.wait_ge(low_ready, m + 1)
                    s.activation(q[:, 0, 0:KD * P], low[:, 0, 0:KD * P], ACT.Exp).then_inc(exp_ready, 1)

            @block.vector
            def _(v):
                one_ahead(v, q_ready, att_ready, added)
                v.wait_ge(blank, 4)
                with v.Fori(0, T) as m:
                    v.wait_ge(q_mm, m + 1)
                    v.tensor_scalar(low[:, 0, 0:KD * P], pQ[0][:, 0:KD * P], 0.0, None, ALU.min).then_inc(low_ready, 1)
                    v.wait_ge(exp_ready, m + 1)
                    v.scalar_tensor_tensor(q[:, 0, 0:KD * P], pQ[0][:, 0:KD * P], 0.0, q[:, 0, 0:KD * P], ALU.max, ALU.add)\
                        .then_inc(q_ready, 1)
                    v.wait_ge(att_mm, m + 1)
                    v.tensor_scalar(inv[:, 0, 0:KD * P], pA[0][:, KD * P:2 * KD * P], 1e-6, None, ALU.max).then_inc(inv_ready, 1)
                    v.wait_ge(inv_ready, m * 2 + 1)
                    v.reciprocal(inv[:, 0, 0:KD * P], inv[:, 0, 0:KD * P]).then_inc(inv_ready, 1)
                    v.wait_ge(inv_ready, m * 2 + 2)
                    v.tensor_tensor(att[:, 0, 0:KD * P], pA[0][:, 0:KD * P], inv[:, 0, 0:KD * P], ALU.mult).then_inc(att_ready, 1)
                    v.wait_ge(y_mm, m + 1)
                    one = bass.ds(m, 1)
                    v.tensor_tensor(k.x[:, one, :], k.acc[:, one, :], pY[0][0:P, 0:D].unsqueeze(1), ALU.add)\
                        .then_inc(added, 1)
                    v.wait_ge(added, 1 + m + 1)
                    v.bn_stats(k.stats[:, one, :], k.x[:, one, :])

            @block.tensor
            def _(pe):
                with pe.Fori(0, T) as m:
                    pe.wait_ge(q_ready, 1 + m)
                    for o in range(KD):
                        for i in range(KD):
                            last = nc.tensor.matmul(pQ[0][:, o * P:(o + 1) * P], w["m1_WqT"][:, i, o * 128:(o + 1) * 128],
                                                    k.xnT[:, i, bass.ds(m * P, P)], start=i == 0, stop=i == KD - 1)
                    last.then_inc(q_mm, 1)
                    pe.wait_ge(q_ready, 1 + m + 1)
                    pe.wait_ge(att_ready, 1 + m)
                    for j in range(2):
                        for i in range(KD):
                            last = nc.tensor.matmul(pA[0][:, (j * KD + i) * P:(j * KD + i + 1) * P], k.ctx[:, i, j, :],
                                                    q[:, 0, i * P:(i + 1) * P], start=True, stop=True)
                    last.then_inc(att_mm, 1)
                    pe.wait_ge(att_ready, 1 + m + 1)
                    pe.wait_ge(added, 1 + m)
                    for i in range(KD):
                        last = nc.tensor.matmul(pY[0][0:P, 0:D], att[:, 0, i * P:(i + 1) * P], w["m1_WpT"][:, i, :],
                                                start=i == 0, stop=i == KD - 1)
                    last.then_inc(y_mm, 1)


def columns(w, blocks=None):
    return w.reshape(-1, 128, w.shape[-1]).transpose(1, 0, 2)


def kernel(**inputs):
    import numpy as np
    from concourse import bacc
    from concourse.bass_utils import run_bass_kernel_spmd

    x = {n: np.asarray(v) for n, v in inputs.items()}

    def spread(v):
        return np.broadcast_to(v.reshape(1, -1), (128, v.size))

    def pack(w1, b1, w2, b2):
        return np.concatenate([
            w1.reshape(X, KD, 128, FF).transpose(0, 2, 1, 3).reshape(X, 128, PK1),
            w2.reshape(X, KF, 128, D).transpose(0, 2, 1, 3).reshape(X, 128, PK2),
            b1.reshape(X, KF, 128).transpose(0, 2, 1),
            np.broadcast_to(b2.reshape(X, 1, D), (X, 128, D))], axis=2)

    arrays = {
        "x": x["x"].reshape(T, P, D).transpose(1, 0, 2),
        "src": x["src"].reshape(P, EC), "dst": x["dst"].reshape(P, EC),
        "edge_weight": x["edge_weight"].reshape(P, EC),
        "g0_W1": columns(x["L0_gnn_W1"]), "g0_b1": x["L0_gnn_b1"].reshape(-1, 128).T,
        "g0_W2": columns(x["L0_gnn_W2"]), "g0_b2": x["L0_gnn_b2"].reshape(1, D),
        "m0_Wq": columns(x["L0_mix_Wq"]), "m0_WkT": columns(x["L0_mix_Wk"].T), "m0_WvT": columns(x["L0_mix_Wv"].T),
        "m0_WfcT": columns(x["L0_mix_Wfc"].T), "m0_bqc": x["L0_mix_bq"].reshape(-1, 128).T,
        "m0_bk": x["L0_mix_bk"].reshape(1, D), "m0_bv": x["L0_mix_bv"].reshape(1, D),
        "m0_bfc": x["L0_mix_bfc"].reshape(1, D),
        "f0_gw": columns(x["L0_ffn_gate_w"]), "f0_gb": spread(np.tile(x["L0_ffn_gate_b"], T)).reshape(128, T, X),
        "f0_pack": pack(x["L0_ffn_w1"], x["L0_ffn_b1"], x["L0_ffn_w2"], x["L0_ffn_b2"]),
        "g1_W1": columns(x["L1_gnn_W1"]), "g1_b1": x["L1_gnn_b1"].reshape(-1, 128).T,
        "g1_W2": columns(x["L1_gnn_W2"]), "g1_b2": x["L1_gnn_b2"].reshape(1, D),
        "g1_wa1": np.broadcast_to(x["L1_gnn_wa1"].reshape(KD, 128, 1).transpose(1, 0, 2), (128, KD, 128)),
        "g1_ba1": spread(x["L1_gnn_ba1"]), "g1_wa2": spread(x["L1_gnn_wa2"]), "g1_ba2": spread(x["L1_gnn_ba2"]),
        "m1_WqT": columns(x["L1_mix_Wq"].T), "m1_WkvT": columns(x["L1_mix_Wkv"].T),
        "m1_WpT": columns(x["L1_mix_Wproj"].T), "m1_bp": spread(x["L1_mix_bproj"]),
        "f1_gw": columns(x["L1_ffn_Wg"]), "f1_gb": spread(np.tile(x["L1_ffn_bg"], T)).reshape(128, T, X),
        "f1_pack": pack(x["L1_ffn_W1"], x["L1_ffn_b1"], x["L1_ffn_W2"], x["L1_ffn_b2"]),
    }
    arrays = {n: np.ascontiguousarray(v) for n, v in arrays.items()}
    nc = bacc.Bacc("TRN2", target_bir_lowering=False, num_devices=1)
    a = {n: nc.dram_tensor(f"in_{n}", v.shape, mybir.dt.from_np(v.dtype), kind="ExternalInput").ap()
         for n, v in arrays.items()}
    a["out"] = nc.dram_tensor("out", (P, T, D), F32, kind="ExternalOutput").ap()
    build(nc, a)
    r = run_bass_kernel_spmd(nc, [{f"in_{n}": v for n, v in arrays.items()}], core_ids=[0])
    return np.ascontiguousarray(r.results[0]["out"].transpose(1, 0, 2)).reshape(N, D)
```

```python
from contextlib import ExitStack, contextmanager

import concourse.bass as bass
from concourse import mybir

F32 = mybir.dt.float32
F32R = mybir.dt.float32r
I32 = mybir.dt.int32
BF16 = mybir.dt.bfloat16
U16 = mybir.dt.uint16
ALU = mybir.AluOpType
ACT = mybir.ActivationFunctionType
AX = mybir.AxisListType

N, D, E = 3125, 256, 50000
P, T = 125, 25
KD = D // 128
EC = E // P
F0 = 512
FF, KF = 1024, 1024 // 128
X = 8
HD = 32
HEADS = D // HD
GT = 5
GR = T // GT
EB = 16
ET = -(-((E + T * 127) // 128) // EB) * EB
ETP = ET + EB
CAP0 = -(-5 * N // (4 * X))
CH = 256
ROW0 = -(-CAP0 // CH) * CH
CHUNKS0 = X * ROW0 // CH
NCH = (2 * N + X * (CH - 1)) // CH
PK = KD * FF
assert PK == KF * D
ROUND = 12582912.0
BIG = 3.4028234663852886e38
XJW = 264


class Chain:

    def __init__(self, eng, sem, base=0):
        self.eng, self.sem, self.n, self.base = eng, sem, 0, base

    def mark(self, ins):
        self.n += 1
        ins.then_inc(self.sem, 1)

    def join(self):
        self.eng.wait_ge(self.sem, self.base + self.n)

    def link(self, ins):
        self.mark(ins)
        self.join()


def one_ahead(eng, *sems):
    for s in sems:
        eng.sem_inc(s, 1)


def build(nc, a):
    persist = ExitStack()

    def sb(name, shape, dt=F32, ctx=persist):
        return ctx.enter_context(nc.sbuf_tensor(name, shape, dt))

    with persist:
        k = Shared(nc, sb, a)
        k.landed = [persist.enter_context(nc.semaphore(f"landed{s}")) for s in range(EB)]
        k.got = [persist.enter_context(nc.semaphore(f"got{t}")) for t in range(T)]
        with k.node_rows(nc, 0):
            prepare(nc, a, k)
            aggregate(nc, a, k, 0)
            gin_and_attention(nc, a, k)
            route(nc, a, k, 0)
        experts(nc, a, k, 0)
        combine(nc, a, k, 0)
        k.recycle(nc)
        with k.node_rows(nc, 1):
            project(nc, a, k)
            aggregate(nc, a, k, 1)
            route(nc, a, k, 1)
        experts(nc, a, k, 1)
        combine(nc, a, k, 1)


class Shared:

    def sem(self, nc, name):
        self.sems.append(nc.alloc_semaphore(name))
        return self.sems[-1]

    def recycle(self, nc):
        nc.clear_and_free_semaphores(self.sems)
        nc.all_engine_barrier()
        self.sems = []

    @contextmanager
    def node_rows(self, nc, layer):
        with ExitStack() as c:
            def sb(name, shape):
                return c.enter_context(nc.sbuf_tensor(f"{name}{layer}", shape, F32))

            self.xn = sb("x_normed", [P, T, D])
            if layer == 0:
                for name in WEIGHTS:
                    if name[:3] in ("g0_", "m0_"):
                        self.w[name] = sb("w_" + name, WEIGHTS[name])
                self.acc = sb("node_sums", [P, T, D])
            else:
                self.xnT = sb("x_normed_T", [128, KD, N + P])
                self.a1 = sb("a1_rows", [128, T, P])
            yield

    def __init__(self, nc, sb, a):
        self.sems = []
        self.x_all = sb("x_res", [P, T + 1, D])
        self.x = self.x_all[:, 0:T, :]
        self.edges = sb("sorted_edges", [128, ETP, 4])
        self.tile_bin = sb("tile_bin", [1, ETP], I32)
        self.ident = sb("ident", [128, 128])
        self.tri = sb("tri_strict", [128, 128])
        self.tri1 = sb("tri_incl", [128, 128])
        self.ones = sb("ones", [128, 128])
        self.iota = sb("iota_row", [128, 128])
        self.stats = sb("ln_stats", [P, T, 6])
        self.mean = sb("ln_mean", [P, T])
        self.rstd = sb("ln_rstd", [P, T])
        self.lnt = sb("ln_tmp", [P, 4, T])
        self.slots = sb("slots", [P, 2, T], I32)
        self.back = sb("slots_back", [P, 2, T], I32)
        self.gate = sb("gates", [P, 2, T])
        self.chunk_x = sb("chunk_expert", [1, NCH + 2], I32)
        self.w = {}
        for name, shape in WEIGHTS.items():
            if name[:3] not in ("g0_", "m0_"):
                self.w[name] = sb("w_" + name, shape)
        self.R = sb("mix0_R", [128, KD, D])
        self.r0 = sb("mix0_r0", [1, D])
        self.ctx = sb("mix1_ctx", [128, KD, 2, 128])
        self.edges_d = nc.dram_tensor("edges_d", [128 * ETP, 4], F32).ap()
        self.xn_d = nc.dram_tensor("xn_d", [N, D], F32).ap()
        self.xj_d = nc.dram_tensor("xj_d", [N, XJW], F32).ap()
        self.buf = [nc.dram_tensor("rows0_d", [X * ROW0 + CH + N, D], F32).ap(),
                    nc.dram_tensor("rows1_d", [NCH * CH + CH, D], F32).ap()]
        self.ybuf = [nc.dram_tensor("y0_d", [X * ROW0, D], F32).ap(),
                     nc.dram_tensor("y1_d", [NCH * CH, D], F32).ap()]


WEIGHTS = {
    "g0_W1": [128, KD, F0], "g0_b1": [128, F0 // 128], "g0_W2": [128, F0 // 128, D], "g0_b2": [1, D],
    "m0_Wq": [128, KD, D], "m0_WkT": [128, KD, D], "m0_WvT": [128, KD, D], "m0_WfcT": [128, KD, D],
    "m0_bqc": [128, KD], "m0_bk": [1, D], "m0_bv": [1, D], "m0_bfc": [1, D],
    "f0_gw": [128, KD, X], "f0_gb": [128, T, X],
    "g1_W1": [128, KD, D], "g1_b1": [128, KD], "g1_W2": [128, KD, D], "g1_b2": [1, D],
    "g1_wa1": [128, KD, 128], "g1_ba1": [128, 1], "g1_wa2": [128, D], "g1_ba2": [128, 1],
    "m1_WqT": [128, KD, D], "m1_WkvT": [128, KD, 2 * D], "m1_WpT": [128, KD, D], "m1_bp": [128, D],
    "f1_gw": [128, KD, X], "f1_gb": [128, T, X],
}


def norm_scale_vector(nc, v, ch, k, var_ready, root_ready, n):
    st, t = k.stats, k.lnt
    even, odd = st[:, :, 1], st[:, :, 4]
    ch.mark(v.tensor_tensor(k.mean[:, :], even, odd, ALU.add))
    ch.mark(v.tensor_tensor(t[:, 0, :], even, odd, ALU.subtract))
    ch.link(v.tensor_tensor(t[:, 1, :], st[:, :, 2], st[:, :, 5], ALU.add))
    ch.mark(v.tensor_scalar(k.mean[:, :], k.mean[:, :], 0.5, None, ALU.mult))
    ch.mark(v.tensor_tensor(t[:, 0, :], t[:, 0, :], t[:, 0, :], ALU.mult))
    ch.link(v.tensor_scalar(t[:, 1, :], t[:, 1, :], 1.0 / D, 1e-5, ALU.mult, ALU.add))
    v.scalar_tensor_tensor(t[:, 1, :], t[:, 0, :], 0.25, t[:, 1, :], ALU.mult, ALU.add).then_inc(var_ready, 1)
    v.wait_ge(root_ready, n)
    ch.link(v.reciprocal(k.rstd[:, :], t[:, 2, :]))
    ch.link(v.tensor_tensor(t[:, 0, :], k.rstd[:, :], k.rstd[:, :], ALU.mult))
    ch.link(v.tensor_tensor(t[:, 0, :], t[:, 0, :], t[:, 1, :], ALU.mult))
    ch.link(v.tensor_scalar(t[:, 0, :], t[:, 0, :], -0.5, 1.5, ALU.mult, ALU.add))
    ch.link(v.tensor_tensor(k.rstd[:, :], k.rstd[:, :], t[:, 0, :], ALU.mult))


def norm_root_scalar(s, k, var_ready, root_ready, n):
    s.wait_ge(var_ready, n)
    s.activation(k.lnt[:, 2, :], k.lnt[:, 1, :], ACT.Sqrt).then_inc(root_ready, 1)


def prepare(nc, a, k):
    with ExitStack() as c:
        def sb(name, shape, dt=F32):
            return c.enter_context(nc.sbuf_tensor(name, shape, dt))

        def sem(name):
            return k.sem(nc, name)

        src_i, dst_i = sb("src_i", [P, EC], I32), sb("dst_i", [P, EC], I32)
        w_e = sb("w_e", [P, EC])
        rec = sb("edge_rec", [P, EC, 4])
        src_f, bin_f = sb("src_f", [P, EC]), sb("bin_f", [P, EC])
        mask = sb("bin_mask", [P, T, EC], BF16)
        run = k.acc[:, :, :].rearrange("p t c -> p (t c)").bitcast(U16)[:, 0:T * EC]\
            .rearrange("p (t e) -> p t e", e=EC)
        pos, tmp = sb("edge_pos", [P, EC]), sb("edge_tmp", [P, EC])
        pos_i, low_i = sb("edge_pos_i", [P, EC], I32), sb("edge_low_i", [P, EC], I32)
        cnt, off = sb("bin_cnt", [P, T]), sb("bin_off", [128, T])
        tot_i, tiles, tiles_to = sb("bin_tot_i", [128, T], I32), sb("bin_tiles", [128, T]), sb("bin_tiles_to", [128, T])
        tix, tb = sb("tile_ix", [1, ETP]), sb("tile_b", [1, ETP])
        iota_i, tix_i = sb("iota_i", [128, 128], I32), sb("tix_i", [1, ETP], I32)
        zero = sb("zero_rows", [128, 8 * D])
        idx_st = sb("scatter_idx", [P, 2, 8], I32)
        rec_st = sb("scatter_rec", [P, 2, 8, 4])
        G, scol, srow = sb("gram", [128, KD, D]), sb("xn_sum_col", [128, KD]), sb("xn_sum_row", [1, D])
        U, Ul, KV, M2 = sb("mix_U", [128, KD, D]), sb("mix_Ul", [1, D]), sb("mix_KV", [128, KD, D]), sb("mix_M2", [128, KD, D])
        nconst = sb("n_const", [1, 1])
        pc = c.enter_context(nc.psum_tensor("p_counts", [128, 512], F32))
        pg = [c.enter_context(nc.psum_tensor(f"p_gram{i}", [128, 512], F32)) for i in range(KD)]
        pu = [c.enter_context(nc.psum_tensor(f"p_mix{i}", [128, 512], F32)) for i in range(KD)]
        pcol = c.enter_context(nc.psum_tensor("p_sumcol", [128, 512], F32))
        psr = c.enter_context(nc.psum_tensor("p_sumrow", [128, 512], F32))

        x_in, edges_in, w_in = sem("x_in"), sem("edges_in"), sem("w_in")
        consts, iotas = sem("consts"), sem("iotas")
        prefilled, zeroed = sem("prefilled"), sem("zeroed")
        vec, cnt_ready, prefix = sem("vec"), sem("cnt_ready"), sem("prefix")
        idx_ready, begun = sem("idx_ready"), sem("scatter_begun")
        staged = [sem(f"staged{i}") for i in range(2)]
        scattered = [sem(f"scattered{i}") for i in range(2)]
        stage_free = [sem(f"stage_free{i}") for i in range(2)]
        reload, var_ready, root_ready = sem("reload"), sem("var_ready"), sem("root_ready")
        normed, xn_out = sem("normed"), sem("xn_out")
        gram_done, mixed, mix_copied = sem("gram_done"), sem("mixed"), sem("mix_copied")
        lnc = sem("ln_chain")

        with nc.Block() as block:
            @block.sync
            def _(sp):
                sp.dma_start(src_i[:, :], a["src"]).then_inc(edges_in, 16)
                sp.dma_start(dst_i[:, :], a["dst"]).then_inc(edges_in, 16)
                sp.dma_start(w_e[:, :], a["edge_weight"]).then_inc(edges_in, 16)
                sp.dma_start(k.x[:, :, :], a["x"]).then_inc(x_in, 16)
                sp.wait_ge(consts, 1)
                sp.dma_start(k.edges_d.rearrange("(p t) c -> p (t c)", p=128),
                             k.edges[:, :, :].rearrange("p t c -> p (t c)")).then_inc(prefilled, 16)
                fills = 0
                for buf, rows in ((k.buf[0], X * ROW0 + CH), (k.buf[1], NCH * CH + CH)):
                    for r in range(0, rows, 1024):
                        m = min(1024, rows - r)
                        sp.dma_start(buf[r:r + m, :].rearrange("(p t) c -> p (t c)", p=128),
                                     zero[:, 0:m // 128 * D]).then_inc(zeroed, 16)
                        fills += 1
                sp.wait_ge(normed, T)
                sp.dma_start(k.xn_d.rearrange("(t p) c -> p t c", p=P), k.xn[:, :, :]).then_inc(xn_out, 16)
                one_ahead(sp, *stage_free)
                with sp.Fori(0, EC // 16) as r:
                    for h in range(2):
                        sp.wait_ge(scattered[h], r * 128 + 128)
                        sp.sem_inc(stage_free[h], 1)
                sp.dma_start(k.edges[:, :, :].rearrange("p t c -> p (t c)"),
                             k.edges_d.rearrange("(p t) c -> p (t c)", p=128)).then_inc(reload, 16)
                sp.wait_ge(reload, 16)
                sp.wait_ge(xn_out, 16)
                sp.wait_ge(zeroed, 16 * fills)

            @block.gpsimd
            def _(g):
                ch = Chain(g, iotas)
                ch.mark(g.memset(k.edges[:, :, :], 0.0))
                ch.mark(g.memset(zero[:, :], 0.0))
                ch.link(g.memset(k.ones[:, :], 1.0))
                ch.link(g.memset(k.edges[:, :, 1], -1.0))
                ch.mark(g.iota(iota_i[:, :], pattern=[[1, 128]], base=0, channel_multiplier=0))
                ch.mark(g.iota(tix_i[:, :], pattern=[[1, ETP]], base=0, channel_multiplier=0))
                ch.mark(g.affine_select(out=k.ident[:, :], in_=k.ones[:, :], compare_op=ALU.is_equal, fill=0.0,
                                        base=0, pattern=[[-1, 128]], channel_multiplier=1))
                ch.mark(g.affine_select(out=k.tri[:, :], in_=k.ones[:, :], compare_op=ALU.is_gt, fill=0.0,
                                        base=0, pattern=[[1, 128]], channel_multiplier=-1))
                ch.link(g.affine_select(out=k.tri1[:, :], in_=k.ones[:, :], compare_op=ALU.is_ge, fill=0.0,
                                        base=0, pattern=[[1, 128]], channel_multiplier=-1))
                ch.mark(g.tensor_copy(k.iota[:, :], iota_i[:, :]))
                ch.link(g.tensor_copy(tix[:, :], tix_i[:, :]))
                g.memset(nconst[:, :], float(N)).then_inc(consts, 1)
                g.wait_ge(prefilled, 16)
                with g.Fori(0, EC // 16) as r:
                    for h in range(2):
                        g.wait_ge(staged[h], r * 2 + 2)
                        g.sem_inc(begun, 1)
                        for j in range(8):
                            g.indirect_dma_start(
                                out=k.edges_d,
                                out_offset=bass.IndirectOffsetOnAxis(ap=idx_st[:, h, j:j + 1], axis=0),
                                in_=rec_st[:, h, j, :], in_offset=None).then_inc(scattered[h], 16)

            @block.scalar
            def _(s):
                for name in WEIGHTS:
                    ap = k.w[name]
                    s.dma_start(ap[tuple(slice(None) for _ in ap.shape)], a[name]).then_inc(w_in, 16)
                norm_root_scalar(s, k, var_ready, root_ready, 1)
                s.wait_ge(idx_ready, 1)
                with s.Fori(0, EC // 16) as r:
                    for h in range(2):
                        s.wait_ge(stage_free[h], r + 1)
                        col = bass.ds(r * 16 + h * 8, 8)
                        s.activation(idx_st[:, h, :], pos[:, col], ACT.Copy).then_inc(staged[h], 1)
                        s.activation(rec_st[:, h, :, :], rec[:, col, :], ACT.Copy).then_inc(staged[h], 1)

            @block.vector
            def _(v):
                ch = Chain(v, vec)
                ln = Chain(v, lnc)
                v.wait_ge(edges_in, 48)
                ch.mark(v.tensor_copy(src_f[:, :], src_i[:, :]))
                ch.mark(v.tensor_copy(rec[:, :, 0], dst_i[:, :]))
                ch.mark(v.tensor_copy(rec[:, :, 2], w_e[:, :]))
                ch.mark(v.memset(rec[:, :, 3], 0.0))
                ch.join()
                ch.link(v.tensor_scalar(bin_f[:, :], src_f[:, :], 1.0 / P, 0.5 / P - 0.5, ALU.mult, ALU.add))
                ch.link(v.tensor_scalar(bin_f[:, :], bin_f[:, :], ROUND, ROUND, ALU.add, ALU.subtract))
                ch.mark(v.scalar_tensor_tensor(rec[:, :, 1], bin_f[:, :], -float(P), src_f[:, :], ALU.mult, ALU.add))
                for b in range(T):
                    ch.mark(v.tensor_scalar(mask[:, b, :], bin_f[:, :], float(b), None, ALU.is_equal))
                ch.join()
                for b in range(T):
                    ch.mark(v.tensor_tensor_scan(run[:, b, :], mask[:, b, :], mask[:, b, :], 0.0, ALU.add, ALU.max))
                ch.join()
                v.tensor_copy(cnt[:, :], run[:, :, EC - 1]).then_inc(cnt_ready, 1)
                v.wait_ge(prefix, 2)
                ch.link(v.tensor_scalar(tot_i[:, :], pc[:, 32:32 + T], 127.0, None, ALU.add))
                ch.link(v.tensor_scalar(tot_i[:, :], tot_i[:, :], 7, None, ALU.logical_shift_right))
                ch.link(v.tensor_copy(tiles[:, :], tot_i[:, :]))
                v.wait_ge(iotas, 11)
                ch.link(v.tensor_tensor_scan(tiles_to[:, :], k.ones[:, 0:T], tiles[:, :], 0.0, ALU.mult, ALU.add))
                ch.link(v.tensor_tensor(off[:, :], tiles_to[:, :], tiles[:, :], ALU.subtract))
                ch.link(v.tensor_scalar(off[:, :], off[:, :], 128.0, -1.0, ALU.mult, ALU.add))
                ch.link(v.tensor_tensor(off[0:P, :], off[0:P, :], pc[0:P, 0:T], ALU.add))
                for b in range(T):
                    ch.link(v.scalar_tensor_tensor(run[:, b, :], run[:, b, :], off[0:P, b:b + 1], mask[:, b, :],
                                                   ALU.add, ALU.mult))
                    if b == 0:
                        ch.link(v.tensor_copy(tmp[:, :], run[:, b, :]))
                    else:
                        ch.link(v.tensor_tensor(tmp[:, :], tmp[:, :], run[:, b, :], ALU.add))
                ch.link(v.tensor_copy(pos_i[:, :], tmp[:, :]))
                ch.mark(v.tensor_scalar(low_i[:, :], pos_i[:, :], 127, None, ALU.bitwise_and))
                ch.link(v.tensor_scalar(pos_i[:, :], pos_i[:, :], 7, None, ALU.logical_shift_right))
                ch.mark(v.tensor_copy(tmp[:, :], low_i[:, :]))
                ch.link(v.tensor_copy(pos[:, :], pos_i[:, :]))
                v.scalar_tensor_tensor(pos[:, :], tmp[:, :], float(ETP), pos[:, :], ALU.mult, ALU.add)\
                    .then_inc(idx_ready, 1)
                v.wait_ge(x_in, 16)
                for t in range(T):
                    ln.mark(v.bn_stats(k.stats[:, t, :], k.x[:, t, :]))
                ln.join()
                norm_scale_vector(nc, v, ln, k, var_ready, root_ready, 1)
                for t in range(T):
                    v.tensor_scalar(k.xn[:, t, :], k.x[:, t, :], k.mean[:, t:t + 1], k.rstd[:, t:t + 1],
                                    ALU.subtract, ALU.mult).then_inc(normed, 1)
                v.wait_ge(normed, T)
                ln.mark(v.tensor_copy(k.acc[:, :, :], k.xn[:, :, :]))
                ln.link(v.tensor_scalar(tb[:, :], tix[:, :], tiles_to[0:1, 0:1], None, ALU.is_ge))
                for b in range(1, T - 1):
                    ln.link(v.scalar_tensor_tensor(tb[:, :], tix[:, :], tiles_to[0:1, b:b + 1], tb[:, :],
                                                   ALU.is_ge, ALU.add))
                ln.mark(v.tensor_copy(k.tile_bin[:, :], tb[:, :]))
                ln.mark(v.memset(KV[:, :, :], 0.0))
                v.wait_ge(gram_done, 1)
                for i in range(KD):
                    v.tensor_copy(G[:, i, :], pg[i][:, 0:D]).then_inc(mix_copied, 1)
                v.tensor_copy(scol[:, :], pcol[:, 0:KD]).then_inc(mix_copied, 1)
                v.tensor_copy(srow[:, :], psr[0:1, 0:D]).then_inc(mix_copied, 1)
                v.wait_ge(mixed, 1)
                for i in range(KD):
                    v.tensor_copy(U[:, i, :], pu[i][:, 0:D]).then_inc(mix_copied, 1)
                v.tensor_copy(Ul[:, :], psr[0:1, 0:D]).then_inc(mix_copied, 1)
                v.wait_ge(mixed, 2)
                ln.join()
                for h in range(HEADS):
                    i, q = h * HD // 128, h * HD % 128
                    v.tensor_scalar(KV[q:q + HD, i, h * HD:(h + 1) * HD], pu[i][q:q + HD, h * HD:(h + 1) * HD],
                                    1.0 / N, None, ALU.mult).then_inc(mix_copied, 1)
                v.wait_ge(mixed, 3)
                for i in range(KD):
                    v.tensor_copy(M2[:, i, :], pu[i][:, 0:D]).then_inc(mix_copied, 1)
                v.wait_ge(mixed, 4)
                for i in range(KD):
                    v.tensor_copy(k.R[:, i, :], pu[i][:, 0:D]).then_inc(mix_copied, 1)
                ln.link(v.tensor_tensor(k.r0[:, :], psr[0:1, 0:D], k.w["m0_bfc"][:, :], ALU.add))
                ln.link(v.tensor_tensor(k.r0[:, :], k.r0[:, :], k.w["g0_b2"][:, :], ALU.add))

            @block.tensor
            def _(pe):
                pe.wait_ge(cnt_ready, 1)
                pe.wait_ge(iotas, 11)
                nc.tensor.matmul(pc[0:P, 0:T], k.tri[0:P, 0:P], cnt[:, :], start=True, stop=True).then_inc(prefix, 1)
                nc.tensor.matmul(pc[:, 32:32 + T], k.ones[0:P, :], cnt[:, :], start=True, stop=True).then_inc(prefix, 1)
                for t in range(T):
                    pe.wait_ge(normed, t + 1)
                    for i in range(KD):
                        nc.tensor.matmul(pg[i][:, 0:D], k.xn[:, t, i * 128:(i + 1) * 128], k.xn[:, t, :],
                                         start=t == 0, stop=t == T - 1)
                    nc.tensor.matmul(psr[0:1, 0:D], k.ones[0:P, 0:1], k.xn[:, t, :], start=t == 0, stop=t == T - 1)
                for i in range(KD):
                    for t in range(T):
                        last = nc.tensor.matmul(pcol[:, i:i + 1], k.xn[:, t, i * 128:(i + 1) * 128],
                                                k.ones[0:P, 0:1], start=t == 0, stop=t == T - 1)
                last.then_inc(gram_done, 1)
                pe.wait_ge(w_in, 16 * len(WEIGHTS))
                pe.wait_ge(mix_copied, KD + 2)
                pe.wait_ge(consts, 1)
                w = k.w
                for i in range(KD):
                    for j in range(KD):
                        nc.tensor.matmul(pu[i][:, 0:D], G[:, j, i * 128:(i + 1) * 128], w["m0_WvT"][:, j, :],
                                         start=j == 0, stop=False)
                    nc.tensor.matmul(pu[i][:, 0:D], srow[:, i * 128:(i + 1) * 128], w["m0_bv"][:, :],
                                     start=False, stop=True)
                for j in range(KD):
                    nc.tensor.matmul(psr[0:1, 0:D], scol[:, j:j + 1], w["m0_WvT"][:, j, :], start=j == 0, stop=False)
                nc.tensor.matmul(psr[0:1, 0:D], nconst[:, :], w["m0_bv"][:, :], start=False, stop=True)\
                    .then_inc(mixed, 1)
                pe.wait_ge(mix_copied, 2 * (KD + 1) + 1)
                for i in range(KD):
                    for j in range(KD):
                        nc.tensor.matmul(pu[i][:, 0:D], U[:, j, i * 128:(i + 1) * 128], w["m0_WkT"][:, j, :],
                                         start=j == 0, stop=False)
                    last = nc.tensor.matmul(pu[i][:, 0:D], Ul[:, i * 128:(i + 1) * 128], w["m0_bk"][:, :],
                                            start=False, stop=True)
                last.then_inc(mixed, 1)
                n = 2 * (KD + 1) + 1 + HEADS
                pe.wait_ge(mix_copied, n)
                for i in range(KD):
                    for j in range(KD):
                        last = nc.tensor.matmul(pu[i][:, 0:D], KV[:, j, i * 128:(i + 1) * 128],
                                                w["m0_WfcT"][:, j, :], start=j == 0, stop=j == KD - 1)
                last.then_inc(mixed, 1)
                pe.wait_ge(mix_copied, n + KD)
                for i in range(KD):
                    for j in range(KD):
                        nc.tensor.matmul(pu[i][:, 0:D], w["m0_Wq"][:, j, i * 128:(i + 1) * 128], M2[:, j, :],
                                         start=j == 0, stop=j == KD - 1)
                for j in range(KD):
                    last = nc.tensor.matmul(psr[0:1, 0:D], w["m0_bqc"][:, j:j + 1], M2[:, j, :],
                                            start=j == 0, stop=j == KD - 1)
                last.then_inc(mixed, 1)


def bins_of(nc, k, engine, r, h):
    _, bins = nc.values_load_multi_w_load_instructions(
        k.tile_bin[0:1, bass.ds(r * EB + h * (EB // 2), EB // 2)], engines=(engine,), min_val=0, max_val=T - 1,
        skip_runtime_bounds_check_because="a count of at most T - 1 node tiles")
    return bins


def aggregate(nc, a, k, layer):
    width = (D, XJW)[layer]
    table = (k.xn_d, k.xj_d)[layer]
    sums = k.x_all if layer else k.acc
    H = EB // 2
    with ExitStack() as c:
        def sem(name):
            return k.sem(nc, f"{name}{layer}")

        rows = c.enter_context(nc.sbuf_tensor(f"edge_rows{layer}", [128, EB, width], F32))
        hot = c.enter_context(nc.sbuf_tensor(f"one_hot{layer}", [128, EB, P], F32))
        att = c.enter_context(nc.sbuf_tensor(f"att{layer}", [128, EB, P], F32)) if layer else None
        idx = c.enter_context(nc.sbuf_tensor(f"gather_idx{layer}", [128, 2, H], I32))
        part = [c.enter_context(nc.psum_tensor(f"p_part{layer}_{i}", [128, 512], F32)) for i in range(4)]
        staged = [sem(f"idx_staged{h}_") for h in range(2)]
        landed, past = k.landed, layer * (ET // EB) * 16
        begun = sem("gather_begun")
        att_ready, hot_ready, summed, added = sem("att_ready"), sem("hot_ready"), sem("summed"), sem("added")
        if layer:
            w = k.w
            low, q, inv, mix = (c.enter_context(nc.sbuf_tensor(n, [128, KD * P], F32))
                                for n in ("q_low", "q_T", "mix_inv", "mix_T"))
            pQ, pM, pY = (c.enter_context(nc.psum_tensor(n, [128, 512], F32)) for n in ("p_q", "p_mixed", "p_proj"))
            q_mm, q_low, q_exp, q_ready = sem("q_mm"), sem("q_low"), sem("q_exp"), sem("q_ready")
            mix_mm, inv_ready, mix_ready = sem("mix_mm"), sem("inv_ready"), sem("mix_ready")
            y_mm, y_added = sem("y_mm"), sem("y_added")

        with nc.Block() as block:
            @block.gpsimd
            def _(g):
                with g.Fori(0, ET // EB) as r:
                    for s in range(EB):
                        if s % H == 0:
                            g.wait_ge(staged[s // H], r + 1)
                            g.sem_inc(begun, 1)
                        g.indirect_dma_start(
                            out=rows[:, s, :], out_offset=None, in_=table,
                            in_offset=bass.IndirectOffsetOnAxis(ap=idx[:, s // H, s % H:s % H + 1], axis=0))\
                            .then_inc(landed[s], 16)

            @block.scalar
            def _(sc):
                for h in range(2):
                    sc.activation(idx[:, h, :], k.edges[:, h * H:(h + 1) * H, 0], ACT.Copy).then_inc(staged[h], 1)
                with sc.Fori(0, ET // EB) as r:
                    for h in range(2):
                        if layer:
                            bins = bins_of(nc, k, mybir.EngineType.Activation, r, h)
                            for j in range(H):
                                s = h * H + j
                                sc.wait_ge(landed[s], past + r * 16 + 16)
                                sc.activation(att[:, s:s + 1, :], k.a1[:, bass.ds(bins[j], 1), :], ACT.Sigmoid,
                                              bias=rows[:, s, D:D + 1]).then_inc(att_ready, 1)
                                if s == H // 2:
                                    sc.wait_ge(q_low, r + 1)
                                    sc.activation(q[:, :], low[:, :], ACT.Exp).then_inc(q_exp, 1)
                        sc.wait_ge(summed, r * EB + (h + 1) * H)
                        sc.activation(idx[:, h, :], k.edges[:, bass.ds(r * EB + EB + h * H, H), 0], ACT.Copy)\
                            .then_inc(staged[h], 1)

            @block.vector
            def _(v):
                one_ahead(v, added)
                if layer:
                    one_ahead(v, q_ready, mix_ready, y_added)

                def mix_step(r, s):
                    if s == 1:
                        v.wait_ge(q_mm, r + 1)
                        v.tensor_scalar(low[:, :], pQ[:, 0:KD * P], 0.0, None, ALU.min).then_inc(q_low, 1)
                    if s == H + 4:
                        v.wait_ge(q_exp, r + 1)
                        v.scalar_tensor_tensor(q[:, :], pQ[:, 0:KD * P], 0.0, q[:, :], ALU.max, ALU.add)\
                            .then_inc(q_ready, 1)
                    if s == 2 * H + 1:
                        v.wait_ge(mix_mm, r + 1)
                        v.tensor_scalar(inv[:, :], pM[:, KD * P:2 * KD * P], 1e-6, None, ALU.max).then_inc(inv_ready, 1)
                        v.wait_ge(inv_ready, r * 2 + 1)
                        v.reciprocal(inv[:, :], inv[:, :]).then_inc(inv_ready, 1)
                        v.wait_ge(inv_ready, r * 2 + 2)
                        v.tensor_tensor(mix[:, :], pM[:, 0:KD * P], inv[:, :], ALU.mult).then_inc(mix_ready, 1)
                    if s == 3 * H - 1:
                        dst = sums[:, bass.ds(r, 1), :]
                        v.wait_ge(y_mm, r + 1)
                        v.wait_ge(added, 1 + r * EB + EB - 1)
                        v.tensor_tensor(dst, dst, pY[0:P, 0:D].unsqueeze(1), ALU.add).then_inc(y_added, 1)
                        v.wait_ge(y_added, 1 + r + 1)

                with v.Fori(0, ET // EB) as r:
                    for h in range(2):
                        bins = bins_of(nc, k, mybir.EngineType.DVE, r, h)
                        for j in range(H):
                            s = h * H + j
                            e = k.edges[:, bass.ds(r * EB + s, 1), :]
                            if layer:
                                if h == 0:
                                    mix_step(r, j)
                                v.wait_ge(att_ready, r * EB + s + 1)
                                v.scalar_tensor_tensor(hot[:, s, :], k.iota[:, 0:P], e[:, 0, 1:2], att[:, s, :],
                                                       ALU.is_equal, ALU.mult).then_inc(hot_ready, 1)
                            else:
                                v.tensor_scalar(hot[:, s, :], k.iota[:, 0:P], e[:, 0, 1:2], e[:, 0, 2:3],
                                                ALU.is_equal, ALU.mult).then_inc(hot_ready, 1)
                        for j in range(H):
                            s = h * H + j
                            if layer:
                                mix_step(r, H * (h + 1) + j)
                            dst = sums[:, bass.ds(bins[j], 1), :]
                            v.wait_ge(summed, r * EB + s + 1)
                            v.wait_ge(added, 1 + r * EB + s)
                            v.tensor_tensor(dst, dst, part[s % 4][0:P, 0:D].unsqueeze(1), ALU.add)\
                                .then_inc(added, 1)

            @block.tensor
            def _(pe):
                def mix_step(r, s):
                    if s == 0:
                        pe.wait_ge(q_ready, 1 + r)
                        for o in range(KD):
                            for i in range(KD):
                                last = nc.tensor.matmul(pQ[:, o * P:(o + 1) * P],
                                                        w["m1_WqT"][:, i, o * 128:(o + 1) * 128],
                                                        k.xnT[:, i, bass.ds(r * P, P)], start=i == 0, stop=i == KD - 1)
                        last.then_inc(q_mm, 1)
                    if s == H:
                        pe.wait_ge(q_ready, 1 + r + 1)
                        pe.wait_ge(mix_ready, 1 + r)
                        for j in range(2):
                            for i in range(KD):
                                last = nc.tensor.matmul(pM[:, (j * KD + i) * P:(j * KD + i + 1) * P],
                                                        k.ctx[:, i, j, :], q[:, i * P:(i + 1) * P],
                                                        start=True, stop=True)
                        last.then_inc(mix_mm, 1)
                    if s == EB - 3:
                        pe.wait_ge(mix_ready, 1 + r + 1)
                        pe.wait_ge(y_added, 1 + r)
                        for i in range(KD):
                            last = nc.tensor.matmul(pY[0:P, 0:D], mix[:, i * P:(i + 1) * P], w["m1_WpT"][:, i, :],
                                                    start=i == 0, stop=i == KD - 1)
                        last.then_inc(y_mm, 1)

                with pe.Fori(0, ET // EB) as r:
                    for s in range(EB):
                        if layer:
                            mix_step(r, s)
                        pe.wait_ge(landed[s], past + r * 16 + 16)
                        pe.wait_ge(hot_ready, r * EB + s + 1)
                        pe.wait_ge(added, 1 + r * EB + max(s - 3, 0))
                        nc.tensor.matmul(part[s % 4][0:P, 0:D], hot[:, s, :], rows[:, s, 0:D],
                                         start=True, stop=True).then_inc(summed, 1)


def gin_and_attention(nc, a, k):
    KH = F0 // 128
    w = k.w
    with ExitStack() as c:
        def sb(name, shape):
            return c.enter_context(nc.sbuf_tensor(name, shape, F32))

        def sem(name):
            return k.sem(nc, name)

        def ps(name):
            return c.enter_context(nc.psum_tensor(name, [128, 512], F32))

        hs, xs = sb("gin_rows", [P, GT, D]), sb("mix_rows", [P, GT, D])
        xT, hT = sb("gin_T", [128, GT, 2 * KD, P]), sb("gin_hidden", [128, GT, KH, P])
        pT, pH, pO = [ps(f"p_gT{i}") for i in range(2)], [ps(f"p_gH{i}") for i in range(2)], [ps(f"p_gO{i}") for i in range(2)]
        rows_in, turned, copied = sem("g_rows_in"), sem("g_turned"), sem("g_copied")
        up, relued, down, added, stat = sem("g_up"), sem("g_relued"), sem("g_down"), sem("g_added"), sem("g_stat")

        with nc.Block() as block:
            @block.scalar
            def _(s):
                one_ahead(s, relued)
                with s.Fori(0, GR) as r:
                    s.wait_ge(down, 1 + r * GT)
                    s.activation(hs[:, :, :], k.acc[:, bass.ds(r * GT, GT), :], ACT.Copy).then_inc(rows_in, 1)
                    s.activation(xs[:, :, :], k.xn[:, bass.ds(r * GT, GT), :], ACT.Copy).then_inc(rows_in, 1)
                    for t in range(GT):
                        s.wait_ge(up, r * GT + t + 1)
                        for f in range(KH):
                            s.activation(hT[:, t, f, :], pH[t % 2][:, f * P:(f + 1) * P], ACT.Relu,
                                         bias=w["g0_b1"][:, f:f + 1]).then_inc(relued, 1)

            @block.vector
            def _(v):
                one_ahead(v, copied, added)
                with v.Fori(0, GR) as r:
                    for t in range(GT):
                        v.wait_ge(turned, r * GT + t + 1)
                        v.tensor_copy(xT[:, t, :, :], pT[t % 2][:, 0:2 * KD * P]
                                      .rearrange("p (a b) -> p a b", a=2 * KD)).then_inc(copied, 1)
                    for t in range(GT):
                        x = k.x[:, bass.ds(r * GT + t, 1), :]
                        v.wait_ge(down, 1 + r * GT + t + 1)
                        v.tensor_tensor(x, x, pO[t % 2][0:P, 0:D].unsqueeze(1), ALU.add).then_inc(added, 1)
                        v.wait_ge(added, 1 + r * GT + t + 1)
                        v.bn_stats(k.stats[:, bass.ds(r * GT + t, 1), :], x)

            @block.tensor
            def _(pe):
                one_ahead(pe, down)
                with pe.Fori(0, GR) as r:
                    pe.wait_ge(rows_in, r * 2 + 2)
                    for t in range(GT):
                        pe.wait_ge(copied, 1 + r * GT + max(t - 1, 0))
                        for q, rows in enumerate((hs, xs)):
                            for i in range(KD):
                                j = q * KD + i
                                last = nc.tensor.transpose(pT[t % 2][:, j * P:(j + 1) * P],
                                                           rows[:, t, i * 128:(i + 1) * 128], k.ident[0:P, 0:P])
                        last.then_inc(turned, 1)
                    for t in range(GT):
                        pe.wait_ge(copied, 1 + r * GT + t + 1)
                        pe.wait_ge(relued, 1 + r * GT * KH + max(t - 1, 0) * KH)
                        for f in range(KH):
                            for i in range(KD):
                                last = nc.tensor.matmul(pH[t % 2][:, f * P:(f + 1) * P],
                                                        w["g0_W1"][:, i, f * 128:(f + 1) * 128], xT[:, t, i, :],
                                                        start=i == 0, stop=i == KD - 1)
                        last.then_inc(up, 1)
                    for t in range(GT):
                        pe.wait_ge(relued, 1 + r * GT * KH + (t + 1) * KH)
                        pe.wait_ge(added, 1 + r * GT + max(t - 1, 0))
                        out = pO[t % 2][0:P, 0:D]
                        for i in range(KD):
                            nc.tensor.matmul(out, xT[:, t, KD + i, :], k.R[:, i, :], start=i == 0, stop=False)
                        nc.tensor.matmul(out, k.ones[0:1, 0:P], k.r0[:, :], start=False, stop=False)
                        for f in range(KH):
                            last = nc.tensor.matmul(out, hT[:, t, f, :], w["g0_W2"][:, f, :],
                                                    start=False, stop=f == KH - 1)
                        last.then_inc(down, 1)


def first_max(v, ch, lg, mx, rev, oh, at):
    ch.link(v.tensor_reduce(mx, lg, AX.X, ALU.max))
    ch.link(v.tensor_tensor(oh, lg, mx.unsqueeze(2).broadcast_to([P, T, X]), ALU.is_equal))
    ch.link(v.tensor_tensor(oh, oh, rev, ALU.mult))
    ch.link(v.tensor_reduce(at, oh, AX.X, ALU.max))
    ch.link(v.tensor_tensor(oh, rev, at.unsqueeze(2).broadcast_to([P, T, X]), ALU.is_equal))


def route(nc, a, k, layer):
    w = k.w
    picks = layer + 1
    gw, gb = w[f"f{layer}_gw"], w[f"f{layer}_gb"]
    with ExitStack() as c:
        def sb(name, shape, dt=F32):
            return c.enter_context(nc.sbuf_tensor(f"{name}_r{layer}", shape, dt))

        def sem(name):
            return k.sem(nc, f"{name}_r{layer}")

        def ps(name):
            return c.enter_context(nc.psum_tensor(f"{name}_r{layer}", [128, 512], F32))

        xs, xT = sb("rows", [P, GT, D]), sb("rowsT", [128, GT, KD, P])
        lg, lg2, rev, tmp = sb("logits", [P, T, X]), sb("logits2", [P, T, X]), sb("rev", [P, T, X]), sb("tmp", [P, T, X])
        oh = [sb(f"onehot{i}", [P, T, X]) for i in range(2)]
        both, tot, upto = sb("both", [P, T, X]), sb("tot", [P, T, X]), sb("upto", [P, T, X])
        mx = [sb(f"mx{i}", [P, T]) for i in range(2)]
        at = [sb(f"at{i}", [P, T]) for i in range(2)]
        e2, inv, pos, keep, node = sb("e2", [P, T]), sb("inv", [P, T]), sb("pos", [P, T]), sb("keep", [P, T]), sb("node", [P, T])
        ch_i, chn, cto = sb("chunks_i", [P, X], I32), sb("chunks", [P, X]), sb("chunks_to", [P, X])
        cx, cix, cix_i = sb("cx", [1, NCH + 2]), sb("cix", [1, NCH + 2]), sb("cix_i", [1, NCH + 2], I32)
        rev_i, node_i = sb("rev_i", [P, T, X], I32), sb("node_i", [P, T], I32)
        pT, pL, pC, pN = [ps(f"p_T{i}") for i in range(2)], ps("p_L"), ps("p_cum"), ps("p_tot")
        normed, turned, copied, kept_x, logits = sem("normed"), sem("turned"), sem("copied"), sem("kept_x"), sem("logits")
        vec, var_ready, root_ready, iotas = sem("vec"), sem("var"), sem("root"), sem("iotas")
        e_in, e_out, hot_ready, cum_ready = sem("e_in"), sem("e_out"), sem("hot_ready"), sem("cum_ready")
        slots_ready, scattered = sem("slots_ready"), sem("scattered")

        with nc.Block() as block:
            @block.gpsimd
            def _(g):
                g.iota(rev_i[:, :, :], pattern=[[0, T], [-1, X]], base=X, channel_multiplier=0).then_inc(iotas, 1)
                g.iota(node_i[:, :], pattern=[[P, T]], base=X * ROW0 + CH, channel_multiplier=1).then_inc(iotas, 1)
                g.iota(cix_i[:, :], pattern=[[1, NCH + 2]], base=0, channel_multiplier=0).then_inc(iotas, 1)
                g.wait_ge(slots_ready, 1)
                for t in range(T):
                    for i in range(picks):
                        g.indirect_dma_start(
                            out=k.buf[layer], out_offset=bass.IndirectOffsetOnAxis(ap=k.slots[:, i, t:t + 1], axis=0),
                            in_=k.xn[:, t, :], in_offset=None).then_inc(scattered, 16)
                g.wait_ge(scattered, 16 * T * picks)

            @block.scalar
            def _(s):
                one_ahead(s, kept_x, copied)
                norm_root_scalar(s, k, var_ready, root_ready, 1)
                with s.Fori(0, GR) as r:
                    s.wait_ge(logits, 1 + r * GT)
                    for t in range(GT):
                        s.wait_ge(turned, r * GT + t + 1)
                        s.activation(xT[:, t, :, :], pT[t % 2][:, 0:KD * P].rearrange("p (a b) -> p a b", a=KD),
                                     ACT.Copy).then_inc(copied, 1)
                        s.activation(k.xn[:, bass.ds(r * GT + t, 1), :], xs[:, t:t + 1, :], ACT.Copy)\
                            .then_inc(kept_x, 1)
                s.wait_ge(e_in, 1)
                if layer == 0:
                    s.activation(tmp[:, :, :], tmp[:, :, :], ACT.Exp).then_inc(e_out, 1)
                else:
                    s.activation(e2[:, :], e2[:, :], ACT.Exp).then_inc(e_out, 1)

            @block.tensor
            def _(pe):
                one_ahead(pe, logits)
                with pe.Fori(0, GR) as r:
                    for t in range(GT):
                        pe.wait_ge(normed, r * GT + t + 1)
                        pe.wait_ge(copied, 1 + r * GT + max(t - 1, 0))
                        for i in range(KD):
                            last = nc.tensor.transpose(pT[t % 2][:, i * P:(i + 1) * P],
                                                       xs[:, t, i * 128:(i + 1) * 128], k.ident[0:P, 0:P])
                        last.then_inc(turned, 1)
                    for t in range(GT):
                        pe.wait_ge(copied, 1 + r * GT + t + 1)
                        for i in range(KD):
                            last = nc.tensor.matmul(pL[0:P, bass.ds((r * GT + t) * X, X)], xT[:, t, i, :], gw[:, i, :],
                                                    start=i == 0, stop=i == KD - 1)
                        last.then_inc(logits, 1)
                pe.wait_ge(hot_ready, 1)
                hot = both[:, :, :].rearrange("p t x -> p (t x)")
                nc.tensor.matmul(pC[0:P, 0:T * X], k.tri1[0:P, 0:P], hot, start=True, stop=True)
                nc.tensor.matmul(pN[0:P, 0:T * X], k.ones[0:P, 0:P], hot, start=True, stop=True).then_inc(cum_ready, 1)

            @block.vector
            def _(v):
                ch = Chain(v, vec)
                if layer:
                    for t in range(T):
                        ch.mark(v.bn_stats(k.stats[:, t, :], k.x[:, t, :]))
                    ch.join()
                norm_scale_vector(nc, v, ch, k, var_ready, root_ready, 1)
                with v.Fori(0, GR) as r:
                    for t in range(GT):
                        if t == 0:
                            v.wait_ge(kept_x, 1 + r * GT)
                        one = bass.ds(r * GT + t, 1)
                        v.tensor_scalar(xs[:, t:t + 1, :], k.x[:, one, :], k.mean[:, one], k.rstd[:, one],
                                        ALU.subtract, ALU.mult).then_inc(normed, 1)
                v.wait_ge(iotas, 3)
                ch.mark(v.tensor_copy(rev[:, :, :], rev_i[:, :, :]))
                ch.mark(v.tensor_copy(node[:, :], node_i[:, :]))
                ch.mark(v.tensor_copy(cix[:, :], cix_i[:, :]))
                v.wait_ge(logits, 1 + T)
                view = "p (t x) -> p t x"
                ch.link(v.tensor_tensor(lg[:, :, :], pL[0:P, 0:T * X].rearrange(view, x=X), gb[0:P, :, :], ALU.add))
                first_max(v, ch, lg[:, :, :], mx[0][:, :], rev[:, :, :], oh[0][:, :, :], at[0][:, :])
                if layer == 0:
                    v.tensor_tensor(tmp[:, :, :], lg[:, :, :], mx[0][:, :].unsqueeze(2).broadcast_to([P, T, X]),
                                    ALU.subtract).then_inc(e_in, 1)
                    v.tensor_copy(both[:, :, :], oh[0][:, :, :]).then_inc(hot_ready, 1)
                    v.wait_ge(e_out, 1)
                    ch.link(v.tensor_reduce(inv[:, :], tmp[:, :, :], AX.X, ALU.add))
                    ch.link(v.reciprocal(inv[:, :], inv[:, :]))
                else:
                    ch.link(v.scalar_tensor_tensor(lg2[:, :, :], oh[0][:, :, :], -BIG, lg[:, :, :], ALU.mult, ALU.add))
                    first_max(v, ch, lg2[:, :, :], mx[1][:, :], rev[:, :, :], oh[1][:, :, :], at[1][:, :])
                    v.tensor_tensor(both[:, :, :], oh[0][:, :, :], oh[1][:, :, :], ALU.add).then_inc(hot_ready, 1)
                    v.tensor_tensor(e2[:, :], mx[1][:, :], mx[0][:, :], ALU.subtract).then_inc(e_in, 1)
                    v.wait_ge(e_out, 1)
                    ch.link(v.tensor_scalar(inv[:, :], e2[:, :], 1.0, None, ALU.add))
                    ch.link(v.reciprocal(k.gate[:, 0, :], inv[:, :]))
                    ch.mark(v.tensor_tensor(k.gate[:, 1, :], k.gate[:, 0, :], e2[:, :], ALU.mult))
                v.wait_ge(cum_ready, 1)
                ch.link(v.tensor_copy(tot[:, :, :], pN[0:P, 0:T * X].rearrange(view, x=X)))
                for e in range(X):
                    ch.mark(v.tensor_tensor_scan(upto[:, :, e], k.ones[0:P, 0:T], tot[:, :, e], 0.0, ALU.mult, ALU.add))
                ch.join()
                ch.link(v.tensor_tensor(tot[:, :, :], upto[:, :, :], tot[:, :, :], ALU.subtract))
                ch.link(v.scalar_tensor_tensor(tot[:, :, :], tot[:, :, :], -1.0,
                                               pC[0:P, 0:T * X].rearrange(view, x=X), ALU.add, ALU.add))
                if layer == 0:
                    ch.link(v.tensor_tensor(tot[:, :, :], tot[:, :, :], oh[0][:, :, :], ALU.mult))
                    ch.link(v.tensor_reduce(pos[:, :], tot[:, :, :], AX.X, ALU.add))
                    ch.link(v.tensor_scalar(keep[:, :], pos[:, :], float(CAP0), None, ALU.is_lt))
                    ch.mark(v.tensor_tensor(k.gate[:, 0, :], inv[:, :], keep[:, :], ALU.mult))
                    ch.link(v.tensor_scalar(at[1][:, :], at[0][:, :], -float(ROW0), float(X * ROW0), ALU.mult, ALU.add))
                    ch.link(v.scalar_tensor_tensor(mx[1][:, :], pos[:, :], float(CAP0 - 1), at[1][:, :], ALU.min, ALU.add))
                    ch.mark(v.tensor_copy(k.back[:, 0, :], mx[1][:, :]))
                    ch.link(v.tensor_scalar(cx[:, :], cix[:, :], float(CH) / ROW0, 0.25 * CH / ROW0 - 0.5, ALU.mult, ALU.add))
                    ch.link(v.tensor_scalar(cx[:, :], cx[:, :], ROUND, ROUND, ALU.add, ALU.subtract))
                    ch.link(v.tensor_scalar(k.chunk_x[:, :], cx[:, :], float(X - 1), None, ALU.min))
                    ch.link(v.tensor_tensor(mx[0][:, :], mx[1][:, :], node[:, :], ALU.subtract))
                    ch.link(v.tensor_tensor(mx[0][:, :], mx[0][:, :], keep[:, :], ALU.mult))
                    ch.link(v.tensor_tensor(mx[0][:, :], mx[0][:, :], node[:, :], ALU.add))
                    v.tensor_copy(k.slots[:, 0, :], mx[0][:, :]).then_inc(slots_ready, 1)
                else:
                    ch.link(v.tensor_scalar(ch_i[:, :], upto[:, T - 1, :], float(CH - 1), None, ALU.add))
                    ch.link(v.tensor_scalar(ch_i[:, :], ch_i[:, :], CH.bit_length() - 1, None, ALU.logical_shift_right))
                    ch.link(v.tensor_copy(chn[:, :], ch_i[:, :]))
                    ch.link(v.tensor_tensor_scan(cto[:, :], k.ones[0:P, 0:X], chn[:, :], 0.0, ALU.mult, ALU.add))
                    ch.link(v.tensor_tensor(chn[:, :], cto[:, :], chn[:, :], ALU.subtract))
                    ch.link(v.tensor_scalar(chn[:, :], chn[:, :], float(CH), None, ALU.mult))
                    ch.link(v.tensor_tensor(tot[:, :, :], tot[:, :, :],
                                            chn[:, :].unsqueeze(1).broadcast_to([P, T, X]), ALU.add))
                    for i in range(2):
                        ch.link(v.tensor_tensor(tmp[:, :, :], tot[:, :, :], oh[i][:, :, :], ALU.mult))
                        ch.link(v.tensor_reduce(pos[:, :], tmp[:, :, :], AX.X, ALU.add))
                        ch.mark(v.tensor_copy(k.back[:, i, :], pos[:, :]))
                        ch.link(v.tensor_copy(k.slots[:, i, :], pos[:, :]))
                    ch.link(v.tensor_scalar(cx[:, :], cix[:, :], cto[0:1, 0:1], None, ALU.is_ge))
                    for e in range(1, X - 1):
                        ch.link(v.scalar_tensor_tensor(cx[:, :], cix[:, :], cto[0:1, e:e + 1], cx[:, :], ALU.is_ge, ALU.add))
                    v.tensor_copy(k.chunk_x[:, :], cx[:, :]).then_inc(slots_ready, 1)


def experts(nc, a, k, layer):
    chunks = (CHUNKS0, NCH)[layer]
    nt, pairs = CH // 128, KF // 2
    act = (ACT.Relu, ACT.Gelu)[layer]
    buf, ybuf = k.buf[layer], k.ybuf[layer]
    aw, ab = a[f"f{layer}_w"], a[f"f{layer}_b"]
    with ExitStack() as c:
        def sb(name, shape, dt=F32):
            return c.enter_context(nc.sbuf_tensor(f"{name}_e{layer}", shape, dt))

        def sem(name):
            return k.sem(nc, f"{name}_e{layer}")

        def ps(name):
            return c.enter_context(nc.psum_tensor(f"{name}_e{layer}", [128, 512], F32))

        raw = [[sb(f"w{p + 1}_raw{h}", [128, PK]) for h in range(2)] for p in range(2)]
        hi = [[sb(f"w{p + 1}_hi{h}", [128, PK], F32R) for h in range(2)] for p in range(2)]
        lo = [[sb(f"w{p + 1}_lo{h}", [128, PK], F32R) for h in range(2)] for p in range(2)]
        bias = [sb(f"bias{h}", [128, KF + D]) for h in range(2)]
        rows = [sb(f"rows{h}", [128, nt, D]) for h in range(2)]
        x_hi, x_lo = sb("x_hi", [128, KD, CH], F32R), sb("x_lo", [128, KD, CH], F32R)
        hid = [sb(f"hidden{q}", [128, 2, CH]) for q in range(2)]
        h_hi, h_lo = sb("h_hi", [128, KF, CH], F32R), sb("h_lo", [128, KF, CH], F32R)
        y = [sb(f"out_rows{h}", [128, nt, D]) for h in range(2)]
        pT, pH, pY = ps("p_T"), [ps(f"p_H{i}") for i in range(2)], [ps(f"p_Y{i}") for i in range(nt)]
        w_in = [[sem(f"w{p + 1}_in{h}") for h in range(2)] for p in range(2)]
        w_hi, w_lo = ([sem(f"w{p + 1}_{s}") for p in range(2)] for s in ("hi", "lo"))
        rows_in, bias_in, y_out, y_free = ([sem(f"{s}{h}") for h in range(2)] for s in ("rows_in", "bias_in", "y_out", "y_free"))
        turned, x_high, x_split = sem("turned"), sem("x_high"), sem("x_split")
        up, acted, h_high, h_split, down, biased = (sem(s) for s in ("up", "acted", "h_high", "h_split", "down", "biased"))

        with nc.Block() as block:
            @block.sync
            def _(sp):
                def load_rows(n, h):
                    sp.dma_start(rows[h][:, :, :], buf[bass.ds(n * CH, CH), :].rearrange("(t p) c -> p t c", p=128))\
                        .then_inc(rows_in[h], 16)

                def load_bias(e, h):
                    sp.dma_start(bias[h][:, :], ab[bass.ds(e, 1), :, :].rearrange("e p c -> p (e c)"))\
                        .then_inc(bias_in[h], 16)

                def load_w(p, e, h):
                    sp.dma_start(raw[p][h][:, :], aw[bass.ds(e, 1), p, :, :].rearrange("e p c -> p (e c)"))\
                        .then_inc(w_in[p][h], 16)

                def expert(n):
                    return sp.value_load(k.chunk_x[0:1, bass.ds(n, 1)], min_val=0, max_val=X - 1)

                e = expert(0)
                load_rows(0, 0)
                load_w(0, e, 0)
                load_bias(e, 0)
                load_w(1, e, 0)
                load_w(0, expert(1), 1)
                with sp.Fori(0, chunks // 2) as r:
                    for h in range(2):
                        n, other = r * 2 + h, 1 - h
                        e1, e2 = expert(n + 1), expert(n + 2)
                        sp.wait_ge(turned, 1 + n)
                        load_rows(n + 1, other)
                        sp.wait_ge(w_lo[1], 1 + n)
                        load_w(1, e1, other)
                        sp.wait_ge(w_lo[0], 1 + n + 1)
                        load_w(0, e2, h)
                        sp.wait_ge(biased, 1 + n * nt)
                        load_bias(e1, other)
                sp.wait_ge(bias_in[0], (chunks // 2 + 1) * 16)

            @block.scalar
            def _(s):
                one_ahead(s, acted)

                def high(p, slot, loads):
                    s.wait_ge(w_in[p][slot], loads * 16)
                    s.activation(hi[p][slot][:, :], raw[p][slot][:, :], ACT.Copy).then_inc(w_hi[p], 1)

                def store(r, h):
                    s.wait_ge(biased, 1 + (r * 2 + h + 1) * nt)
                    s.dma_start(ybuf[bass.ds((r * 2 + h) * CH, CH), :].rearrange("(t p) c -> p t c", p=128),
                                y[h][:, :, :]).then_inc(y_out[h], 16)

                high(0, 0, 1)
                high(1, 0, 1)
                high(0, 1, 1)
                with s.Fori(0, chunks // 2) as r:
                    for h in range(2):
                        n = r * 2 + h
                        s.wait_ge(bias_in[h], r * 16 + 16)
                        for q in range(pairs):
                            s.wait_ge(up, 1 + n * pairs + q + 1)
                            s.wait_ge(h_split, 1 + n * pairs + max(q - 1, 0))
                            for f in range(2):
                                s.activation(hid[q % 2][:, f, :], pH[q % 2][:, f * CH:(f + 1) * CH], act,
                                             bias=bias[h][:, 2 * q + f:2 * q + f + 1]).then_inc(acted, 1)
                        if h == 1:
                            store(r, 0)
                        s.wait_ge(down, 1 + n * nt)
                        high(1, 1 - h, r + 1 + h)
                        high(0, h, r + 2)
                    store(r, 1)
                for h in range(2):
                    s.wait_ge(y_out[h], chunks // 2 * 16)

            @block.gpsimd
            def _(g):
                one_ahead(g, *y_free, *w_lo)

                def low(p, slot, n):
                    g.wait_ge(w_hi[p], n)
                    g.tensor_tensor(lo[p][slot][:, :], raw[p][slot][:, :], hi[p][slot][:, :].bitcast(F32),
                                    ALU.subtract).then_inc(w_lo[p], 1)

                low(0, 0, 1)
                low(1, 0, 1)
                low(0, 1, 2)
                with g.Fori(0, chunks // 2) as r:
                    for h in range(2):
                        n = r * 2 + h
                        low(1, 1 - h, n + 2)
                        low(0, h, n + 3)
                    for h in range(2):
                        g.wait_ge(y_out[h], r * 16 + 16)
                        g.sem_inc(y_free[h], 1)

            @block.vector
            def _(v):
                one_ahead(v, h_split, biased)
                both = pT[:, :].rearrange("p (i n) -> p i n", i=KD)

                def split_x(n):
                    v.wait_ge(turned, 1 + n + 1)
                    v.tensor_copy(x_hi[:, :, :], both).then_inc(x_high, 1)
                    v.wait_ge(x_high, n + 1)
                    v.tensor_tensor(x_lo[:, :, :], both, x_hi[:, :, :].bitcast(F32), ALU.subtract).then_inc(x_split, 1)

                split_x(0)
                with v.Fori(0, chunks // 2) as r:
                    for h in range(2):
                        n = r * 2 + h
                        for q in range(pairs):
                            pair = slice(2 * q, 2 * q + 2)
                            v.wait_ge(acted, 1 + n * KF + 2 * q + 2)
                            v.wait_ge(down, 1 + n * nt)
                            v.tensor_copy(h_hi[:, pair, :], hid[q % 2][:, :, :]).then_inc(h_high, 1)
                            v.wait_ge(h_high, n * pairs + q + 1)
                            v.tensor_tensor(h_lo[:, pair, :], hid[q % 2][:, :, :], h_hi[:, pair, :].bitcast(F32),
                                            ALU.subtract).then_inc(h_split, 1)
                        split_x(n + 1)
                        v.wait_ge(y_free[h], r + 1)
                        for t in range(nt):
                            v.wait_ge(down, 1 + n * nt + t + 1)
                            v.tensor_tensor(y[h][:, t, :], pY[t][:, 0:D], bias[h][:, KF:KF + D], ALU.add)\
                                .then_inc(biased, 1)

            @block.tensor
            def _(pe):
                one_ahead(pe, down, up, turned)

                def product(out, stationary, moving, first, last):
                    nc.tensor.matmul(out, stationary[0], moving[0], start=first, stop=False)
                    nc.tensor.matmul(out, stationary[0], moving[1], start=False, stop=False)
                    return nc.tensor.matmul(out, stationary[1], moving[0], start=False, stop=last)

                def turn(h, loads):
                    pe.wait_ge(rows_in[h], loads * 16)
                    for i in range(KD):
                        for t in range(nt):
                            last = nc.tensor.transpose(pT[:, i * CH + t * 128:i * CH + (t + 1) * 128],
                                                       rows[h][:, t, i * 128:(i + 1) * 128], k.ident[:, :])
                    last.then_inc(turned, 1)

                def first(n, h):
                    pe.wait_ge(w_lo[0], 1 + n + 1)
                    pe.wait_ge(x_split, n + 1)
                    for q in range(pairs):
                        pe.wait_ge(acted, 1 + n * KF + 2 * max(q - 1, 0))
                        for f in range(2):
                            for i in range(KD):
                                at = i * FF + (2 * q + f) * 128
                                last = product(pH[q % 2][:, f * CH:(f + 1) * CH],
                                               (hi[0][h][:, at:at + 128], lo[0][h][:, at:at + 128]),
                                               (x_hi[:, i, :], x_lo[:, i, :]), i == 0, i == KD - 1)
                        last.then_inc(up, 1)

                def second(n, h):
                    pe.wait_ge(w_lo[1], 1 + n + 1)
                    pe.wait_ge(biased, 1 + n * nt)
                    for t in range(nt):
                        for f in range(KF):
                            if t == 0 and f % 2 == 0:
                                pe.wait_ge(h_split, 1 + n * pairs + f // 2 + 1)
                            at = slice(t * 128, (t + 1) * 128)
                            last = product(pY[t][:, 0:D], (h_hi[:, f, at], h_lo[:, f, at]),
                                           (hi[1][h][:, f * D:(f + 1) * D], lo[1][h][:, f * D:(f + 1) * D]),
                                           f == 0, f == KF - 1)
                        last.then_inc(down, 1)

                turn(0, 1)
                with pe.Fori(0, chunks // 2) as r:
                    for h in range(2):
                        n = r * 2 + h
                        first(n, h)
                        turn(1 - h, r + 1 + h)
                        second(n, h)


def combine(nc, a, k, layer):
    with ExitStack() as c:
        def sem(name):
            return k.sem(nc, f"{name}_c{layer}")

        got = k.got
        vec, stored = sem("vec"), sem("stored")
        held = [c.enter_context(nc.sbuf_tensor(f"picked{i}_c{layer}", [P, T, D], F32)) for i in range(layer + 1)]
        guard = [c.enter_context(nc.sbuf_tensor(f"guard{i}", [P, GT, D], F32)) for i in range(3)] if layer == 0 else None
        fin = c.enter_context(nc.sbuf_tensor("guard_ok", [P, GT, D], I32)) if layer == 0 else None

        with nc.Block() as block:
            @block.gpsimd
            def _(g):
                for t in range(T):
                    for i in range(layer + 1):
                        g.indirect_dma_start(
                            out=held[i][:, t, :], out_offset=None, in_=k.ybuf[layer],
                            in_offset=bass.IndirectOffsetOnAxis(ap=k.back[:, i, t:t + 1], axis=0)).then_inc(got[t], 16)

            @block.vector
            def _(v):
                ch = Chain(v, vec)
                if layer == 0:
                    for r in range(GR):
                        ts = slice(r * GT, (r + 1) * GT)
                        y = held[0][:, ts, :]
                        for t in range(r * GT, (r + 1) * GT):
                            v.wait_ge(got[t], 16)
                            ch.mark(v.tensor_scalar(held[0][:, t, :], held[0][:, t, :], k.gate[:, 0, t:t + 1], None, ALU.mult))
                        ch.join()
                        ch.mark(v.tensor_scalar(fin[:, :, :], y, 0.0, 0.0, ALU.mult, ALU.is_equal))
                        ch.mark(v.tensor_scalar(guard[0][:, :, :], y, BIG, 1e4, ALU.is_gt, ALU.mult))
                        ch.link(v.tensor_scalar(guard[1][:, :, :], y, -BIG, -1e4, ALU.is_lt, ALU.mult))
                        ch.link(v.tensor_tensor(guard[2][:, :, :], guard[0][:, :, :], guard[1][:, :, :], ALU.add))
                        ch.link(v.copy_predicated(guard[2][:, :, :], fin[:, :, :], y))
                        ch.link(v.tensor_tensor(k.x[:, ts, :], k.x[:, ts, :], guard[2][:, :, :], ALU.add))
                        for t in range(r * GT, (r + 1) * GT):
                            ch.mark(v.bn_stats(k.stats[:, t, :], k.x[:, t, :]))
                else:
                    for t in range(T):
                        v.wait_ge(got[t], 16 + 32)
                        ch.link(v.scalar_tensor_tensor(k.x[:, t, :], held[0][:, t, :], k.gate[:, 0, t:t + 1], k.x[:, t, :],
                                                       ALU.mult, ALU.add))
                        ch.mark(v.scalar_tensor_tensor(k.x[:, t, :], held[1][:, t, :], k.gate[:, 1, t:t + 1], k.x[:, t, :],
                                                       ALU.mult, ALU.add))

            @block.sync
            def _(sp):
                if layer == 1:
                    for r in range(GR):
                        ts = slice(r * GT, (r + 1) * GT)
                        sp.wait_ge(vec, 2 * GT * (r + 1))
                        sp.dma_start(a["out"][:, ts, :], k.x[:, ts, :]).then_inc(stored, 16)
                    sp.wait_ge(stored, 16 * GR)


def project(nc, a, k):
    w = k.w
    with ExitStack() as c:
        def sb(name, shape):
            return c.enter_context(nc.sbuf_tensor(name, shape, F32))

        def sem(name):
            return k.sem(nc, name)

        def ps(name):
            return c.enter_context(nc.psum_tensor(name, [128, 512], F32))

        xs, xT = sb("p_rows", [P, GT, D]), sb("p_rowsT", [128, GT, KD, P])
        xj, junk = sb("xj", [P, GT, XJW]), sb("xj_wa2", [P, D])
        low, kk, vv = sb("k_low", [P, D]), sb("k_feat", [P, GT, D]), sb("v_rows", [P, GT, D + 1])
        xi = sb("xi_T", [128, KD, P])
        ba = sb("ba12", [128, 1])
        zero = sb("zero_row", [1, D + 1])
        pT, pJ, pK, pV, pI, pA = (ps(n) for n in ("p_pT", "p_xj", "p_k", "p_v", "p_xi", "p_a1"))
        pc = [ps(f"p_ctx{i}") for i in range(KD)]
        normed, turned, copied, kept = sem("p_normed"), sem("p_turned"), sem("p_copied"), sem("p_kept")
        init, vec, var_ready, root_ready = sem("p_init"), sem("p_vec"), sem("p_var"), sem("p_root")
        xj_mm, kv_mm, xi_mm, a1_mm, ctx_mm = sem("xj_mm"), sem("kv_mm"), sem("xi_mm"), sem("a1_mm"), sem("ctx_mm")
        xj_max, xi_max, xj_free = sem("xj_max"), sem("xi_max"), sem("xj_free")
        xj_act, a2_ready, v_ready, low_ready, exp_ready = sem("xj_act"), sem("a2_ready"), sem("v_ready"), sem("low_ready"), sem("exp_ready")
        k_ready, xi_ready, a1_ready, xj_out, sums = sem("k_ready"), sem("xi_ready"), sem("a1_ready"), sem("xj_out"), sem("p_sums")

        with nc.Block() as block:
            @block.gpsimd
            def _(g):
                g.memset(xj[:, :, D:XJW], 0.0).then_inc(init, 1)
                g.memset(vv[:, :, D], 1.0).then_inc(init, 1)
                g.memset(zero[:, :], 0.0).then_inc(init, 1)
                g.memset(k.ctx[:, :, :, :], 0.0).then_inc(init, 1)
                g.memset(k.x_all[:, T, :], 0.0).then_inc(init, 1)
                g.memset(k.xnT[:, :, N:N + P], 0.0).then_inc(init, 1)
                for r in range(GR):
                    x = k.x[:, r * GT:(r + 1) * GT, :]
                    g.wait_ge(kept, 1 + 2 * GT * (r + 1))
                    g.tensor_tensor(x, x, k.xn[:, r * GT:(r + 1) * GT, :], ALU.add).then_inc(sums, 1)
                    g.wait_ge(sums, r * 2 + 1)
                    g.tensor_tensor(x, x, w["m1_bp"][0:P, :].unsqueeze(1).broadcast_to([P, GT, D]), ALU.add)\
                        .then_inc(sums, 1)

            @block.sync
            def _(sp):
                one_ahead(sp, xj_free)
                with sp.Fori(0, GR) as r:
                    sp.wait_ge(a2_ready, r * GT + GT)
                    sp.dma_start(k.xj_d[bass.ds(r * GT * P, GT * P), :].rearrange("(t p) c -> p t c", p=P),
                                 xj[:, :, :]).then_inc(xj_out, 16)
                    sp.wait_ge(xj_out, r * 16 + 16)
                    sp.sem_inc(xj_free, 1)

            @block.scalar
            def _(s):
                one_ahead(s, kept, copied, v_ready, xi_ready, exp_ready)
                norm_root_scalar(s, k, var_ready, root_ready, 1)
                s.wait_ge(init, 6)
                with s.Fori(0, GR) as r:
                    for t in range(GT):
                        m = r * GT + t
                        s.wait_ge(turned, m + 1)
                        view = pT[:, 0:KD * P].rearrange("p (a b) -> p a b", a=KD)
                        s.activation(xT[:, t, :, :], view, ACT.Copy).then_inc(copied, 1)
                        s.activation(k.xnT[:, :, bass.ds(m * P, P)], view, ACT.Copy).then_inc(kept, 1)
                        s.activation(k.xn[:, bass.ds(m, 1), :], xs[:, t:t + 1, :], ACT.Copy).then_inc(kept, 1)
                        if t == 0:
                            s.wait_ge(xj_free, r + 1)
                        s.wait_ge(xj_mm, m + 1)
                        s.activation(xj[:, t, 0:D], pJ[0:P, 0:D], ACT.Copy, scale=0.2).then_inc(xj_act, 1)
                        s.wait_ge(kv_mm, m + 1)
                        if t == 0:
                            s.wait_ge(ctx_mm, 1 + r * GT)
                        s.activation(vv[:, t, 0:D], pV[0:P, 0:D], ACT.Copy).then_inc(v_ready, 1)
                        s.wait_ge(low_ready, m + 1)
                        s.activation(kk[:, t, :], low[:, :], ACT.Exp).then_inc(exp_ready, 1)
                        s.wait_ge(xi_mm, m + 1)
                        for i in range(KD):
                            s.activation(xi[:, i, :], pI[:, i * P:(i + 1) * P], ACT.Identity,
                                         bias=w["g1_b1"][:, i:i + 1]).then_inc(xi_ready, 1)

            @block.vector
            def _(v):
                one_ahead(v, xj_max, k_ready, a1_ready)
                ch = Chain(v, vec)
                norm_scale_vector(nc, v, ch, k, var_ready, root_ready, 1)
                ch.link(v.tensor_tensor(ba[:, :], w["g1_ba1"][:, :], w["g1_ba2"][:, :], ALU.add))
                v.wait_ge(init, 6)
                with v.Fori(0, GR) as r:
                    v.wait_ge(kept, 1 + r * 2 * GT)
                    for t in range(GT):
                        one = bass.ds(r * GT + t, 1)
                        v.tensor_scalar(xs[:, t:t + 1, :], k.x[:, one, :], k.mean[:, one], k.rstd[:, one],
                                        ALU.subtract, ALU.mult).then_inc(normed, 1)
                    for t in range(GT):
                        m = r * GT + t
                        v.wait_ge(kv_mm, m + 1)
                        v.wait_ge(exp_ready, 1 + m)
                        v.tensor_scalar(low[:, :], pK[0:P, 0:D], 0.0, None, ALU.min).then_inc(low_ready, 1)
                        v.wait_ge(xj_act, m + 1)
                        v.tensor_tensor(xj[:, t, 0:D], xj[:, t, 0:D], pJ[0:P, 0:D], ALU.max).then_inc(xj_max, 1)
                        v.wait_ge(xj_max, 1 + m + 1)
                        v.scalar_tensor_tensor(junk[:, :], xj[:, t, 0:D], 1.0, w["g1_wa2"][0:P, :], ALU.mult, ALU.mult,
                                               accum_out=xj[:, t, D:D + 1]).then_inc(a2_ready, 1)
                        v.wait_ge(a2_ready, m + 1)
                        v.wait_ge(exp_ready, 1 + m + 1)
                        v.scalar_tensor_tensor(kk[:, t, :], pK[0:P, 0:D], 0.0, kk[:, t, :], ALU.max, ALU.add)\
                            .then_inc(k_ready, 1)
                        v.wait_ge(xi_ready, 1 + (m + 1) * KD)
                        v.scalar_tensor_tensor(xi[:, :, :], xi[:, :, :], 0.2, xi[:, :, :], ALU.mult, ALU.max)\
                            .then_inc(xi_max, 1)
                        v.wait_ge(a1_mm, m + 1)
                        v.tensor_scalar(k.a1[:, bass.ds(m, 1), :], pA[:, 0:P].unsqueeze(1), ba[:, 0:1], None, ALU.add)\
                            .then_inc(a1_ready, 1)
                v.wait_ge(ctx_mm, 1 + T + 1)
                for h in range(HEADS):
                    i, q = h * HD // 128, h * HD % 128
                    v.tensor_copy(k.ctx[q:q + HD, i, 0, q:q + HD], pc[i][q:q + HD, h * HD:(h + 1) * HD])
                    v.tensor_copy(k.ctx[q:q + HD, i, 1, q:q + HD], pc[i][q:q + HD, D:D + 1].broadcast_to([HD, HD]))

            @block.tensor
            def _(pe):
                one_ahead(pe, ctx_mm)
                pe.wait_ge(init, 6)
                for i in range(KD):
                    nc.tensor.matmul(pc[i][:, 0:D + 1], k.ones[0:1, :], zero[:, :], start=True, stop=False)
                with pe.Fori(0, GR) as r:
                    for t in range(GT):
                        m = r * GT + t
                        pe.wait_ge(normed, m + 1)
                        pe.wait_ge(kept, 1 + m * 2)
                        pe.wait_ge(copied, 1 + m)
                        for i in range(KD):
                            last = nc.tensor.transpose(pT[:, i * P:(i + 1) * P], xs[:, t, i * 128:(i + 1) * 128],
                                                       k.ident[0:P, 0:P])
                        last.then_inc(turned, 1)
                        pe.wait_ge(copied, 1 + m + 1)
                        pe.wait_ge(xj_max, 1 + m)
                        for i in range(KD):
                            nc.tensor.matmul(pJ[0:P, 0:D], xT[:, t, i, :], w["g1_W2"][:, i, :], start=i == 0, stop=False)
                        nc.tensor.matmul(pJ[0:P, 0:D], k.ones[0:1, 0:P], w["g1_b2"][:, :], start=False, stop=True)\
                            .then_inc(xj_mm, 1)
                        pe.wait_ge(k_ready, 1 + m)
                        pe.wait_ge(v_ready, 1 + m)
                        for bank, at in ((pK, 0), (pV, D)):
                            for i in range(KD):
                                last = nc.tensor.matmul(bank[0:P, 0:D], xT[:, t, i, :], w["m1_WkvT"][:, i, at:at + D],
                                                        start=i == 0, stop=i == KD - 1)
                        last.then_inc(kv_mm, 1)
                        pe.wait_ge(xi_ready, 1 + m * KD)
                        for o in range(KD):
                            for i in range(KD):
                                last = nc.tensor.matmul(pI[:, o * P:(o + 1) * P], w["g1_W1"][:, i, o * 128:(o + 1) * 128],
                                                        xT[:, t, i, :], start=i == 0, stop=i == KD - 1)
                        last.then_inc(xi_mm, 1)
                        pe.wait_ge(xi_max, m + 1)
                        pe.wait_ge(a1_ready, 1 + m)
                        for o in range(KD):
                            last = nc.tensor.matmul(pA[:, 0:P], w["g1_wa1"][:, o, :], xi[:, o, :],
                                                    start=o == 0, stop=o == KD - 1)
                        last.then_inc(a1_mm, 1)
                        pe.wait_ge(k_ready, 1 + m + 1)
                        pe.wait_ge(v_ready, 1 + m + 1)
                        for i in range(KD):
                            last = nc.tensor.matmul(pc[i][:, 0:D + 1], kk[:, t, i * 128:(i + 1) * 128], vv[:, t, :],
                                                    start=False, stop=False)
                        last.then_inc(ctx_mm, 1)
                for i in range(KD):
                    last = nc.tensor.matmul(pc[i][:, 0:D + 1], k.ones[0:1, :], zero[:, :], start=False, stop=True)
                last.then_inc(ctx_mm, 1)


def columns(w, blocks=None):
    return w.reshape(-1, 128, w.shape[-1]).transpose(1, 0, 2)


def kernel(**inputs):
    import numpy as np
    from concourse import bacc
    from concourse.bass_utils import run_bass_kernel_spmd

    x = {n: np.asarray(v) for n, v in inputs.items()}

    def spread(v):
        return np.broadcast_to(v.reshape(1, -1), (128, v.size))

    def pack(w1, w2):
        return np.stack([w1.reshape(X, KD, 128, FF).transpose(0, 2, 1, 3).reshape(X, 128, PK),
                         w2.reshape(X, KF, 128, D).transpose(0, 2, 1, 3).reshape(X, 128, PK)], axis=1)

    def biases(b1, b2):
        return np.concatenate([b1.reshape(X, KF, 128).transpose(0, 2, 1),
                               np.broadcast_to(b2.reshape(X, 1, D), (X, 128, D))], axis=2)

    arrays = {
        "x": x["x"].reshape(T, P, D).transpose(1, 0, 2),
        "src": x["src"].reshape(P, EC), "dst": x["dst"].reshape(P, EC),
        "edge_weight": x["edge_weight"].reshape(P, EC),
        "g0_W1": columns(x["L0_gnn_W1"]), "g0_b1": x["L0_gnn_b1"].reshape(-1, 128).T,
        "g0_W2": columns(x["L0_gnn_W2"]), "g0_b2": x["L0_gnn_b2"].reshape(1, D),
        "m0_Wq": columns(x["L0_mix_Wq"]), "m0_WkT": columns(x["L0_mix_Wk"].T), "m0_WvT": columns(x["L0_mix_Wv"].T),
        "m0_WfcT": columns(x["L0_mix_Wfc"].T), "m0_bqc": x["L0_mix_bq"].reshape(-1, 128).T,
        "m0_bk": x["L0_mix_bk"].reshape(1, D), "m0_bv": x["L0_mix_bv"].reshape(1, D),
        "m0_bfc": x["L0_mix_bfc"].reshape(1, D),
        "f0_gw": columns(x["L0_ffn_gate_w"]), "f0_gb": spread(np.tile(x["L0_ffn_gate_b"], T)).reshape(128, T, X),
        "f0_w": pack(x["L0_ffn_w1"], x["L0_ffn_w2"]), "f0_b": biases(x["L0_ffn_b1"], x["L0_ffn_b2"]),
        "g1_W1": columns(x["L1_gnn_W1"]), "g1_b1": x["L1_gnn_b1"].reshape(-1, 128).T,
        "g1_W2": columns(x["L1_gnn_W2"]), "g1_b2": x["L1_gnn_b2"].reshape(1, D),
        "g1_wa1": np.broadcast_to(x["L1_gnn_wa1"].reshape(KD, 128, 1).transpose(1, 0, 2), (128, KD, 128)),
        "g1_ba1": spread(x["L1_gnn_ba1"]), "g1_wa2": spread(x["L1_gnn_wa2"]), "g1_ba2": spread(x["L1_gnn_ba2"]),
        "m1_WqT": columns(x["L1_mix_Wq"].T), "m1_WkvT": columns(x["L1_mix_Wkv"].T),
        "m1_WpT": columns(x["L1_mix_Wproj"].T), "m1_bp": spread(x["L1_mix_bproj"]),
        "f1_gw": columns(x["L1_ffn_Wg"]), "f1_gb": spread(np.tile(x["L1_ffn_bg"], T)).reshape(128, T, X),
        "f1_w": pack(x["L1_ffn_W1"], x["L1_ffn_W2"]), "f1_b": biases(x["L1_ffn_b1"], x["L1_ffn_b2"]),
    }
    arrays = {n: np.ascontiguousarray(v) for n, v in arrays.items()}
    nc = bacc.Bacc("TRN2", target_bir_lowering=False, num_devices=1)
    a = {n: nc.dram_tensor(f"in_{n}", v.shape, mybir.dt.from_np(v.dtype), kind="ExternalInput").ap()
         for n, v in arrays.items()}
    a["out"] = nc.dram_tensor("out", (P, T, D), F32, kind="ExternalOutput").ap()
    build(nc, a)
    r = run_bass_kernel_spmd(nc, [{f"in_{n}": v for n, v in arrays.items()}], core_ids=[0])
    return np.ascontiguousarray(r.results[0]["out"].transpose(1, 0, 2)).reshape(N, D)
```

```python
from contextlib import ExitStack, contextmanager

import concourse.bass as bass
from concourse import mybir

F32 = mybir.dt.float32
F32R = mybir.dt.float32r
I32 = mybir.dt.int32
U16 = mybir.dt.uint16
ALU = mybir.AluOpType
ACT = mybir.ActivationFunctionType
AX = mybir.AxisListType

N, D, E = 3125, 256, 50000
P, T = 125, 25
KD = D // 128
EC = E // P
F0 = 512
FF, KF = 1024, 1024 // 128
X = 8
HD = 32
HEADS = D // HD
GT = 5
GR = T // GT
EB = 16
ET = -(-((E + T * 127) // 128) // EB) * EB
ETP = ET + EB
CAP0 = -(-5 * N // (4 * X))
CH = 256
ROW0 = -(-CAP0 // CH) * CH
CHUNKS0 = X * ROW0 // CH
NCH = (2 * N + X * (CH - 1)) // CH
PK = KD * FF
assert PK == KF * D
ROUND = 12582912.0
ZR = 4
SH = 4
EC_R = EC // T
BIG = 3.4028234663852886e38
XJW = 264


class Chain:

    def __init__(self, eng, sem, base=0):
        self.eng, self.sem, self.n, self.base = eng, sem, 0, base

    def mark(self, ins):
        self.n += 1
        ins.then_inc(self.sem, 1)

    def join(self):
        self.eng.wait_ge(self.sem, self.base + self.n)

    def link(self, ins):
        self.mark(ins)
        self.join()


def one_ahead(eng, *sems):
    for s in sems:
        eng.sem_inc(s, 1)


def slots_free(eng, n, *sems):
    for s in sems:
        eng.sem_inc(s, n)


def build(nc, a):
    persist = ExitStack()

    def sb(name, shape, dt=F32, ctx=persist):
        return ctx.enter_context(nc.sbuf_tensor(name, shape, dt))

    with persist:
        k = Shared(nc, sb, a)
        k.landed = [persist.enter_context(nc.semaphore(f"landed{s}")) for s in range(EB)]
        k.got = [persist.enter_context(nc.semaphore(f"got{t}")) for t in range(T)]
        with k.node_rows(nc, 0):
            prepare(nc, a, k)
            aggregate(nc, a, k, 0)
            gin(nc, a, k)
            route(nc, a, k, 0)
        experts(nc, a, k, 0)
        combine(nc, a, k, 0)
        k.recycle(nc)
        with k.node_rows(nc, 1):
            project(nc, a, k)
            aggregate(nc, a, k, 1)
            route(nc, a, k, 1)
        experts(nc, a, k, 1)
        combine(nc, a, k, 1)


class Shared:

    def sem(self, nc, name):
        self.sems.append(nc.alloc_semaphore(name))
        return self.sems[-1]

    def recycle(self, nc):
        nc.clear_and_free_semaphores(self.sems)
        nc.all_engine_barrier()
        self.sems = []

    @contextmanager
    def node_rows(self, nc, layer):
        with ExitStack() as c:
            def sb(name, shape):
                return c.enter_context(nc.sbuf_tensor(f"{name}{layer}", shape, F32))

            self.xn_all = sb("x_normed", [P, T + 1, D])
            self.xn = self.xn_all[:, 0:T, :]
            if layer == 0:
                for name in WEIGHTS:
                    if name[:3] in ("g0_", "m0_"):
                        self.w[name] = sb("w_" + name, WEIGHTS[name])
                self.acc = sb("node_sums", [P, T, D])
            else:
                self.xnT = sb("x_normed_T", [128, KD, N + P])
                self.a1 = sb("a1_rows", [128, T, P])
            yield

    def __init__(self, nc, sb, a):
        self.sems = []
        self.x_all = sb("x_res", [P, T + 1, D])
        self.x = self.x_all[:, 0:T, :]
        self.edges = sb("sorted_edges", [128, ETP, 4])
        self.tile_bin = sb("tile_bin", [1, ETP], I32)
        self.ident = sb("ident", [128, 128])
        self.tri = sb("tri_strict", [128, 128])
        self.tri1 = sb("tri_incl", [128, 128])
        self.ones = sb("ones", [128, 128])
        self.iota = sb("iota_row", [128, 128])
        self.stats = sb("ln_stats", [P, T, 6])
        self.mean = sb("ln_mean", [P, T])
        self.rstd = sb("ln_rstd", [P, T])
        self.lnt = sb("ln_tmp", [P, 4, T])
        self.slots = sb("slots", [P, 2, T], I32)
        self.back = sb("slots_back", [P, 2, T], I32)
        self.gate = sb("gates", [P, 2, T])
        self.chunk_x = sb("chunk_expert", [1, NCH + 2], I32)
        self.w_early = sb("w_raw_early", [128, 3, PK])
        self.w = {}
        for name, shape in WEIGHTS.items():
            if name[:3] not in ("g0_", "m0_"):
                self.w[name] = sb("w_" + name, shape)
        self.R = sb("mix0_R", [128, KD, D])
        self.r0 = sb("mix0_r0", [1, D])
        self.ctx = sb("mix1_ctx", [128, KD, 2, 128])
        self.edges_d = nc.dram_tensor("edges_d", [128 * ETP, 4], F32).ap()
        self.xn_d = nc.dram_tensor("xn_d", [N, D], F32).ap()
        self.xj_d = nc.dram_tensor("xj_d", [N, XJW], F32).ap()
        self.buf = [nc.dram_tensor("rows0_d", [X * ROW0 + CH + N, D], F32).ap(),
                    nc.dram_tensor("rows1_d", [NCH * CH + CH, D], F32).ap()]
        self.ybuf = [nc.dram_tensor("y0_d", [X * ROW0, D], F32).ap(),
                     nc.dram_tensor("y1_d", [NCH * CH, D], F32).ap()]


WEIGHTS = {
    "g0_W1": [128, KD, F0], "g0_b1": [128, F0 // 128], "g0_W2": [128, F0 // 128, D], "g0_b2": [1, D],
    "m0_Wq": [128, KD, D], "m0_WkT": [128, KD, D], "m0_WvT": [128, KD, D], "m0_WfcT": [128, KD, D],
    "m0_bqc": [128, KD], "m0_bk": [1, D], "m0_bv": [1, D], "m0_bfc": [1, D],
    "f0_gw": [128, KD, X], "f0_gb": [128, T, X],
    "g1_W1": [128, KD, D], "g1_b1": [128, KD], "g1_W2": [128, KD, D], "g1_b2": [128, D],
    "g1_wa1": [128, KD, 128], "g1_ba1": [128, 1], "g1_wa2": [128, D], "g1_ba2": [128, 1],
    "m1_WqT": [128, KD, D], "m1_WkvT": [128, KD, 2 * D], "m1_WpT": [128, KD, D], "m1_bp": [128, D],
    "f1_gw": [128, KD, X], "f1_gb": [128, T, X],
}


def norm_scale_vector(nc, v, ch, k, var_ready, root_ready, n):
    st, t = k.stats, k.lnt
    even, odd = st[:, :, 1], st[:, :, 4]
    ch.mark(v.tensor_tensor(k.mean[:, :], even, odd, ALU.add))
    ch.mark(v.tensor_tensor(t[:, 0, :], even, odd, ALU.subtract))
    ch.link(v.tensor_tensor(t[:, 1, :], st[:, :, 2], st[:, :, 5], ALU.add))
    ch.mark(v.tensor_scalar(k.mean[:, :], k.mean[:, :], 0.5, None, ALU.mult))
    ch.mark(v.tensor_tensor(t[:, 0, :], t[:, 0, :], t[:, 0, :], ALU.mult))
    ch.link(v.tensor_scalar(t[:, 1, :], t[:, 1, :], 1.0 / D, 1e-5, ALU.mult, ALU.add))
    v.scalar_tensor_tensor(t[:, 1, :], t[:, 0, :], 0.25, t[:, 1, :], ALU.mult, ALU.add).then_inc(var_ready, 1)
    v.wait_ge(root_ready, n)
    ch.link(v.reciprocal(k.rstd[:, :], t[:, 2, :]))
    ch.link(v.tensor_tensor(t[:, 0, :], k.rstd[:, :], k.rstd[:, :], ALU.mult))
    ch.link(v.tensor_tensor(t[:, 0, :], t[:, 0, :], t[:, 1, :], ALU.mult))
    ch.link(v.tensor_scalar(t[:, 0, :], t[:, 0, :], -0.5, 1.5, ALU.mult, ALU.add))
    ch.link(v.tensor_tensor(k.rstd[:, :], k.rstd[:, :], t[:, 0, :], ALU.mult))


def norm_root_scalar(s, k, var_ready, root_ready, n):
    s.wait_ge(var_ready, n)
    s.activation(k.lnt[:, 2, :], k.lnt[:, 1, :], ACT.Sqrt).then_inc(root_ready, 1)


def prepare(nc, a, k):
    with ExitStack() as c:
        def sb(name, shape, dt=F32):
            return c.enter_context(nc.sbuf_tensor(name, shape, dt))

        def sem(name):
            return k.sem(nc, name)

        src_i, dst_i = sb("src_i", [P, EC], I32), sb("dst_i", [P, EC], I32)
        w_e = sb("w_e", [P, EC])
        rec = sb("edge_rec", [P, EC, 4])
        w_high = sb("w_high", [P, EC], F32R)
        src_f, bin_f = sb("src_f", [P, EC]), sb("bin_f", [P, EC])
        early = k.w_early[:, :, :].rearrange("p s c -> p (s c)")
        mask = early[0:P, :].bitcast(U16)[:, 0:T * EC].rearrange("p (t e) -> p t e", e=EC)
        run = k.acc[:, :, :].rearrange("p t c -> p (t c)")[:, 0:2 * EC].rearrange("p (t e) -> p t e", e=EC)
        pos, tmp = sb("edge_pos", [P, EC]), sb("edge_tmp", [P, EC])
        high = sb("edge_high", [P, EC])
        pos_i, low_i = sb("edge_pos_i", [P, EC], I32), sb("edge_low_i", [P, EC], I32)
        cnt, off = sb("bin_cnt", [P, T]), sb("bin_off", [128, T])
        tot_i, tiles, tiles_to = sb("bin_tot_i", [128, T], I32), sb("bin_tiles", [128, T]), sb("bin_tiles_to", [128, T])
        tix, ends_at, ended = sb("tile_ix", [128, ETP]), sb("bin_ends_at", [T - 1, 1]), sb("bin_ended", [T - 1, ETP])
        iota_i, tix_i = sb("iota_i", [128, 128], I32), sb("tix_i", [128, ETP], I32)
        zero = sb("zero_rows", [128, ZR * D])
        idx_st = sb("scatter_idx", [P, 2, SH], I32)
        rec_st = sb("scatter_rec", [P, 2, SH, 4])
        HS = 4
        BY_SCALAR = (3, 7)
        hot_p = [sb(f"hot_row{i}", [P, 4, 128], F32R) for i in range(HS)]
        hot_t = [sb(f"hot_tile{i}", [P, ET], F32R) for i in range(HS)]
        xs = sb("normed_tile", [P, D + 1])
        places = [early[:, i * KD * (D + 1):(i + 1) * KD * (D + 1)]
                  .rearrange("p (i c) -> p i c", i=KD) for i in range(4)]
        G, U, KV, M2 = places[0], *(m[:, :, 0:D] for m in places[1:])
        at = 4 * KD * (D + 1)
        Ul, srow = early[0:1, at:at + D], early[0:1, at + D:at + 2 * D]
        nconst = sb("n_const", [1, 1])
        pc = c.enter_context(nc.psum_tensor("p_counts", [128, 512], F32))
        pg = [c.enter_context(nc.psum_tensor(f"p_gram{i}", [128, 512], F32)) for i in range(KD)]
        pu = pg
        pS = [c.enter_context(nc.psum_tensor(f"p_sorted{i}", [128, 512], F32)) for i in range(4)]
        psr = c.enter_context(nc.psum_tensor("p_sumrow", [128, 512], F32))

        IOTAS = 13
        x_in, edges_in, w_in = sem("x_in"), sem("edges_in"), sem("w_in")
        consts, iotas = sem("consts"), sem("iotas")
        prefilled, zeroed = sem("prefilled"), sem("zeroed")
        vec, cnt_ready, prefix = sem("vec"), sem("cnt_ready"), sem("prefix")
        idx_ready, begun = sem("idx_ready"), sem("scatter_begun")
        staged = [sem(f"staged{i}") for i in range(2)]
        scattered = [sem(f"scattered{i}") for i in range(2)]
        stage_free = [sem(f"stage_free{i}") for i in range(2)]
        reload, var_ready, root_ready = sem("reload"), sem("var_ready"), sem("root_ready")
        xs_ready, kept, xn_out = sem("xs_ready"), sem("xn_kept"), sem("xn_out")
        scanned, taken = sem("scanned"), sem("taken")
        abs_made, hot_act = sem("abs_made"), sem("hot_act")
        neg_high, away = early[0:P, 3 * PK - 1024:3 * PK - 1024 + EC], early[0:P, 3 * PK - 512:3 * PK - 512 + ET]
        bin_steps, bin_mm = sem("bin_steps"), sem("bin_mm")
        hot_made, placed, gram_step = sem("hot_made"), sem("placed"), sem("gram_step")
        gram_done, mixed, mix_copied = sem("gram_done"), sem("mixed"), sem("mix_copied")
        lnc = sem("ln_chain")

        with nc.Block() as block:
            @block.sync
            def _(sp):
                sp.dma_start(src_i[:, :], a["src"]).then_inc(edges_in, 16)
                sp.dma_start(dst_i[:, :], a["dst"]).then_inc(edges_in, 16)
                sp.dma_start(w_e[:, :], a["edge_weight"]).then_inc(edges_in, 16)
                sp.dma_start(k.x[:, :, :], a["x"]).then_inc(x_in, 16)
                sp.wait_ge(consts, 1)
                sp.dma_start(k.edges_d.rearrange("(p t) c -> p (t c)", p=128),
                             k.edges[:, :, :].rearrange("p t c -> p (t c)")).then_inc(prefilled, 16)
                fills = 0
                for buf, rows in ((k.buf[0], X * ROW0 + CH), (k.buf[1], NCH * CH + CH)):
                    for r in range(0, rows, ZR * 128):
                        m = min(ZR * 128, rows - r)
                        sp.dma_start(buf[r:r + m, :].rearrange("(p t) c -> p (t c)", p=128),
                                     zero[:, 0:m // 128 * D]).then_inc(zeroed, 16)
                        fills += 1
                one_ahead(sp, *stage_free)
                with sp.Fori(0, T) as r:
                    for h in range(2):
                        sp.wait_ge(scattered[h], r * 16 * SH + 16 * SH)
                        sp.sem_inc(stage_free[h], 1)
                sp.dma_start(k.edges[:, :, :].rearrange("p t c -> p (t c)"),
                             k.edges_d.rearrange("(p t) c -> p (t c)", p=128)).then_inc(reload, 16)
                sp.wait_ge(reload, 16)
                sp.wait_ge(xn_out, 16)
                sp.wait_ge(zeroed, 16 * fills)

            @block.gpsimd
            def _(g):
                ch = Chain(g, iotas)
                ch.mark(g.memset(k.edges[:, :, :], 0.0))
                ch.mark(g.memset(zero[:, :], 0.0))
                ch.link(g.memset(k.ones[:, :], 1.0))
                ch.mark(g.memset(xs[:, D:D + 1], 1.0))
                ch.mark(g.memset(k.x_all[:, T, :], 0.0))
                ch.mark(g.memset(k.xn_all[:, T, :], 0.0))
                ch.mark(g.iota(iota_i[:, :], pattern=[[1, 128]], base=0, channel_multiplier=0))
                ch.mark(g.iota(tix_i[:, :], pattern=[[1, ETP]], base=0, channel_multiplier=0))
                ch.mark(g.affine_select(out=k.ident[:, :], in_=k.ones[:, :], compare_op=ALU.is_equal, fill=0.0,
                                        base=0, pattern=[[-1, 128]], channel_multiplier=1))
                ch.mark(g.affine_select(out=k.tri[:, :], in_=k.ones[:, :], compare_op=ALU.is_gt, fill=0.0,
                                        base=0, pattern=[[1, 128]], channel_multiplier=-1))
                ch.link(g.affine_select(out=k.tri1[:, :], in_=k.ones[:, :], compare_op=ALU.is_ge, fill=0.0,
                                        base=0, pattern=[[1, 128]], channel_multiplier=-1))
                ch.mark(g.tensor_copy(k.iota[:, :], iota_i[:, :]))
                ch.link(g.tensor_copy(tix[:, :], tix_i[:, :]))
                g.memset(nconst[:, :], float(N)).then_inc(consts, 1)
                g.wait_ge(prefilled, 16)
                with g.Fori(0, T) as r:
                    for h in range(2):
                        g.wait_ge(staged[h], r * 2 + 2)
                        g.sem_inc(begun, 1)
                        for j in range(SH):
                            g.indirect_dma_start(
                                out=k.edges_d,
                                out_offset=bass.IndirectOffsetOnAxis(ap=idx_st[:, h, j:j + 1], axis=0),
                                in_=rec_st[:, h, j, :], in_offset=None).then_inc(scattered[h], 16)

            @block.scalar
            def _(s):
                for name in WEIGHTS:
                    ap = k.w[name]
                    s.dma_start(ap[tuple(slice(None) for _ in ap.shape)], a[name]).then_inc(w_in, 16)
                norm_root_scalar(s, k, var_ready, root_ready, 1)
                s.wait_ge(idx_ready, 1)
                one_ahead(s, kept, hot_act)
                with s.Fori(0, T) as r:
                    for h in range(2):
                        s.wait_ge(stage_free[h], r + 1)
                        col = bass.ds(r * EC_R + h * SH, SH)
                        s.activation(idx_st[:, h, :], pos[:, col], ACT.Copy).then_inc(staged[h], 1)
                        s.activation(rec_st[:, h, :, :], rec[:, col, :], ACT.Copy).then_inc(staged[h], 1)
                        j, n = BY_SCALAR[h], EC_R - 2 * SH
                        s.wait_ge(hot_act, 1 + r * 2 + h)
                        s.activation(away[:, :], tix[0:P, 0:ET], ACT.Abs, bias=neg_high[:, bass.ds(r * EC_R + 2 * SH + j, 1)])\
                            .then_inc(abs_made, 1)
                        s.wait_ge(placed, r * n + j + 1)
                        s.wait_ge(abs_made, r * 2 + h + 1)
                        s.activation(hot_t[j % HS][:, :], away[:, :], ACT.Relu, bias=k.ones[0:P, 0:1], scale=-1.0)\
                            .then_inc(hot_act, 1)
                    s.wait_ge(xs_ready, r + 1)
                    for rows in (k.xn, k.acc):
                        s.activation(rows[:, bass.ds(r, 1), :], xs[:, 0:D].unsqueeze(1), ACT.Copy).then_inc(kept, 1)
                s.wait_ge(kept, 1 + 2 * T)
                s.dma_start(k.xn_d.rearrange("(t p) c -> p t c", p=P), k.xn[:, :, :]).then_inc(xn_out, 16)

            @block.vector
            def _(v):
                ch = Chain(v, vec)
                ln = Chain(v, lnc)
                v.wait_ge(edges_in, 48)
                ch.mark(v.tensor_copy(src_f[:, :], src_i[:, :]))
                ch.mark(v.tensor_copy(rec[:, :, 0], dst_i[:, :]))
                ch.mark(v.tensor_copy(w_high[:, :], w_e[:, :]))
                ch.join()
                ch.mark(v.tensor_copy(rec[:, :, 2], w_high[:, :].bitcast(F32)))
                ch.mark(v.tensor_tensor(rec[:, :, 3], w_e[:, :], w_high[:, :].bitcast(F32), ALU.subtract))
                ch.link(v.tensor_scalar(bin_f[:, :], src_f[:, :], 1.0 / P, 0.5 / P - 0.5, ALU.mult, ALU.add))
                ch.link(v.tensor_scalar(bin_f[:, :], bin_f[:, :], ROUND, ROUND, ALU.add, ALU.subtract))
                ch.link(v.scalar_tensor_tensor(src_f[:, :], bin_f[:, :], -float(P), src_f[:, :], ALU.mult, ALU.add))
                ch.mark(v.tensor_scalar(rec[:, :, 1], src_f[:, :], 1.0, None, ALU.add))
                for b in range(T):
                    ch.mark(v.tensor_scalar(mask[:, b, :], bin_f[:, :], float(b), 0.0, ALU.is_equal, ALU.add,
                                            accum_out=cnt[:, b:b + 1]))
                ch.mark(v.memset(tmp[:, :], 0.0))
                ch.join()
                v.sem_inc(cnt_ready, 1)
                v.wait_ge(prefix, 2)
                ch.link(v.tensor_scalar(tot_i[:, :], pc[:, 32:32 + T], 127.0, None, ALU.add))
                ch.link(v.tensor_scalar(tot_i[:, :], tot_i[:, :], 7, None, ALU.logical_shift_right))
                ch.link(v.tensor_copy(tiles[:, :], tot_i[:, :]))
                v.wait_ge(iotas, IOTAS)
                ch.link(v.tensor_tensor_scan(tiles_to[:, :], k.ones[:, 0:T], tiles[:, :], 0.0, ALU.mult, ALU.add))
                ch.link(v.tensor_tensor(off[:, :], tiles_to[:, :], tiles[:, :], ALU.subtract))
                ch.link(v.tensor_scalar(off[:, :], off[:, :], 128.0, None, ALU.mult))
                ch.mark(v.tensor_tensor(off[0:P, :], off[0:P, :], pc[0:P, 0:T], ALU.add))
                ch.join()
                v.sem_inc(bin_steps, 1)
                def take(b):
                    v.wait_ge(scanned, b + 1)
                    if b:
                        v.wait_ge(taken, b)
                    v.copy_predicated(tmp[:, :], mask[:, b, :], run[:, b % 2, :]).then_inc(taken, 1)

                for b in range(T):
                    if b > 1:
                        v.wait_ge(taken, b - 1)
                    v.tensor_tensor_scan(run[:, b % 2, :], mask[:, b, :], mask[:, b, :], off[0:P, b:b + 1],
                                         ALU.add, ALU.max).then_inc(scanned, 1)
                    if b:
                        take(b - 1)
                take(T - 1)
                v.wait_ge(taken, T)
                ch.link(v.tensor_scalar(pos_i[:, :], tmp[:, :], -1.0, None, ALU.add))
                ch.mark(v.tensor_scalar(low_i[:, :], pos_i[:, :], 127, None, ALU.bitwise_and))
                ch.link(v.tensor_scalar(pos_i[:, :], pos_i[:, :], 7, None, ALU.logical_shift_right))
                ch.mark(v.tensor_copy(tmp[:, :], low_i[:, :]))
                ch.link(v.tensor_copy(high[:, :], pos_i[:, :]))
                ch.link(v.tensor_scalar(neg_high[:, :], high[:, :], -1.0, None, ALU.mult))
                v.scalar_tensor_tensor(pos[:, :], tmp[:, :], float(ETP), high[:, :], ALU.mult, ALU.add)\
                    .then_inc(idx_ready, 1)
                v.wait_ge(x_in, 16)
                for t in range(T):
                    ln.mark(v.bn_stats(k.stats[:, t, :], k.x[:, t, :]))
                ln.join()
                norm_scale_vector(nc, v, ln, k, var_ready, root_ready, 1)
                v.wait_ge(bin_mm, 1)
                ln.link(v.tensor_copy(ends_at[:, :], pc[0:T - 1, 64:65]))
                v.tensor_scalar(ended[:, :], tix[0:T - 1, :], ends_at[:, 0:1], None, ALU.is_ge).then_inc(bin_steps, 1)
                v.wait_ge(iotas, IOTAS)
                with v.Fori(0, T) as r:
                    one = bass.ds(r, 1)
                    v.wait_ge(kept, 1 + 2 * r)
                    v.wait_ge(gram_step, 1 + r)
                    v.tensor_scalar(xs[:, 0:D].unsqueeze(1), k.x[:, one, :], k.mean[:, one], k.rstd[:, one],
                                    ALU.subtract, ALU.mult).then_inc(xs_ready, 1)
                    for j in range(EC_R - 2 * SH):
                        col = bass.ds(r * EC_R + 2 * SH + j, 1)
                        v.wait_ge(placed, r * (EC_R - 2 * SH) + j + 1)
                        if j not in BY_SCALAR:
                            v.tensor_scalar(hot_t[j % HS][:, :], tix[0:P, 0:ET], high[:, col], None, ALU.is_equal)\
                                .then_inc(hot_made, 1)
                        v.scalar_tensor_tensor(hot_p[j % HS][:, :, :], k.iota[0:P, :].unsqueeze(1).broadcast_to([P, 4, 128]),
                                               tmp[:, col], rec[:, col, :].rearrange("p a c -> p (a c)").unsqueeze(2)
                                               .broadcast_to([P, 4, 128]), ALU.is_equal, ALU.mult).then_inc(hot_made, 1)
                v.wait_ge(bin_mm, 2)
                ln.mark(v.tensor_copy(k.tile_bin[:, :], pc[0:1, 0:ETP]))
                ln.mark(v.memset(KV[:, :, :], 0.0))
                v.wait_ge(gram_done, 1)
                for i in range(KD):
                    v.tensor_copy(G[:, i, :], pg[i][:, 0:D + 1]).then_inc(mix_copied, 1)
                v.tensor_copy(srow[:, :], psr[0:1, 0:D]).then_inc(mix_copied, 1)
                v.wait_ge(mixed, 1)
                for i in range(KD):
                    v.tensor_copy(U[:, i, :], pu[i][:, 0:D]).then_inc(mix_copied, 1)
                v.tensor_copy(Ul[:, :], psr[0:1, 0:D]).then_inc(mix_copied, 1)
                v.wait_ge(mixed, 2)
                ln.join()
                for h in range(HEADS):
                    i, q = h * HD // 128, h * HD % 128
                    v.tensor_scalar(KV[q:q + HD, i, h * HD:(h + 1) * HD], pu[i][q:q + HD, h * HD:(h + 1) * HD],
                                    1.0 / N, None, ALU.mult).then_inc(mix_copied, 1)
                v.wait_ge(mixed, 3)
                for i in range(KD):
                    v.tensor_copy(M2[:, i, :], pu[i][:, 0:D]).then_inc(mix_copied, 1)
                v.wait_ge(mixed, 4)
                for i in range(KD):
                    v.tensor_copy(k.R[:, i, :], pu[i][:, 0:D]).then_inc(mix_copied, 1)
                ln.link(v.tensor_tensor(k.r0[:, :], psr[0:1, 0:D], k.w["m0_bfc"][:, :], ALU.add))
                ln.link(v.tensor_tensor(k.r0[:, :], k.r0[:, :], k.w["g0_b2"][:, :], ALU.add))
                v.wait_ge(reload, 16)
                for i in range(4):
                    value = k.edges[:, 0:ET, i]
                    ln.mark(v.tensor_tensor(value, value, pS[i][:, 0:ET], ALU.add))
                ln.join()
                ln.mark(v.tensor_scalar(k.edges[:, 0:ET, 1], k.edges[:, 0:ET, 1], -1.0, None, ALU.add))
                ln.link(v.tensor_tensor(k.edges[:, 0:ET, 2], k.edges[:, 0:ET, 2], k.edges[:, 0:ET, 3], ALU.add))

            @block.tensor
            def _(pe):
                pe.wait_ge(cnt_ready, 1)
                pe.wait_ge(iotas, IOTAS)
                nc.tensor.matmul(pc[0:P, 0:T], k.tri[0:P, 0:P], cnt[:, :], start=True, stop=True).then_inc(prefix, 1)
                nc.tensor.matmul(pc[:, 32:32 + T], k.ones[0:P, :], cnt[:, :], start=True, stop=True).then_inc(prefix, 1)
                pe.wait_ge(bin_steps, 1)
                nc.tensor.matmul(pc[0:T - 1, 64:65], tiles_to[0:1, 0:T - 1], k.ones[0:1, 0:1], start=True, stop=True)\
                    .then_inc(bin_mm, 1)
                pe.wait_ge(bin_steps, 2)
                nc.tensor.matmul(pc[0:1, 0:ETP], k.ones[0:T - 1, 0:1], ended[:, :], start=True, stop=True)\
                    .then_inc(bin_mm, 1)
                pe.sem_inc(placed, HS)
                one_ahead(pe, gram_step)

                def edge(start, stop):
                    for i in range(4):
                        nc.tensor.matmul(pS[i][:, 0:ET], k.ones[0:1, :], zero[0:1, 0:ET], start=start, stop=stop)
                    for i in range(KD):
                        nc.tensor.matmul(pg[i][:, 0:D + 1], k.ones[0:1, :], zero[0:1, 0:D + 1], start=start, stop=stop)
                    return nc.tensor.matmul(psr[0:1, 0:D], k.ones[0:1, 0:1], zero[0:1, 0:D], start=start, stop=stop)

                edge(True, False)
                with pe.Fori(0, T) as r:
                    n = EC_R - 2 * SH
                    for j in range(n):
                        pe.wait_ge(hot_made, r * (2 * n - 2) + 2 * j + 2 - sum(c <= j for c in BY_SCALAR))
                        if j in BY_SCALAR:
                            pe.wait_ge(hot_act, 1 + r * 2 + BY_SCALAR.index(j) + 1)
                        for i in range(4):
                            last = nc.tensor.matmul(pS[i][:, 0:ET], hot_p[j % HS][:, i, :], hot_t[j % HS][:, :],
                                                    start=False, stop=False)
                        last.then_inc(placed, 1)
                        if j == n // 2:
                            pe.wait_ge(xs_ready, r + 1)
                            for i in range(KD):
                                nc.tensor.matmul(pg[i][:, 0:D + 1], xs[:, i * 128:(i + 1) * 128], xs[:, :],
                                                 start=False, stop=False)
                            nc.tensor.matmul(psr[0:1, 0:D], k.ones[0:P, 0:1], xs[:, 0:D], start=False, stop=False)\
                                .then_inc(gram_step, 1)
                edge(False, True).then_inc(gram_done, 1)
                pe.wait_ge(w_in, 16 * len(WEIGHTS))
                pe.wait_ge(mix_copied, KD + 1)
                pe.wait_ge(consts, 1)
                w = k.w
                for i in range(KD):
                    for j in range(KD):
                        nc.tensor.matmul(pu[i][:, 0:D], G[:, j, i * 128:(i + 1) * 128], w["m0_WvT"][:, j, :],
                                         start=j == 0, stop=False)
                    nc.tensor.matmul(pu[i][:, 0:D], srow[:, i * 128:(i + 1) * 128], w["m0_bv"][:, :],
                                     start=False, stop=True)
                for j in range(KD):
                    nc.tensor.matmul(psr[0:1, 0:D], G[:, j, D:D + 1], w["m0_WvT"][:, j, :], start=j == 0, stop=False)
                nc.tensor.matmul(psr[0:1, 0:D], nconst[:, :], w["m0_bv"][:, :], start=False, stop=True)\
                    .then_inc(mixed, 1)
                pe.wait_ge(mix_copied, 2 * (KD + 1))
                for i in range(KD):
                    for j in range(KD):
                        nc.tensor.matmul(pu[i][:, 0:D], U[:, j, i * 128:(i + 1) * 128], w["m0_WkT"][:, j, :],
                                         start=j == 0, stop=False)
                    last = nc.tensor.matmul(pu[i][:, 0:D], Ul[:, i * 128:(i + 1) * 128], w["m0_bk"][:, :],
                                            start=False, stop=True)
                last.then_inc(mixed, 1)
                n = 2 * (KD + 1) + HEADS
                pe.wait_ge(mix_copied, n)
                for i in range(KD):
                    for j in range(KD):
                        last = nc.tensor.matmul(pu[i][:, 0:D], KV[:, j, i * 128:(i + 1) * 128],
                                                w["m0_WfcT"][:, j, :], start=j == 0, stop=j == KD - 1)
                last.then_inc(mixed, 1)
                pe.wait_ge(mix_copied, n + KD)
                for i in range(KD):
                    for j in range(KD):
                        nc.tensor.matmul(pu[i][:, 0:D], w["m0_Wq"][:, j, i * 128:(i + 1) * 128], M2[:, j, :],
                                         start=j == 0, stop=j == KD - 1)
                for j in range(KD):
                    last = nc.tensor.matmul(psr[0:1, 0:D], w["m0_bqc"][:, j:j + 1], M2[:, j, :],
                                            start=j == 0, stop=j == KD - 1)
                last.then_inc(mixed, 1)


def bins_of(nc, k, engine, r, h):
    _, bins = nc.values_load_multi_w_load_instructions(
        k.tile_bin[0:1, bass.ds(r * EB + h * (EB // 2), EB // 2)], engines=(engine,), min_val=0, max_val=T - 1,
        skip_runtime_bounds_check_because="a count of at most T - 1 node tiles")
    return bins


def aggregate(nc, a, k, layer):
    width = (D, XJW)[layer]
    table = (k.xn_d, k.xj_d)[layer]
    sums = k.x_all if layer else k.acc
    H, QT = EB // 2, EB // 4
    ROUNDS = ET // EB
    AHEAD = 2
    with ExitStack() as c:
        def sem(name):
            return k.sem(nc, f"{name}{layer}")

        rows = c.enter_context(nc.sbuf_tensor(f"edge_rows{layer}", [128, EB, width], F32))
        hot = c.enter_context(nc.sbuf_tensor(f"one_hot{layer}", [128, EB, P], F32))
        att = c.enter_context(nc.sbuf_tensor(f"att{layer}", [128, EB, P], F32)) if layer else None
        idx = c.enter_context(nc.sbuf_tensor(f"gather_idx{layer}", [128, 4, QT], I32))
        part = [c.enter_context(nc.psum_tensor(f"p_part{layer}_{i}", [128, 512], F32)) for i in range(4)]
        staged = [sem(f"idx_staged{q}_") for q in range(4)]
        landed, past = k.landed, layer * (ET // EB) * 16
        begun = sem("gather_begun")
        att_ready, hot_ready, summed, added = sem("att_ready"), sem("hot_ready"), sem("summed"), sem("added")
        w = k.w
        pQ, pM, pY = (c.enter_context(nc.psum_tensor(f"{n}{layer}", [128, 512], F32)) for n in ("p_q", "p_mixed", "p_proj"))
        if layer == 0:
            xs = c.enter_context(nc.sbuf_tensor("mix_rows", [P, D], F32))
            xsT = c.enter_context(nc.sbuf_tensor("mix_rowsT", [128, KD, P], F32))
            xs_in, turned, xsT_ready, y_mm, y_added = sem("xs_in"), sem("turned"), sem("xsT_ready"), sem("y_mm"), sem("y_added")
        else:
            low, q, inv, mix = (c.enter_context(nc.sbuf_tensor(n, [128, KD * P], F32))
                                for n in ("q_low", "q_T", "mix_inv", "mix_T"))
            q_mm, q_low, q_exp, q_ready = sem("q_mm"), sem("q_low"), sem("q_exp"), sem("q_ready")
            mix_mm, inv_ready, mix_ready = sem("mix_mm"), sem("inv_ready"), sem("mix_ready")
            y_mm, y_added = sem("y_mm"), sem("y_added")

        with nc.Block() as block:
            @block.gpsimd
            def _(g):
                with g.Fori(0, ROUNDS) as r:
                    for s in range(EB):
                        if s % QT == 0:
                            g.wait_ge(staged[s // QT], r + 1)
                            g.sem_inc(begun, 1)
                        g.indirect_dma_start(
                            out=rows[:, s, :], out_offset=None, in_=table,
                            in_offset=bass.IndirectOffsetOnAxis(ap=idx[:, s // QT, s % QT:s % QT + 1], axis=0))\
                            .then_inc(landed[s], 16)

            @block.scalar
            def _(sc):
                def stage(tile, quarter):
                    sc.activation(idx[:, quarter, :], k.edges[:, bass.ds(tile, QT), 0], ACT.Copy)\
                        .then_inc(staged[quarter], 1)

                for quarter in range(3):
                    stage(quarter * QT, quarter)
                with sc.Fori(0, ROUNDS) as r:
                    for s in range(EB):
                        if layer:
                            if s % H == 0:
                                bins = bins_of(nc, k, mybir.EngineType.Activation, r, s // H)
                            sc.wait_ge(landed[s], past + r * 16 + 16)
                            sc.activation(att[:, s:s + 1, :], k.a1[:, bass.ds(bins[s % H], 1), :], ACT.Sigmoid,
                                          bias=rows[:, s, D:D + 1]).then_inc(att_ready, 1)
                        if s == 2:
                            sc.wait_ge(summed, 1 + r * EB)
                            stage(r * EB + 3 * QT, 3)
                        if s in (6, 10, 14):
                            quarter = s // QT - 1
                            sc.wait_ge(summed, 1 + r * EB + (quarter + 1) * QT)
                            stage(r * EB + EB + quarter * QT, quarter)
                        if layer == 0 and s == 0:
                            sc.wait_ge(turned, 1 + r)
                            sc.activation(xs[:, :].unsqueeze(1), k.xn_all[:, bass.ds(r, 1), :], ACT.Copy).then_inc(xs_in, 1)
                        if layer == 0 and s == 6:
                            sc.wait_ge(turned, 1 + r + 1)
                            sc.wait_ge(y_mm, 1 + r)
                            sc.activation(xsT[:, :, :], pQ[:, 0:KD * P].rearrange("p (i n) -> p i n", i=KD), ACT.Copy)\
                                .then_inc(xsT_ready, 1)
                        if layer and s == 5:
                            sc.wait_ge(q_mm, r + 1)
                            sc.activation(low[:, :], pQ[:, 0:KD * P], ACT.Relu, scale=-1.0).then_inc(q_low, 1)
                            sc.wait_ge(q_low, r + 1)
                            sc.wait_ge(mix_mm, 1 + r)
                            sc.activation(q[:, :], low[:, :], ACT.Exp, scale=-1.0).then_inc(q_exp, 1)

            @block.vector
            def _(v):
                one_ahead(v, added)
                one_ahead(v, y_added)
                if layer:
                    one_ahead(v, q_ready, mix_ready)

                def one_hot(r, s):
                    e = k.edges[:, bass.ds(r * EB + s, 1), :]
                    if layer:
                        v.wait_ge(att_ready, r * EB + s + 1)
                        v.scalar_tensor_tensor(hot[:, s, :], k.iota[:, 0:P], e[:, 0, 1:2], att[:, s, :],
                                               ALU.is_equal, ALU.mult).then_inc(hot_ready, 1)
                    else:
                        v.tensor_scalar(hot[:, s, :], k.iota[:, 0:P], e[:, 0, 1:2], e[:, 0, 2:3],
                                        ALU.is_equal, ALU.mult).then_inc(hot_ready, 1)

                def mix_step(r, s):
                    if s == 7:
                        v.wait_ge(q_exp, r + 1)
                        v.scalar_tensor_tensor(q[:, :], pQ[:, 0:KD * P], 0.0, q[:, :], ALU.max, ALU.add)\
                            .then_inc(q_ready, 1)
                    if s == 10:
                        v.wait_ge(mix_mm, 1 + r + 1)
                        v.tensor_scalar(inv[:, :], pM[:, KD * P:2 * KD * P], 1e-6, None, ALU.max).then_inc(inv_ready, 1)
                    if s == 11:
                        v.wait_ge(inv_ready, r * 2 + 1)
                        v.reciprocal(inv[:, :], inv[:, :]).then_inc(inv_ready, 1)
                    if s == 12:
                        v.wait_ge(inv_ready, r * 2 + 2)
                        v.tensor_tensor(mix[:, :], pM[:, 0:KD * P], inv[:, :], ALU.mult).then_inc(mix_ready, 1)
                    if s == 15:
                        dst = sums[:, bass.ds(r, 1), :]
                        v.wait_ge(y_mm, r + 1)
                        v.wait_ge(added, 1 + r * EB + s)
                        v.tensor_tensor(dst, dst, pY[0:P, 0:D].unsqueeze(1), ALU.add).then_inc(y_added, 1)
                        v.wait_ge(y_added, 1 + r + 1)

                def tiles_of_round(r, more):
                    for s in range(EB):
                        if s % H == 0:
                            bins = bins_of(nc, k, mybir.EngineType.DVE, r, s // H)
                        if s + AHEAD < EB:
                            one_hot(r, s + AHEAD)
                        elif more:
                            one_hot(r + 1, s + AHEAD - EB)
                        if layer:
                            mix_step(r, s)
                        elif s == 15:
                            x = k.x_all[:, bass.ds(r, 1), :]
                            v.wait_ge(y_mm, 1 + r + 1)
                            v.tensor_tensor(x, x, pY[0:P, 0:D].unsqueeze(1), ALU.add).then_inc(y_added, 1)
                        dst = sums[:, bass.ds(bins[s % H], 1), :]
                        v.wait_ge(summed, 1 + r * EB + s + 1)
                        v.wait_ge(added, 1 + r * EB + s)
                        v.tensor_tensor(dst, dst, part[s % 4][0:P, 0:D].unsqueeze(1), ALU.add).then_inc(added, 1)

                for s in range(AHEAD):
                    one_hot(0, s)
                with v.Fori(0, ROUNDS - 1) as r:
                    tiles_of_round(r, True)
                tiles_of_round(ROUNDS - 1, False)

            @block.tensor
            def _(pe):
                one_ahead(pe, summed)
                if layer == 0:
                    one_ahead(pe, turned, y_mm)
                else:
                    one_ahead(pe, mix_mm)

                def mix0_step(r, s):
                    if s == 2:
                        pe.wait_ge(xs_in, r + 1)
                        for i in range(KD):
                            last = nc.tensor.transpose(pQ[:, i * P:(i + 1) * P], xs[:, i * 128:(i + 1) * 128],
                                                       k.ident[0:P, 0:P])
                        last.then_inc(turned, 1)
                    if s == 10:
                        pe.wait_ge(xsT_ready, r + 1)
                        pe.wait_ge(y_added, 1 + r)
                        for i in range(KD):
                            nc.tensor.matmul(pY[0:P, 0:D], xsT[:, i, :], k.R[:, i, :], start=i == 0, stop=False)
                        nc.tensor.matmul(pY[0:P, 0:D], k.ones[0:1, 0:P], k.r0[:, :], start=False, stop=True)\
                            .then_inc(y_mm, 1)

                def mix1_step(r, s):
                    if s == 0:
                        pe.wait_ge(q_ready, 1 + r)
                        for o in range(KD):
                            for i in range(KD):
                                last = nc.tensor.matmul(pQ[:, o * P:(o + 1) * P],
                                                        w["m1_WqT"][:, i, o * 128:(o + 1) * 128],
                                                        k.xnT[:, i, bass.ds(r * P, P)], start=i == 0, stop=i == KD - 1)
                        last.then_inc(q_mm, 1)
                    if s == 9:
                        pe.wait_ge(q_ready, 1 + r + 1)
                        pe.wait_ge(mix_ready, 1 + r)
                        for j in range(2):
                            for i in range(KD):
                                last = nc.tensor.matmul(pM[:, (j * KD + i) * P:(j * KD + i + 1) * P],
                                                        k.ctx[:, i, j, :], q[:, i * P:(i + 1) * P],
                                                        start=True, stop=True)
                        last.then_inc(mix_mm, 1)
                    if s == 15:
                        pe.wait_ge(mix_ready, 1 + r + 1)
                        pe.wait_ge(y_added, 1 + r)
                        for i in range(KD):
                            last = nc.tensor.matmul(pY[0:P, 0:D], mix[:, i * P:(i + 1) * P], w["m1_WpT"][:, i, :],
                                                    start=i == 0, stop=i == KD - 1)
                        last.then_inc(y_mm, 1)

                with pe.Fori(0, ROUNDS) as r:
                    for s in range(EB):
                        (mix0_step, mix1_step)[layer](r, s)
                        pe.wait_ge(landed[s], past + r * 16 + 16)
                        pe.wait_ge(hot_ready, r * EB + s + 1)
                        pe.wait_ge(added, 1 + r * EB + max(s - 3, 0))
                        nc.tensor.matmul(part[s % 4][0:P, 0:D], hot[:, s, :], rows[:, s, 0:D],
                                         start=True, stop=True).then_inc(summed, 1)


def gin(nc, a, k):
    KH = F0 // 128
    w = k.w
    with ExitStack() as c:
        def sb(name, shape):
            return c.enter_context(nc.sbuf_tensor(name, shape, F32))

        def sem(name):
            return k.sem(nc, name)

        def ps(name):
            return c.enter_context(nc.psum_tensor(name, [128, 512], F32))

        hs, xT, hT = sb("gin_rows", [P, GT, D]), sb("gin_T", [128, GT, KD, P]), sb("gin_hidden", [128, GT, KH, P])
        pT, pH, pO = [ps(f"p_gT{i}") for i in range(2)], [ps(f"p_gH{i}") for i in range(2)], [ps(f"p_gO{i}") for i in range(2)]
        rows_in, turned, copied = sem("g_rows_in"), sem("g_turned"), sem("g_copied")
        up, relued, down, added = sem("g_up"), sem("g_relued"), sem("g_down"), sem("g_added")

        with nc.Block() as block:
            @block.scalar
            def _(s):
                one_ahead(s, relued)
                with s.Fori(0, GR) as r:
                    s.wait_ge(turned, 1 + r * GT)
                    for t in range(GT):
                        s.activation(hs[:, t:t + 1, :], k.acc[:, bass.ds(r * GT + t, 1), :], ACT.Copy).then_inc(rows_in, 1)
                    s.wait_ge(down, 1 + r * GT)
                    for t in range(GT):
                        s.wait_ge(up, r * GT + t + 1)
                        for f in range(KH):
                            s.activation(hT[:, t, f, :], pH[t % 2][:, f * P:(f + 1) * P], ACT.Relu,
                                         bias=w["g0_b1"][:, f:f + 1]).then_inc(relued, 1)

            @block.vector
            def _(v):
                one_ahead(v, copied, added)

                def copy(r, t):
                    v.wait_ge(turned, 1 + r * GT + t + 1)
                    v.tensor_copy(xT[:, t, :, :], pT[t % 2][:, 0:KD * P].rearrange("p (a b) -> p a b", a=KD))\
                        .then_inc(copied, 1)

                def add(r, t):
                    x = k.x[:, bass.ds(r * GT + t, 1), :]
                    v.wait_ge(down, 1 + r * GT + t + 1)
                    v.tensor_tensor(x, x, pO[t % 2][0:P, 0:D].unsqueeze(1), ALU.add).then_inc(added, 1)
                    v.wait_ge(added, 1 + r * GT + t + 1)
                    v.bn_stats(k.stats[:, bass.ds(r * GT + t, 1), :], x)

                with v.Fori(0, GR) as r:
                    copy(r, 0)
                    copy(r, 1)
                    for t in range(GT):
                        if t + 2 < GT:
                            copy(r, t + 2)
                        add(r, t)

            @block.tensor
            def _(pe):
                one_ahead(pe, turned, down)

                def turn(r, t):
                    pe.wait_ge(rows_in, r * GT + t + 1)
                    pe.wait_ge(copied, 1 + r * GT + max(t - 1, 0))
                    for i in range(KD):
                        last = nc.tensor.transpose(pT[t % 2][:, i * P:(i + 1) * P], hs[:, t, i * 128:(i + 1) * 128],
                                                   k.ident[0:P, 0:P])
                    last.then_inc(turned, 1)

                def first(r, t):
                    pe.wait_ge(copied, 1 + r * GT + t + 1)
                    pe.wait_ge(relued, 1 + (r * GT + max(t - 1, 0)) * KH)
                    for f in range(KH):
                        for i in range(KD):
                            last = nc.tensor.matmul(pH[t % 2][:, f * P:(f + 1) * P],
                                                    w["g0_W1"][:, i, f * 128:(f + 1) * 128], xT[:, t, i, :],
                                                    start=i == 0, stop=i == KD - 1)
                    last.then_inc(up, 1)

                def second(r, t):
                    pe.wait_ge(relued, 1 + (r * GT + t + 1) * KH)
                    pe.wait_ge(added, 1 + r * GT + max(t - 1, 0))
                    for f in range(KH):
                        last = nc.tensor.matmul(pO[t % 2][0:P, 0:D], hT[:, t, f, :], w["g0_W2"][:, f, :],
                                                start=f == 0, stop=f == KH - 1)
                    last.then_inc(down, 1)

                with pe.Fori(0, GR) as r:
                    turn(r, 0)
                    for t in range(GT):
                        if t + 1 < GT:
                            turn(r, t + 1)
                        first(r, t)
                        if t:
                            second(r, t - 1)
                    second(r, GT - 1)


def first_max(v, ch, lg, mx, rev, oh, at):
    ch.link(v.tensor_reduce(mx, lg, AX.X, ALU.max))
    ch.link(v.tensor_tensor(oh, lg, mx.unsqueeze(2).broadcast_to([P, T, X]), ALU.is_equal))
    ch.link(v.tensor_tensor(oh, oh, rev, ALU.mult))
    ch.link(v.tensor_reduce(at, oh, AX.X, ALU.max))
    ch.link(v.tensor_tensor(oh, rev, at.unsqueeze(2).broadcast_to([P, T, X]), ALU.is_equal))


def route(nc, a, k, layer):
    w = k.w
    picks = layer + 1
    gw, gb = w[f"f{layer}_gw"], w[f"f{layer}_gb"]
    with ExitStack() as c:
        def sb(name, shape, dt=F32):
            return c.enter_context(nc.sbuf_tensor(f"{name}_r{layer}", shape, dt))

        def sem(name):
            return k.sem(nc, f"{name}_r{layer}")

        def ps(name):
            return c.enter_context(nc.psum_tensor(f"{name}_r{layer}", [128, 512], F32))

        xs, xT = sb("rows", [P, GT, D]), sb("rowsT", [128, GT, KD, P])
        lg, lg2, rev, tmp = sb("logits", [P, T, X]), sb("logits2", [P, T, X]), sb("rev", [P, T, X]), sb("tmp", [P, T, X])
        oh = [sb(f"onehot{i}", [P, T, X]) for i in range(2)]
        both, tot, upto = sb("both", [P, T, X]), sb("tot", [P, T, X]), sb("upto", [P, T, X])
        mx = [sb(f"mx{i}", [P, T]) for i in range(2)]
        at = [sb(f"at{i}", [P, T]) for i in range(2)]
        e2, inv, pos, keep, node = sb("e2", [P, T]), sb("inv", [P, T]), sb("pos", [P, T]), sb("keep", [P, T]), sb("node", [P, T])
        ch_i, chn, cto = sb("chunks_i", [P, X], I32), sb("chunks", [P, X]), sb("chunks_to", [P, X])
        cx, cix, cix_i = sb("cx", [1, NCH + 2]), sb("cix", [1, NCH + 2]), sb("cix_i", [1, NCH + 2], I32)
        rev_i, node_i = sb("rev_i", [P, T, X], I32), sb("node_i", [P, T], I32)
        pT, pL, pC, pN = [ps(f"p_T{i}") for i in range(2)], ps("p_L"), ps("p_cum"), ps("p_tot")
        normed, turned, copied, kept_x, logits = sem("normed"), sem("turned"), sem("copied"), sem("kept_x"), sem("logits")
        vec, var_ready, root_ready, iotas = sem("vec"), sem("var"), sem("root"), sem("iotas")
        e_in, e_out, hot_ready, cum_ready = sem("e_in"), sem("e_out"), sem("hot_ready"), sem("cum_ready")
        slots_ready, scattered = sem("slots_ready"), sem("scattered")
        k.w_in = [[sem(f"w{p + 1}_in{h}") for h in range(2)] for p in range(2)]

        with nc.Block() as block:
            @block.sync
            def _(sp):
                sp.wait_ge(slots_ready, 1)
                for slot, (n, p) in enumerate(((0, 0), (1, 0), (0, 1))):
                    e = sp.value_load(k.chunk_x[0:1, n:n + 1], min_val=0, max_val=X - 1)
                    sp.dma_start(k.w_early[:, slot, :], a[f"f{layer}_w"][bass.ds(e, 1), p, :, :]
                                 .rearrange("e p c -> p (e c)")).then_inc(k.w_in[p][n], 16)

            @block.gpsimd
            def _(g):
                g.iota(rev_i[:, :, :], pattern=[[0, T], [-1, X]], base=X, channel_multiplier=0).then_inc(iotas, 1)
                g.iota(node_i[:, :], pattern=[[P, T]], base=X * ROW0 + CH, channel_multiplier=1).then_inc(iotas, 1)
                g.iota(cix_i[:, :], pattern=[[1, NCH + 2]], base=0, channel_multiplier=0).then_inc(iotas, 1)
                g.wait_ge(slots_ready, 1)
                for t in range(T):
                    for i in range(picks):
                        g.indirect_dma_start(
                            out=k.buf[layer], out_offset=bass.IndirectOffsetOnAxis(ap=k.slots[:, i, t:t + 1], axis=0),
                            in_=k.xn[:, t, :], in_offset=None).then_inc(scattered, 16)
                g.wait_ge(scattered, 16 * T * picks)

            @block.scalar
            def _(s):
                slots_free(s, GT, kept_x)
                slots_free(s, 2, copied)
                norm_root_scalar(s, k, var_ready, root_ready, 1)
                with s.Fori(0, GR) as r:
                    for t in range(GT):
                        s.wait_ge(turned, r * GT + t + 1)
                        s.wait_ge(logits, r * GT + t + 1)
                        s.activation(xT[:, t, :, :], pT[t % 2][:, 0:KD * P].rearrange("p (a b) -> p a b", a=KD),
                                     ACT.Copy).then_inc(copied, 1)
                        s.activation(k.xn[:, bass.ds(r * GT + t, 1), :], xs[:, t:t + 1, :], ACT.Copy)\
                            .then_inc(kept_x, 1)
                s.wait_ge(e_in, 1)
                if layer == 0:
                    s.activation(tmp[:, :, :], tmp[:, :, :], ACT.Exp).then_inc(e_out, 1)
                else:
                    s.activation(e2[:, :], e2[:, :], ACT.Exp).then_inc(e_out, 1)

            @block.tensor
            def _(pe):
                slots_free(pe, GT, logits)

                def turn(m, t):
                    pe.wait_ge(normed, m + 1)
                    pe.wait_ge(copied, m + 1 + (t == 0))
                    for i in range(KD):
                        last = nc.tensor.transpose(pT[t % 2][:, i * P:(i + 1) * P],
                                                   xs[:, t, i * 128:(i + 1) * 128], k.ident[0:P, 0:P])
                    last.then_inc(turned, 1)

                def gate(m, t):
                    pe.wait_ge(copied, 2 + m + 1)
                    for i in range(KD):
                        last = nc.tensor.matmul(pL[0:P, bass.ds(m * X, X)], xT[:, t, i, :], gw[:, i, :],
                                                start=i == 0, stop=i == KD - 1)
                    last.then_inc(logits, 1)

                with pe.Fori(0, GR) as r:
                    turn(r * GT, 0)
                    for t in range(GT):
                        if t + 1 < GT:
                            turn(r * GT + t + 1, t + 1)
                        gate(r * GT + t, t)
                pe.wait_ge(hot_ready, 1)
                hot = both[:, :, :].rearrange("p t x -> p (t x)")
                nc.tensor.matmul(pC[0:P, 0:T * X], k.tri1[0:P, 0:P], hot, start=True, stop=True)
                nc.tensor.matmul(pN[0:P, 0:T * X], k.ones[0:P, 0:P], hot, start=True, stop=True).then_inc(cum_ready, 1)

            @block.vector
            def _(v):
                ch = Chain(v, vec)
                if layer:
                    for t in range(T):
                        ch.mark(v.bn_stats(k.stats[:, t, :], k.x[:, t, :]))
                    ch.join()
                norm_scale_vector(nc, v, ch, k, var_ready, root_ready, 1)
                with v.Fori(0, GR) as r:
                    for t in range(GT):
                        v.wait_ge(kept_x, r * GT + t + 1)
                        one = bass.ds(r * GT + t, 1)
                        v.tensor_scalar(xs[:, t:t + 1, :], k.x[:, one, :], k.mean[:, one], k.rstd[:, one],
                                        ALU.subtract, ALU.mult).then_inc(normed, 1)
                v.wait_ge(iotas, 3)
                ch.mark(v.tensor_copy(rev[:, :, :], rev_i[:, :, :]))
                ch.mark(v.tensor_copy(node[:, :], node_i[:, :]))
                ch.mark(v.tensor_copy(cix[:, :], cix_i[:, :]))
                v.wait_ge(logits, GT + T)
                view = "p (t x) -> p t x"
                ch.link(v.tensor_tensor(lg[:, :, :], pL[0:P, 0:T * X].rearrange(view, x=X), gb[0:P, :, :], ALU.add))
                first_max(v, ch, lg[:, :, :], mx[0][:, :], rev[:, :, :], oh[0][:, :, :], at[0][:, :])
                if layer == 0:
                    v.tensor_tensor(tmp[:, :, :], lg[:, :, :], mx[0][:, :].unsqueeze(2).broadcast_to([P, T, X]),
                                    ALU.subtract).then_inc(e_in, 1)
                    v.tensor_copy(both[:, :, :], oh[0][:, :, :]).then_inc(hot_ready, 1)
                    v.wait_ge(e_out, 1)
                    ch.link(v.tensor_reduce(inv[:, :], tmp[:, :, :], AX.X, ALU.add))
                    ch.link(v.reciprocal(inv[:, :], inv[:, :]))
                else:
                    ch.link(v.scalar_tensor_tensor(lg2[:, :, :], oh[0][:, :, :], -BIG, lg[:, :, :], ALU.mult, ALU.add))
                    first_max(v, ch, lg2[:, :, :], mx[1][:, :], rev[:, :, :], oh[1][:, :, :], at[1][:, :])
                    v.tensor_tensor(both[:, :, :], oh[0][:, :, :], oh[1][:, :, :], ALU.add).then_inc(hot_ready, 1)
                    v.tensor_tensor(e2[:, :], mx[1][:, :], mx[0][:, :], ALU.subtract).then_inc(e_in, 1)
                    v.wait_ge(e_out, 1)
                    ch.link(v.tensor_scalar(inv[:, :], e2[:, :], 1.0, None, ALU.add))
                    ch.link(v.reciprocal(k.gate[:, 0, :], inv[:, :]))
                    ch.mark(v.tensor_tensor(k.gate[:, 1, :], k.gate[:, 0, :], e2[:, :], ALU.mult))
                v.wait_ge(cum_ready, 1)
                ch.link(v.tensor_copy(tot[:, :, :], pN[0:P, 0:T * X].rearrange(view, x=X)))
                for e in range(X):
                    ch.mark(v.tensor_tensor_scan(upto[:, :, e], k.ones[0:P, 0:T], tot[:, :, e], 0.0, ALU.mult, ALU.add))
                ch.join()
                ch.link(v.tensor_tensor(tot[:, :, :], upto[:, :, :], tot[:, :, :], ALU.subtract))
                ch.link(v.scalar_tensor_tensor(tot[:, :, :], tot[:, :, :], -1.0,
                                               pC[0:P, 0:T * X].rearrange(view, x=X), ALU.add, ALU.add))
                if layer == 0:
                    ch.link(v.tensor_tensor(tot[:, :, :], tot[:, :, :], oh[0][:, :, :], ALU.mult))
                    ch.link(v.tensor_reduce(pos[:, :], tot[:, :, :], AX.X, ALU.add))
                    ch.link(v.tensor_scalar(keep[:, :], pos[:, :], float(CAP0), None, ALU.is_lt))
                    ch.mark(v.tensor_tensor(k.gate[:, 0, :], inv[:, :], keep[:, :], ALU.mult))
                    ch.link(v.tensor_scalar(at[1][:, :], at[0][:, :], -float(ROW0), float(X * ROW0), ALU.mult, ALU.add))
                    ch.link(v.scalar_tensor_tensor(mx[1][:, :], pos[:, :], float(CAP0 - 1), at[1][:, :], ALU.min, ALU.add))
                    ch.mark(v.tensor_copy(k.back[:, 0, :], mx[1][:, :]))
                    ch.link(v.tensor_scalar(cx[:, :], cix[:, :], float(CH) / ROW0, 0.25 * CH / ROW0 - 0.5, ALU.mult, ALU.add))
                    ch.link(v.tensor_scalar(cx[:, :], cx[:, :], ROUND, ROUND, ALU.add, ALU.subtract))
                    ch.link(v.tensor_scalar(k.chunk_x[:, :], cx[:, :], float(X - 1), None, ALU.min))
                    ch.link(v.tensor_tensor(mx[0][:, :], mx[1][:, :], node[:, :], ALU.subtract))
                    ch.link(v.tensor_tensor(mx[0][:, :], mx[0][:, :], keep[:, :], ALU.mult))
                    ch.link(v.tensor_tensor(mx[0][:, :], mx[0][:, :], node[:, :], ALU.add))
                    v.tensor_copy(k.slots[:, 0, :], mx[0][:, :]).then_inc(slots_ready, 1)
                else:
                    ch.link(v.tensor_scalar(ch_i[:, :], upto[:, T - 1, :], float(CH - 1), None, ALU.add))
                    ch.link(v.tensor_scalar(ch_i[:, :], ch_i[:, :], CH.bit_length() - 1, None, ALU.logical_shift_right))
                    ch.link(v.tensor_copy(chn[:, :], ch_i[:, :]))
                    ch.link(v.tensor_tensor_scan(cto[:, :], k.ones[0:P, 0:X], chn[:, :], 0.0, ALU.mult, ALU.add))
                    ch.link(v.tensor_tensor(chn[:, :], cto[:, :], chn[:, :], ALU.subtract))
                    ch.link(v.tensor_scalar(chn[:, :], chn[:, :], float(CH), None, ALU.mult))
                    ch.link(v.tensor_tensor(tot[:, :, :], tot[:, :, :],
                                            chn[:, :].unsqueeze(1).broadcast_to([P, T, X]), ALU.add))
                    for i in range(2):
                        ch.link(v.tensor_tensor(tmp[:, :, :], tot[:, :, :], oh[i][:, :, :], ALU.mult))
                        ch.link(v.tensor_reduce(pos[:, :], tmp[:, :, :], AX.X, ALU.add))
                        ch.mark(v.tensor_copy(k.back[:, i, :], pos[:, :]))
                        ch.link(v.tensor_copy(k.slots[:, i, :], pos[:, :]))
                    ch.link(v.tensor_scalar(cx[:, :], cix[:, :], cto[0:1, 0:1], None, ALU.is_ge))
                    for e in range(1, X - 1):
                        ch.link(v.scalar_tensor_tensor(cx[:, :], cix[:, :], cto[0:1, e:e + 1], cx[:, :], ALU.is_ge, ALU.add))
                    v.tensor_copy(k.chunk_x[:, :], cx[:, :]).then_inc(slots_ready, 1)


def experts(nc, a, k, layer):
    chunks = (CHUNKS0, NCH)[layer]
    nt, pairs = CH // 128, KF // 2
    act = (ACT.Relu, ACT.Gelu)[layer]
    buf, ybuf = k.buf[layer], k.ybuf[layer]
    aw, ab = a[f"f{layer}_w"], a[f"f{layer}_b"]
    with ExitStack() as c:
        def sb(name, shape, dt=F32):
            return c.enter_context(nc.sbuf_tensor(f"{name}_e{layer}", shape, dt))

        def sem(name):
            return k.sem(nc, f"{name}_e{layer}")

        def ps(name):
            return c.enter_context(nc.psum_tensor(f"{name}_e{layer}", [128, 512], F32))

        raw = [[k.w_early[:, 0, :], k.w_early[:, 1, :]], [k.w_early[:, 2, :], sb("w2_raw1", [128, PK])[:, :]]]
        hi = [[sb(f"w{p + 1}_hi{h}", [128, PK], F32R) for h in range(2)] for p in range(2)]
        lo = [[sb(f"w{p + 1}_lo{h}", [128, PK], F32R) for h in range(2)] for p in range(2)]
        bias = [sb(f"bias{h}", [128, KF + D]) for h in range(2)]
        rows = [sb(f"rows{h}", [128, nt, D]) for h in range(2)]
        x_hi, x_lo = sb("x_hi", [128, KD, CH], F32R), sb("x_lo", [128, KD, CH], F32R)
        hid = [sb(f"hidden{q}", [128, 2, CH]) for q in range(2)]
        h_hi, h_lo = sb("h_hi", [128, KF, CH], F32R), sb("h_lo", [128, KF, CH], F32R)
        y = [sb(f"out_rows{h}", [128, nt, D]) for h in range(2)]
        warm = sb("warm", [128, 1])
        pT, pH, pY = ps("p_T"), [ps(f"p_H{i}") for i in range(2)], [ps(f"p_Y{i}") for i in range(nt)]
        w_in = k.w_in
        w_hi, w_lo = ([sem(f"w{p + 1}_{s}") for p in range(2)] for s in ("hi", "lo"))
        rows_in, bias_in, y_out, y_free = ([sem(f"{s}{h}") for h in range(2)] for s in ("rows_in", "bias_in", "y_out", "y_free"))
        turned, x_high, x_split = sem("turned"), sem("x_high"), sem("x_split")
        up, acted, h_high, h_split, down, biased = (sem(s) for s in ("up", "acted", "h_high", "h_split", "down", "biased"))

        with nc.Block() as block:
            @block.sync
            def _(sp):
                def load_rows(n, h):
                    sp.dma_start(rows[h][:, :, :], buf[bass.ds(n * CH, CH), :].rearrange("(t p) c -> p t c", p=128))\
                        .then_inc(rows_in[h], 16)

                def load_bias(e, h):
                    sp.dma_start(bias[h][:, :], ab[bass.ds(e, 1), :, :].rearrange("e p c -> p (e c)"))\
                        .then_inc(bias_in[h], 16)

                def load_w(p, e, h):
                    sp.dma_start(raw[p][h], aw[bass.ds(e, 1), p, :, :].rearrange("e p c -> p (e c)"))\
                        .then_inc(w_in[p][h], 16)

                def expert(n):
                    return sp.value_load(k.chunk_x[0:1, bass.ds(n, 1)], min_val=0, max_val=X - 1)

                e = expert(0)
                load_rows(0, 0)
                load_bias(e, 0)
                with sp.Fori(0, chunks // 2) as r:
                    for h in range(2):
                        n, other = r * 2 + h, 1 - h
                        e1, e2 = expert(n + 1), expert(n + 2)
                        sp.wait_ge(turned, 1 + n)
                        load_rows(n + 1, other)
                        sp.wait_ge(w_lo[1], 1 + n)
                        load_w(1, e1, other)
                        sp.wait_ge(w_lo[0], 1 + n + 1)
                        load_w(0, e2, h)
                        sp.wait_ge(biased, 1 + n * nt)
                        load_bias(e1, other)
                sp.wait_ge(bias_in[0], (chunks // 2 + 1) * 16)

            @block.scalar
            def _(s):
                one_ahead(s, acted)

                def high(p, slot, loads):
                    s.wait_ge(w_in[p][slot], loads * 16)
                    s.activation(hi[p][slot][:, :], raw[p][slot], ACT.Copy).then_inc(w_hi[p], 1)

                def store(r, h):
                    s.wait_ge(biased, 1 + (r * 2 + h + 1) * nt)
                    s.dma_start(ybuf[bass.ds((r * 2 + h) * CH, CH), :].rearrange("(t p) c -> p t c", p=128),
                                y[h][:, :, :]).then_inc(y_out[h], 16)

                s.activation(warm[:, :], k.ones[:, 0:1], act)
                high(0, 0, 1)
                high(1, 0, 1)
                high(0, 1, 1)
                with s.Fori(0, chunks // 2) as r:
                    for h in range(2):
                        n = r * 2 + h
                        s.wait_ge(bias_in[h], r * 16 + 16)
                        for q in range(pairs):
                            s.wait_ge(up, 1 + n * pairs + q + 1)
                            s.wait_ge(h_split, 1 + n * pairs + max(q - 1, 0))
                            for f in range(2):
                                s.activation(hid[q % 2][:, f, :], pH[q % 2][:, f * CH:(f + 1) * CH], act,
                                             bias=bias[h][:, 2 * q + f:2 * q + f + 1]).then_inc(acted, 1)
                        if h == 1:
                            store(r, 0)
                        s.wait_ge(down, 1 + n * nt)
                        high(1, 1 - h, r + 1 + h)
                        high(0, h, r + 2)
                    store(r, 1)
                for h in range(2):
                    s.wait_ge(y_out[h], chunks // 2 * 16)

            @block.gpsimd
            def _(g):
                one_ahead(g, *y_free, *w_lo)

                def low(p, slot, n):
                    g.wait_ge(w_hi[p], n)
                    g.tensor_tensor(lo[p][slot][:, :], raw[p][slot], hi[p][slot][:, :].bitcast(F32),
                                    ALU.subtract).then_inc(w_lo[p], 1)

                low(0, 0, 1)
                low(1, 0, 1)
                low(0, 1, 2)
                with g.Fori(0, chunks // 2 - 1) as r:
                    for h in range(2):
                        n = r * 2 + h
                        low(1, 1 - h, n + 2)
                        low(0, h, n + 3)
                    for h in range(2):
                        g.wait_ge(y_out[h], r * 16 + 16)
                        g.sem_inc(y_free[h], 1)
                low(1, 1, chunks)

            @block.vector
            def _(v):
                one_ahead(v, h_split, biased)
                both = pT[:, :].rearrange("p (i n) -> p i n", i=KD)

                def split_x(n):
                    v.wait_ge(turned, 1 + n + 1)
                    v.tensor_copy(x_hi[:, :, :], both).then_inc(x_high, 1)
                    v.wait_ge(x_high, n + 1)
                    v.tensor_tensor(x_lo[:, :, :], both, x_hi[:, :, :].bitcast(F32), ALU.subtract).then_inc(x_split, 1)

                split_x(0)
                with v.Fori(0, chunks // 2) as r:
                    for h in range(2):
                        n = r * 2 + h
                        for q in range(pairs):
                            pair = slice(2 * q, 2 * q + 2)
                            v.wait_ge(acted, 1 + n * KF + 2 * q + 2)
                            v.wait_ge(down, 1 + n * nt)
                            v.tensor_copy(h_hi[:, pair, :], hid[q % 2][:, :, :]).then_inc(h_high, 1)
                            v.wait_ge(h_high, n * pairs + q + 1)
                            v.tensor_tensor(h_lo[:, pair, :], hid[q % 2][:, :, :], h_hi[:, pair, :].bitcast(F32),
                                            ALU.subtract).then_inc(h_split, 1)
                        split_x(n + 1)
                        v.wait_ge(y_free[h], r + 1)
                        for t in range(nt):
                            v.wait_ge(down, 1 + n * nt + t + 1)
                            v.tensor_tensor(y[h][:, t, :], pY[t][:, 0:D], bias[h][:, KF:KF + D], ALU.add)\
                                .then_inc(biased, 1)

            @block.tensor
            def _(pe):
                one_ahead(pe, down, up, turned)

                def product(out, stationary, moving, first, last):
                    nc.tensor.matmul(out, stationary[0], moving[0], start=first, stop=False)
                    nc.tensor.matmul(out, stationary[0], moving[1], start=False, stop=False)
                    return nc.tensor.matmul(out, stationary[1], moving[0], start=False, stop=last)

                def turn(h, loads):
                    pe.wait_ge(rows_in[h], loads * 16)
                    for i in range(KD):
                        for t in range(nt):
                            last = nc.tensor.transpose(pT[:, i * CH + t * 128:i * CH + (t + 1) * 128],
                                                       rows[h][:, t, i * 128:(i + 1) * 128], k.ident[:, :])
                    last.then_inc(turned, 1)

                def first(n, h):
                    pe.wait_ge(w_lo[0], 1 + n + 1)
                    pe.wait_ge(x_split, n + 1)
                    for q in range(pairs):
                        pe.wait_ge(acted, 1 + n * KF + 2 * max(q - 1, 0))
                        for f in range(2):
                            for i in range(KD):
                                at = i * FF + (2 * q + f) * 128
                                last = product(pH[q % 2][:, f * CH:(f + 1) * CH],
                                               (hi[0][h][:, at:at + 128], lo[0][h][:, at:at + 128]),
                                               (x_hi[:, i, :], x_lo[:, i, :]), i == 0, i == KD - 1)
                        last.then_inc(up, 1)

                def second(n, h):
                    pe.wait_ge(w_lo[1], 1 + n + 1)
                    pe.wait_ge(biased, 1 + n * nt)
                    for t in range(nt):
                        for f in range(KF):
                            if t == 0 and f % 2 == 0:
                                pe.wait_ge(h_split, 1 + n * pairs + f // 2 + 1)
                            at = slice(t * 128, (t + 1) * 128)
                            last = product(pY[t][:, 0:D], (h_hi[:, f, at], h_lo[:, f, at]),
                                           (hi[1][h][:, f * D:(f + 1) * D], lo[1][h][:, f * D:(f + 1) * D]),
                                           f == 0, f == KF - 1)
                        last.then_inc(down, 1)

                turn(0, 1)
                with pe.Fori(0, chunks // 2) as r:
                    for h in range(2):
                        n = r * 2 + h
                        first(n, h)
                        turn(1 - h, r + 1 + h)
                        second(n, h)


def combine(nc, a, k, layer):
    with ExitStack() as c:
        def sem(name):
            return k.sem(nc, f"{name}_c{layer}")

        got = k.got
        vec, stored = sem("vec"), sem("stored")
        held = [c.enter_context(nc.sbuf_tensor(f"picked{i}_c{layer}", [P, T, D], F32)) for i in range(layer + 1)]
        gated, finite, signed, replaced = sem("gated"), sem("finite"), sem("signed"), sem("replaced")
        if layer == 0:
            over = c.enter_context(nc.sbuf_tensor("guard_over", [P, GT, D], F32))
            sign = [c.enter_context(nc.sbuf_tensor(f"guard_sign{i}", [P, GT, D], F32)) for i in range(2)]
            fin = [c.enter_context(nc.sbuf_tensor(f"guard_finite{i}", [P, GT, D], I32)) for i in range(2)]

            def replace(s, r):
                s.wait_ge(signed, r + 1)
                s.activation(sign[r % 2][:, :, :], sign[r % 2][:, :, :], ACT.Copy, scale=-1e4).then_inc(replaced, 1)

        with nc.Block() as block:
            @block.gpsimd
            def _(g):
                for t in range(T):
                    for i in range(layer + 1):
                        g.indirect_dma_start(
                            out=held[i][:, t, :], out_offset=None, in_=k.ybuf[layer],
                            in_offset=bass.IndirectOffsetOnAxis(ap=k.back[:, i, t:t + 1], axis=0)).then_inc(got[t], 16)

            @block.scalar
            def _(s):
                if layer == 0:
                    for r in range(GR):
                        for t in range(r * GT, (r + 1) * GT):
                            s.wait_ge(got[t], 16)
                            s.activation(held[0][:, t, :], held[0][:, t, :], ACT.Copy, scale=k.gate[:, 0, t:t + 1])\
                                .then_inc(gated, 1)
                        if r:
                            replace(s, r - 1)
                    replace(s, GR - 1)

            @block.vector
            def _(v):
                ch = Chain(v, vec)
                if layer == 0:
                    def signs(r):
                        y = held[0][:, r * GT:(r + 1) * GT, :]
                        v.wait_ge(gated, GT * (r + 1))
                        if r:
                            v.wait_ge(signed, r)
                            ch.join()
                        v.tensor_scalar(fin[r % 2][:, :, :], y, 0.0, 0.0, ALU.mult, ALU.is_equal).then_inc(finite, 1)
                        ch.link(v.tensor_scalar(over[:, :, :], y, BIG, None, ALU.is_gt))
                        v.scalar_tensor_tensor(sign[r % 2][:, :, :], y, -BIG, over[:, :, :], ALU.is_lt, ALU.subtract)\
                            .then_inc(signed, 1)

                    def take(r):
                        ts = slice(r * GT, (r + 1) * GT)
                        new = sign[r % 2][:, :, :]
                        v.wait_ge(finite, r + 1)
                        v.wait_ge(replaced, r + 1)
                        ch.link(v.copy_predicated(new, fin[r % 2][:, :, :], held[0][:, ts, :]))
                        ch.link(v.tensor_tensor(k.x[:, ts, :], k.x[:, ts, :], new, ALU.add))
                        for t in range(r * GT, (r + 1) * GT):
                            ch.mark(v.bn_stats(k.stats[:, t, :], k.x[:, t, :]))

                    signs(0)
                    for r in range(1, GR):
                        signs(r)
                        take(r - 1)
                    take(GR - 1)
                else:
                    for t in range(T):
                        v.wait_ge(got[t], 16 + 32)
                        ch.link(v.scalar_tensor_tensor(k.x[:, t, :], held[0][:, t, :], k.gate[:, 0, t:t + 1], k.x[:, t, :],
                                                       ALU.mult, ALU.add))
                        ch.mark(v.scalar_tensor_tensor(k.x[:, t, :], held[1][:, t, :], k.gate[:, 1, t:t + 1], k.x[:, t, :],
                                                       ALU.mult, ALU.add))

            @block.sync
            def _(sp):
                if layer == 1:
                    for r in range(GR):
                        ts = slice(r * GT, (r + 1) * GT)
                        sp.wait_ge(vec, 2 * GT * (r + 1))
                        sp.dma_start(a["out"][:, ts, :], k.x[:, ts, :]).then_inc(stored, 16)
                    sp.wait_ge(stored, 16 * GR)


def project(nc, a, k):
    w = k.w
    with ExitStack() as c:
        def sb(name, shape):
            return c.enter_context(nc.sbuf_tensor(name, shape, F32))

        def sem(name):
            return k.sem(nc, name)

        def ps(name):
            return c.enter_context(nc.psum_tensor(name, [128, 512], F32))

        xs, xT = sb("p_rows", [P, GT, D]), sb("p_rowsT", [128, GT, KD, P])
        xj, z, junk = sb("xj", [P, GT, XJW]), sb("xj_z", [P, D]), sb("xj_wa2", [P, D])
        low, kk, vv = sb("k_low", [P, D]), sb("k_feat", [P, GT, D]), sb("v_rows", [P, GT, D + 1])
        xi = sb("xi_T", [128, GT, KD, P])
        ba, warm = sb("ba12", [128, 1]), sb("warm", [128, 1])
        zero = sb("zero_row", [1, D + 1])
        pT, pJ, pK, pV, pI, pA = (ps(n) for n in ("p_pT", "p_xj", "p_k", "p_v", "p_xi", "p_a1"))
        pc = [ps(f"p_ctx{i}") for i in range(KD)]
        normed, turned, copied, kept = sem("p_normed"), sem("p_turned"), sem("p_copied"), sem("p_kept")
        init, vec, var_ready, root_ready = sem("p_init"), sem("p_vec"), sem("p_var"), sem("p_root")
        xj_mm, kv_mm, xi_mm, a1_mm, ctx_mm = sem("xj_mm"), sem("kv_mm"), sem("xi_mm"), sem("a1_mm"), sem("ctx_mm")
        xj_max, xi_max, xj_free, z_ready = sem("xj_max"), sem("xi_max"), sem("xj_free"), sem("z_ready")
        a2_ready, v_ready, low_ready, exp_ready = sem("a2_ready"), sem("v_ready"), sem("low_ready"), sem("exp_ready")
        k_ready, xi_ready, a1_ready, xj_out, sums = sem("k_ready"), sem("xi_ready"), sem("a1_ready"), sem("xj_out"), sem("p_sums")

        with nc.Block() as block:
            @block.gpsimd
            def _(g):
                g.memset(xj[:, :, D:XJW], 0.0).then_inc(init, 1)
                g.memset(vv[:, :, D], 1.0).then_inc(init, 1)
                g.memset(zero[:, :], 0.0).then_inc(init, 1)
                g.memset(k.ctx[:, :, :, :], 0.0).then_inc(init, 1)
                g.memset(k.x_all[:, T, :], 0.0).then_inc(init, 1)
                g.memset(k.xnT[:, :, N:N + P], 0.0).then_inc(init, 1)
                for r in range(GR):
                    x = k.x[:, r * GT:(r + 1) * GT, :]
                    g.wait_ge(kept, 1 + 2 * GT * (r + 1))
                    g.tensor_tensor(x, x, k.xn[:, r * GT:(r + 1) * GT, :], ALU.add).then_inc(sums, 1)
                    g.wait_ge(sums, r * 2 + 1)
                    g.tensor_tensor(x, x, w["m1_bp"][0:P, :].unsqueeze(1).broadcast_to([P, GT, D]), ALU.add)\
                        .then_inc(sums, 1)

            @block.sync
            def _(sp):
                one_ahead(sp, xj_free)
                with sp.Fori(0, GR) as r:
                    sp.wait_ge(a2_ready, r * GT + GT)
                    sp.dma_start(k.xj_d[bass.ds(r * GT * P, GT * P), :].rearrange("(t p) c -> p t c", p=P),
                                 xj[:, :, :]).then_inc(xj_out, 16)
                    sp.wait_ge(xj_out, r * 16 + 16)
                    sp.sem_inc(xj_free, 1)

            @block.scalar
            def _(s):
                one_ahead(s, kept, copied, v_ready, xi_ready, exp_ready)
                norm_root_scalar(s, k, var_ready, root_ready, 1)
                s.activation(warm[:, :], k.ones[:, 0:1], ACT.Exp)
                s.wait_ge(init, 6)

                def take(r, t):
                    m = r * GT + t
                    s.wait_ge(turned, m + 1)
                    view = pT[:, 0:KD * P].rearrange("p (a b) -> p a b", a=KD)
                    s.activation(xT[:, t, :, :], view, ACT.Copy).then_inc(copied, 1)
                    s.activation(k.xnT[:, :, bass.ds(m * P, P)], view, ACT.Copy).then_inc(kept, 1)
                    s.activation(k.xn[:, bass.ds(m, 1), :], xs[:, t:t + 1, :], ACT.Copy).then_inc(kept, 1)

                with s.Fori(0, GR) as r:
                    s.wait_ge(xi_mm, 1 + r * GT)
                    take(r, 0)
                    for t in range(GT):
                        m = r * GT + t
                        s.wait_ge(kv_mm, m + 1)
                        if t == 0:
                            s.wait_ge(ctx_mm, 1 + r * GT)
                            s.wait_ge(a1_mm, 1 + r * GT)
                        s.activation(vv[:, t, 0:D], pV[0:P, 0:D], ACT.Copy).then_inc(v_ready, 1)
                        if t + 1 < GT:
                            take(r, t + 1)
                        s.wait_ge(low_ready, m + 1)
                        s.activation(kk[:, t, :], low[:, :], ACT.Exp).then_inc(exp_ready, 1)
                        s.wait_ge(xi_mm, 1 + m + 1)
                        for i in range(KD):
                            s.activation(xi[:, t, i, :], pI[:, i * P:(i + 1) * P], ACT.Identity,
                                         bias=w["g1_b1"][:, i:i + 1]).then_inc(xi_ready, 1)

            @block.vector
            def _(v):
                one_ahead(v, xj_max, k_ready, a1_ready, z_ready)

                def norm(r, t):
                    one = bass.ds(r * GT + t, 1)
                    v.tensor_scalar(xs[:, t:t + 1, :], k.x[:, one, :], k.mean[:, one], k.rstd[:, one],
                                    ALU.subtract, ALU.mult).then_inc(normed, 1)

                def keep_a1(m):
                    v.wait_ge(a1_mm, 1 + m + 1)
                    v.tensor_scalar(k.a1[:, bass.ds(m, 1), :], pA[:, 0:P].unsqueeze(1), ba[:, 0:1], None, ALU.add)\
                        .then_inc(a1_ready, 1)

                ch = Chain(v, vec)
                norm_scale_vector(nc, v, ch, k, var_ready, root_ready, 1)
                ch.link(v.tensor_tensor(ba[:, :], w["g1_ba1"][:, :], w["g1_ba2"][:, :], ALU.add))
                v.wait_ge(init, 6)
                with v.Fori(0, GR) as r:
                    v.wait_ge(kept, 1 + r * 2 * GT)
                    norm(r, 0)
                    for t in range(GT):
                        m = r * GT + t
                        if t + 1 < GT:
                            norm(r, t + 1)
                        if t == 0:
                            v.wait_ge(xj_free, r + 1)
                        v.wait_ge(xj_mm, m + 1)
                        v.wait_ge(xj_max, 1 + m)
                        v.tensor_tensor(z[:, :], pJ[0:P, 0:D], w["g1_b2"][0:P, :], ALU.add).then_inc(z_ready, 1)
                        v.wait_ge(kv_mm, m + 1)
                        v.wait_ge(exp_ready, 1 + m)
                        v.tensor_scalar(low[:, :], pK[0:P, 0:D], 0.0, None, ALU.min).then_inc(low_ready, 1)
                        v.wait_ge(z_ready, 1 + m + 1)
                        v.scalar_tensor_tensor(xj[:, t, 0:D], z[:, :], 0.2, z[:, :], ALU.mult, ALU.max).then_inc(xj_max, 1)
                        v.wait_ge(xj_max, 1 + m + 1)
                        v.scalar_tensor_tensor(junk[:, :], xj[:, t, 0:D], 1.0, w["g1_wa2"][0:P, :], ALU.mult, ALU.mult,
                                               accum_out=xj[:, t, D:D + 1]).then_inc(a2_ready, 1)
                        v.wait_ge(exp_ready, 1 + m + 1)
                        v.scalar_tensor_tensor(kk[:, t, :], pK[0:P, 0:D], 0.0, kk[:, t, :], ALU.max, ALU.add)\
                            .then_inc(k_ready, 1)
                        v.wait_ge(xi_ready, 1 + (m + 1) * KD)
                        v.scalar_tensor_tensor(xi[:, t, :, :], xi[:, t, :, :], 0.2, xi[:, t, :, :], ALU.mult, ALU.max)\
                            .then_inc(xi_max, 1)
                        if t:
                            keep_a1(m - 1)
                    keep_a1(r * GT + GT - 1)
                v.wait_ge(ctx_mm, 1 + T + 1)
                for h in range(HEADS):
                    i, q = h * HD // 128, h * HD % 128
                    v.tensor_copy(k.ctx[q:q + HD, i, 0, q:q + HD], pc[i][q:q + HD, h * HD:(h + 1) * HD])
                    v.tensor_copy(k.ctx[q:q + HD, i, 1, q:q + HD], pc[i][q:q + HD, D:D + 1].broadcast_to([HD, HD]))

            @block.tensor
            def _(pe):
                one_ahead(pe, ctx_mm, a1_mm, xi_mm)
                pe.wait_ge(init, 6)
                for i in range(KD):
                    nc.tensor.matmul(pc[i][:, 0:D + 1], k.ones[0:1, :], zero[:, :], start=True, stop=False)

                def turn(m, t):
                    pe.wait_ge(normed, m + 1)
                    pe.wait_ge(kept, 1 + m * 2)
                    for i in range(KD):
                        last = nc.tensor.transpose(pT[:, i * P:(i + 1) * P], xs[:, t, i * 128:(i + 1) * 128],
                                                   k.ident[0:P, 0:P])
                    last.then_inc(turned, 1)

                def sums_and_a1(m, t):
                    pe.wait_ge(k_ready, 1 + m + 1)
                    pe.wait_ge(v_ready, 1 + m + 1)
                    for i in range(KD):
                        last = nc.tensor.matmul(pc[i][:, 0:D + 1], kk[:, t, i * 128:(i + 1) * 128], vv[:, t, :],
                                                start=False, stop=False)
                    last.then_inc(ctx_mm, 1)
                    pe.wait_ge(xi_max, m + 1)
                    pe.wait_ge(a1_ready, 1 + m)
                    for o in range(KD):
                        last = nc.tensor.matmul(pA[:, 0:P], w["g1_wa1"][:, o, :], xi[:, t, o, :],
                                                start=o == 0, stop=o == KD - 1)
                    last.then_inc(a1_mm, 1)

                with pe.Fori(0, GR) as r:
                    turn(r * GT, 0)
                    for t in range(GT):
                        m = r * GT + t
                        pe.wait_ge(copied, 1 + m + 1)
                        pe.wait_ge(z_ready, 1 + m)
                        for i in range(KD):
                            last = nc.tensor.matmul(pJ[0:P, 0:D], xT[:, t, i, :], w["g1_W2"][:, i, :],
                                                    start=i == 0, stop=i == KD - 1)
                        last.then_inc(xj_mm, 1)
                        pe.wait_ge(k_ready, 1 + m)
                        pe.wait_ge(v_ready, 1 + m)
                        for bank, at in ((pK, 0), (pV, D)):
                            for i in range(KD):
                                last = nc.tensor.matmul(bank[0:P, 0:D], xT[:, t, i, :], w["m1_WkvT"][:, i, at:at + D],
                                                        start=i == 0, stop=i == KD - 1)
                        last.then_inc(kv_mm, 1)
                        if t + 1 < GT:
                            turn(m + 1, t + 1)
                        pe.wait_ge(xi_ready, 1 + m * KD)
                        for o in range(KD):
                            for i in range(KD):
                                last = nc.tensor.matmul(pI[:, o * P:(o + 1) * P], w["g1_W1"][:, i, o * 128:(o + 1) * 128],
                                                        xT[:, t, i, :], start=i == 0, stop=i == KD - 1)
                        last.then_inc(xi_mm, 1)
                        if t:
                            sums_and_a1(m - 1, t - 1)
                    sums_and_a1(r * GT + GT - 1, GT - 1)
                for i in range(KD):
                    last = nc.tensor.matmul(pc[i][:, 0:D + 1], k.ones[0:1, :], zero[:, :], start=False, stop=True)
                last.then_inc(ctx_mm, 1)


def columns(w):
    return w.reshape(-1, 128, w.shape[-1]).transpose(1, 0, 2)


def kernel(**inputs):
    import numpy as np
    from concourse import bacc
    from concourse.bass_utils import run_bass_kernel_spmd

    x = {n: np.asarray(v) for n, v in inputs.items()}

    def spread(v):
        return np.broadcast_to(v.reshape(1, -1), (128, v.size))

    def pack(w1, w2):
        return np.stack([w1.reshape(X, KD, 128, FF).transpose(0, 2, 1, 3).reshape(X, 128, PK),
                         w2.reshape(X, KF, 128, D).transpose(0, 2, 1, 3).reshape(X, 128, PK)], axis=1)

    def biases(b1, b2):
        return np.concatenate([b1.reshape(X, KF, 128).transpose(0, 2, 1),
                               np.broadcast_to(b2.reshape(X, 1, D), (X, 128, D))], axis=2)

    arrays = {
        "x": x["x"].reshape(T, P, D).transpose(1, 0, 2),
        "src": x["src"].reshape(P, EC), "dst": x["dst"].reshape(P, EC),
        "edge_weight": x["edge_weight"].reshape(P, EC),
        "g0_W1": columns(x["L0_gnn_W1"]), "g0_b1": x["L0_gnn_b1"].reshape(-1, 128).T,
        "g0_W2": columns(x["L0_gnn_W2"]), "g0_b2": x["L0_gnn_b2"].reshape(1, D),
        "m0_Wq": columns(x["L0_mix_Wq"]), "m0_WkT": columns(x["L0_mix_Wk"].T), "m0_WvT": columns(x["L0_mix_Wv"].T),
        "m0_WfcT": columns(x["L0_mix_Wfc"].T), "m0_bqc": x["L0_mix_bq"].reshape(-1, 128).T,
        "m0_bk": x["L0_mix_bk"].reshape(1, D), "m0_bv": x["L0_mix_bv"].reshape(1, D),
        "m0_bfc": x["L0_mix_bfc"].reshape(1, D),
        "f0_gw": columns(x["L0_ffn_gate_w"]), "f0_gb": spread(np.tile(x["L0_ffn_gate_b"], T)).reshape(128, T, X),
        "f0_w": pack(x["L0_ffn_w1"], x["L0_ffn_w2"]), "f0_b": biases(x["L0_ffn_b1"], x["L0_ffn_b2"]),
        "g1_W1": columns(x["L1_gnn_W1"]), "g1_b1": x["L1_gnn_b1"].reshape(-1, 128).T,
        "g1_W2": columns(x["L1_gnn_W2"]), "g1_b2": spread(x["L1_gnn_b2"]),
        "g1_wa1": np.broadcast_to(x["L1_gnn_wa1"].reshape(KD, 128, 1).transpose(1, 0, 2), (128, KD, 128)),
        "g1_ba1": spread(x["L1_gnn_ba1"]), "g1_wa2": spread(x["L1_gnn_wa2"]), "g1_ba2": spread(x["L1_gnn_ba2"]),
        "m1_WqT": columns(x["L1_mix_Wq"].T), "m1_WkvT": columns(x["L1_mix_Wkv"].T),
        "m1_WpT": columns(x["L1_mix_Wproj"].T), "m1_bp": spread(x["L1_mix_bproj"]),
        "f1_gw": columns(x["L1_ffn_Wg"]), "f1_gb": spread(np.tile(x["L1_ffn_bg"], T)).reshape(128, T, X),
        "f1_w": pack(x["L1_ffn_W1"], x["L1_ffn_W2"]), "f1_b": biases(x["L1_ffn_b1"], x["L1_ffn_b2"]),
    }
    arrays = {n: np.ascontiguousarray(v) for n, v in arrays.items()}
    nc = bacc.Bacc("TRN2", target_bir_lowering=False, num_devices=1)
    a = {n: nc.dram_tensor(f"in_{n}", v.shape, mybir.dt.from_np(v.dtype), kind="ExternalInput").ap()
         for n, v in arrays.items()}
    a["out"] = nc.dram_tensor("out", (P, T, D), F32, kind="ExternalOutput").ap()
    build(nc, a)
    r = run_bass_kernel_spmd(nc, [{f"in_{n}": v for n, v in arrays.items()}], core_ids=[0])
    return np.ascontiguousarray(r.results[0]["out"].transpose(1, 0, 2)).reshape(N, D)
```
